# Optimizing a Trainium2 kernel written in Bass

```python
import numpy as np
import jax
import jax.numpy as jnp

def _softmax(x, axis=-1):
    return jax.nn.softmax(x, axis=axis)

def _gelu(x):
    return jax.nn.gelu(x, approximate=True)

def _silu(x):
    return jax.nn.silu(x)

def _sigmoid(x):
    return jax.nn.sigmoid(x)

def _layernorm(x, axis=-1, eps=1e-05):
    m = jnp.mean(x, axis=axis, keepdims=True)
    v = jnp.var(x, axis=axis, keepdims=True)
    return (x - m) / jnp.sqrt(v + eps)

def _scatter_add(tgt, idx, src, axis=0):
    return tgt.at[idx].add(src)

def _segment_sum(src, seg, n):
    return jax.ops.segment_sum(src, seg, n)
kernel_name = 'mk_adj_preln_d4_adj_r2_6d0a5b'

def setup_inputs(seed: int=0):
    np.random.seed(seed)
    _w = jnp.asarray

    def _rec_inputs():
        import jax
        import jax.numpy as jnp
        _gk = jax.random.key(seed)
        x = -0.0003929 + 0.9999 * jax.random.normal(jax.random.fold_in(_gk, 1), (16, 512, 128), jnp.float32)
        _a = jax.random.bernoulli(jax.random.fold_in(_gk, 2), 0.0078125, (512, 512))
        _a = jnp.logical_or(_a, jnp.swapaxes(_a, -1, -2))
        _a = jnp.logical_or(_a, jnp.eye(512, dtype=bool))
        _af = _a.astype(jnp.float32)
        _af = _af * jax.random.uniform(jax.random.fold_in(_gk, 3), (512, 512), jnp.float32, 0.05, 1)
        adj = _af
        return (x, adj)
    x, adj = _rec_inputs()

    def _L0_gnn_setup():
        import jax, jax.numpy as jnp
        import numpy as np
        EPS = 1e-05

        def _batchnorm(x, gamma, beta):
            mu = jnp.mean(x, axis=0)
            var = jnp.var(x, axis=0)
            return (x - mu) * jax.lax.rsqrt(var + EPS) * gamma + beta
        key = jax.random.key(seed)
        ks = jax.random.split(key, 4)
        b, n, d, h, o = (32, 1024, 128, 256, 128)
        features = jax.random.normal(ks[0], (b, n, d), dtype=jnp.float32)
        A = jax.random.uniform(ks[1], (n, n), dtype=jnp.float32)
        lim1 = float(np.sqrt(6.0 / (d + h)))
        W1 = jax.random.uniform(ks[2], (h, d), minval=-lim1, maxval=lim1, dtype=jnp.float32)
        b1 = jnp.zeros((h,), jnp.float32)
        lim2 = float(np.sqrt(6.0 / (h + o)))
        W2 = jax.random.uniform(ks[3], (o, h), minval=-lim2, maxval=lim2, dtype=jnp.float32)
        b2 = jnp.zeros((o,), jnp.float32)
        g1 = jnp.ones((h,), jnp.float32)
        be1 = jnp.zeros((h,), jnp.float32)
        g2 = jnp.ones((o,), jnp.float32)
        be2 = jnp.zeros((o,), jnp.float32)
        return {'features': features, 'A': A, 'W1': W1, 'b1': b1, 'g1': g1, 'be1': be1, 'W2': W2, 'b2': b2, 'g2': g2, 'be2': be2}
    _L0_gnn_all = _L0_gnn_setup()
    _L0_gnn_in = {k: v for k, v in _L0_gnn_all.items() if k in ('W1', 'b1', 'g1', 'be1', 'W2', 'b2', 'g2', 'be2')}
    del _L0_gnn_all

    def _L1_gnn_setup():
        import jax, jax.numpy as jnp
        import numpy as np
        B, T, D, H = (64, 1024, 128, 128)
        MAX_SKIP = 4

        def _lstm_last(Wih, Whh, bih, bhh, xs):
            N, _, Hd = xs.shape
            bias = bih + bhh

            def step(carry, x_t):
                h, c = carry
                g = x_t @ Wih.T + h @ Whh.T + bias
                i, f, gg, o = jnp.split(g, 4, axis=-1)
                c = jax.nn.sigmoid(f) * c + jax.nn.sigmoid(i) * jnp.tanh(gg)
                h = jax.nn.sigmoid(o) * jnp.tanh(c)
                return ((h, c), None)
            init = (jnp.zeros((N, Hd), xs.dtype), jnp.zeros((N, Hd), xs.dtype))
            (h_last, _), _ = jax.lax.scan(step, init, jnp.swapaxes(xs, 0, 1))
            return h_last
        key = jax.random.key(seed)
        ks = jax.random.split(key, 8)
        s = 0.05
        x = jax.random.normal(ks[0], (B, T, D), jnp.float32)
        adj = jax.random.uniform(ks[1], (T, T), jnp.float32) / T
        Wg0 = jax.random.normal(ks[2], (D, H), jnp.float32) * s
        bg0 = jnp.zeros((H,), jnp.float32)
        Wg1 = jax.random.normal(ks[3], (H, H), jnp.float32) * s
        bg1 = jnp.zeros((H,), jnp.float32)
        Wih = jax.random.normal(ks[4], (MAX_SKIP, 4 * H, H), jnp.float32) * s
        Whh = jax.random.normal(ks[5], (MAX_SKIP, 4 * H, H), jnp.float32) * s
        bih = jax.random.normal(ks[6], (MAX_SKIP, 4 * H), jnp.float32) * s
        bhh = jax.random.normal(ks[7], (MAX_SKIP, 4 * H), jnp.float32) * s
        return dict(x=x, adj=adj, Wg0=Wg0, bg0=bg0, Wg1=Wg1, bg1=bg1, Wih=Wih, Whh=Whh, bih=bih, bhh=bhh)
    _L1_gnn_all = _L1_gnn_setup()
    _L1_gnn_in = {k: v for k, v in _L1_gnn_all.items() if k in ('Wg0', 'bg0', 'Wg1', 'bg1', 'Wih', 'Whh', 'bih', 'bhh')}
    del _L1_gnn_all

    def _L2_gnn_setup():
        import jax, jax.numpy as jnp
        import numpy as np
        N = 3445
        B = 32
        IN_DIM = 128
        HID_DIM = 128

        def _make_adj(key):
            a = jax.random.uniform(key, (N, N), dtype=jnp.float32)
            a = (a < 0.001).astype(jnp.float32)
            a = jnp.maximum(a, a.T)
            deg = jnp.sum(a, axis=1, keepdims=True)
            return a / jnp.maximum(deg, 1.0)

        def _graph_conv(x, adj, w_loop, w_neigh, b):
            loop = jnp.einsum('bnd,dh->bnh', x, w_loop)
            neigh = jnp.einsum('nm,bmh->bnh', adj, jnp.einsum('bnd,dh->bnh', x, w_neigh))
            return loop + neigh + b
        key = jax.random.key(seed)
        k = jax.random.split(key, 8)
        s1 = 1.0 / np.sqrt(IN_DIM)
        s2 = 1.0 / np.sqrt(HID_DIM)
        return {'x': jax.random.normal(k[0], (B, N, IN_DIM), dtype=jnp.float32), 'adj': _make_adj(k[1]), 'w1_loop': jax.random.normal(k[2], (IN_DIM, HID_DIM), dtype=jnp.float32) * s1, 'w1_neigh': jax.random.normal(k[3], (IN_DIM, HID_DIM), dtype=jnp.float32) * s1, 'b1': jnp.zeros((HID_DIM,), dtype=jnp.float32), 'w2_loop': jax.random.normal(k[4], (HID_DIM, IN_DIM), dtype=jnp.float32) * s2, 'w2_neigh': jax.random.normal(k[5], (HID_DIM, IN_DIM), dtype=jnp.float32) * s2, 'b2': jnp.zeros((IN_DIM,), dtype=jnp.float32)}
    _L2_gnn_all = _L2_gnn_setup()
    _L2_gnn_in = {k: v for k, v in _L2_gnn_all.items() if k in ('w1_loop', 'w1_neigh', 'b1', 'w2_loop', 'w2_neigh', 'b2')}
    del _L2_gnn_all

    def _L3_gnn_setup():
        import jax, jax.numpy as jnp
        import numpy as np
        EPS_LN = 1e-05

        def _layernorm(x, g, b):
            mu = x.mean(-1, keepdims=True)
            var = ((x - mu) ** 2).mean(-1, keepdims=True)
            return (x - mu) / jnp.sqrt(var + EPS_LN) * g + b
        key = jax.random.key(seed)
        B, N, D, H = (4, 1024, 128, 4)
        hid = int(D * 2.0)
        ks = jax.random.split(key, 12)
        x = jax.random.normal(ks[0], (B, N, D), jnp.float32)
        Au = jax.random.uniform(ks[1], (N, N)) < 0.004
        A = jnp.logical_or(Au, Au.T)
        A = A.at[jnp.arange(N), jnp.arange(N)].set(False)
        Af = A.astype(jnp.float32)
        deg = Af.sum(axis=1)
        L = jnp.diag(deg) - Af
        adjacency = Af + jnp.eye(N, dtype=jnp.float32)
        s = lambda k, sh, f: jax.random.normal(k, sh, jnp.float32) * f
        sc = 1.0 / np.sqrt(D)
        Wc = s(ks[2], (D, D), sc)
        bc = jnp.zeros((D,), jnp.float32)
        Wq = s(ks[3], (D, D), sc)
        Wk = s(ks[4], (D, D), sc)
        Wv = s(ks[5], (D, D), sc)
        Wo = s(ks[6], (D, D), sc)
        bo = jnp.zeros((D,), jnp.float32)
        W1 = s(ks[7], (D, hid), sc)
        b1 = jnp.zeros((hid,), jnp.float32)
        W2 = s(ks[8], (hid, D), 1.0 / np.sqrt(hid))
        b2 = jnp.zeros((D,), jnp.float32)
        g1 = jnp.ones((D,), jnp.float32)
        be1 = jnp.zeros((D,), jnp.float32)
        g2 = jnp.ones((D,), jnp.float32)
        be2 = jnp.zeros((D,), jnp.float32)
        g3 = jnp.ones((D,), jnp.float32)
        be3 = jnp.zeros((D,), jnp.float32)
        return dict(x=x, L=L, adjacency=adjacency, Wc=Wc, bc=bc, g1=g1, be1=be1, Wq=Wq, Wk=Wk, Wv=Wv, Wo=Wo, bo=bo, g2=g2, be2=be2, W1=W1, b1=b1, W2=W2, b2=b2, g3=g3, be3=be3)
    _L3_gnn_all = _L3_gnn_setup()
    _L3_gnn_in = {k: v for k, v in _L3_gnn_all.items() if k in ('Wc', 'bc', 'g1', 'be1', 'Wq', 'Wk', 'Wv', 'Wo', 'bo', 'g2', 'be2', 'W1', 'b1', 'W2', 'b2', 'g3', 'be3')}
    del _L3_gnn_all
    return {'x': x, 'adj': adj, 'L0_gnn_W1': _L0_gnn_in['W1'], 'L0_gnn_b1': _L0_gnn_in['b1'], 'L0_gnn_g1': _L0_gnn_in['g1'], 'L0_gnn_be1': _L0_gnn_in['be1'], 'L0_gnn_W2': _L0_gnn_in['W2'], 'L0_gnn_b2': _L0_gnn_in['b2'], 'L0_gnn_g2': _L0_gnn_in['g2'], 'L0_gnn_be2': _L0_gnn_in['be2'], 'L1_gnn_Wg0': _L1_gnn_in['Wg0'], 'L1_gnn_bg0': _L1_gnn_in['bg0'], 'L1_gnn_Wg1': _L1_gnn_in['Wg1'], 'L1_gnn_bg1': _L1_gnn_in['bg1'], 'L1_gnn_Wih': _L1_gnn_in['Wih'], 'L1_gnn_Whh': _L1_gnn_in['Whh'], 'L1_gnn_bih': _L1_gnn_in['bih'], 'L1_gnn_bhh': _L1_gnn_in['bhh'], 'L2_gnn_w1_loop': _L2_gnn_in['w1_loop'], 'L2_gnn_w1_neigh': _L2_gnn_in['w1_neigh'], 'L2_gnn_b1': _L2_gnn_in['b1'], 'L2_gnn_w2_loop': _L2_gnn_in['w2_loop'], 'L2_gnn_w2_neigh': _L2_gnn_in['w2_neigh'], 'L2_gnn_b2': _L2_gnn_in['b2'], 'L3_gnn_Wc': _L3_gnn_in['Wc'], 'L3_gnn_bc': _L3_gnn_in['bc'], 'L3_gnn_g1': _L3_gnn_in['g1'], 'L3_gnn_be1': _L3_gnn_in['be1'], 'L3_gnn_Wq': _L3_gnn_in['Wq'], 'L3_gnn_Wk': _L3_gnn_in['Wk'], 'L3_gnn_Wv': _L3_gnn_in['Wv'], 'L3_gnn_Wo': _L3_gnn_in['Wo'], 'L3_gnn_bo': _L3_gnn_in['bo'], 'L3_gnn_g2': _L3_gnn_in['g2'], 'L3_gnn_be2': _L3_gnn_in['be2'], 'L3_gnn_W1': _L3_gnn_in['W1'], 'L3_gnn_b1': _L3_gnn_in['b1'], 'L3_gnn_W2': _L3_gnn_in['W2'], 'L3_gnn_b2': _L3_gnn_in['b2'], 'L3_gnn_g3': _L3_gnn_in['g3'], 'L3_gnn_be3': _L3_gnn_in['be3']}

def reference(x, adj, L0_gnn_W1, L0_gnn_b1, L0_gnn_g1, L0_gnn_be1, L0_gnn_W2, L0_gnn_b2, L0_gnn_g2, L0_gnn_be2, L1_gnn_Wg0, L1_gnn_bg0, L1_gnn_Wg1, L1_gnn_bg1, L1_gnn_Wih, L1_gnn_Whh, L1_gnn_bih, L1_gnn_bhh, L2_gnn_w1_loop, L2_gnn_w1_neigh, L2_gnn_b1, L2_gnn_w2_loop, L2_gnn_w2_neigh, L2_gnn_b2, L3_gnn_Wc, L3_gnn_bc, L3_gnn_g1, L3_gnn_be1, L3_gnn_Wq, L3_gnn_Wk, L3_gnn_Wv, L3_gnn_Wo, L3_gnn_bo, L3_gnn_g2, L3_gnn_be2, L3_gnn_W1, L3_gnn_b1, L3_gnn_W2, L3_gnn_b2, L3_gnn_g3, L3_gnn_be3):
    import jax
    import jax.numpy as jnp

    def _L0_gnn_ref(features, A, W1, b1, g1, be1, W2, b2, g2, be2):
        import jax, jax.numpy as jnp
        import numpy as np
        EPS = 1e-05

        def _batchnorm(x, gamma, beta):
            mu = jnp.mean(x, axis=0)
            var = jnp.var(x, axis=0)
            return (x - mu) * jax.lax.rsqrt(var + EPS) * gamma + beta
        b, n, d = features.shape
        A_norm = A + jnp.eye(n, dtype=A.dtype)
        deg = jnp.sum(A_norm, axis=0) + jnp.sum(A_norm, axis=1) - jnp.diagonal(A_norm)
        dinv = jax.lax.rsqrt(deg)
        A_hat = A_norm * dinv[:, None] * dinv[None, :]
        agg = jnp.einsum('nm,bmd->bnd', A_hat, features)
        x = agg.reshape(-1, d)
        h = jax.nn.relu(_batchnorm(x @ W1.T + b1, g1, be1))
        out = h @ W2.T + b2
        out = _batchnorm(out, g2, be2)
        return out.reshape(b, n, -1)

    def _L1_gnn_ref(x, adj, Wg0, bg0, Wg1, bg1, Wih, Whh, bih, bhh):
        import jax, jax.numpy as jnp
        import numpy as np
        B, T, D, H = (64, 1024, 128, 128)
        MAX_SKIP = 4

        def _lstm_last(Wih, Whh, bih, bhh, xs):
            N, _, Hd = xs.shape
            bias = bih + bhh

            def step(carry, x_t):
                h, c = carry
                g = x_t @ Wih.T + h @ Whh.T + bias
                i, f, gg, o = jnp.split(g, 4, axis=-1)
                c = jax.nn.sigmoid(f) * c + jax.nn.sigmoid(i) * jnp.tanh(gg)
                h = jax.nn.sigmoid(o) * jnp.tanh(c)
                return ((h, c), None)
            init = (jnp.zeros((N, Hd), xs.dtype), jnp.zeros((N, Hd), xs.dtype))
            (h_last, _), _ = jax.lax.scan(step, init, jnp.swapaxes(xs, 0, 1))
            return h_last
        h = jax.nn.relu(jnp.einsum('ts,bsh->bth', adj, x @ Wg0 + bg0))
        h = jax.nn.relu(jnp.einsum('ts,bsh->bth', adj, h @ Wg1 + bg1))
        Bv, Tv, Hd = h.shape
        for p in range(1, MAX_SKIP + 1):
            nw = Tv // p
            wins = h[:, :nw * p, :].reshape(Bv * nw, p, Hd)
            last = _lstm_last(Wih[p - 1], Whh[p - 1], bih[p - 1], bhh[p - 1], wins)
            idx = jnp.arange(nw) * p + (p - 1)
            h = h.at[:, idx, :].set(last.reshape(Bv, nw, Hd))
        return h

    def _L2_gnn_ref(x, adj, w1_loop, w1_neigh, b1, w2_loop, w2_neigh, b2):
        import jax, jax.numpy as jnp
        import numpy as np
        N = 3445
        B = 32
        IN_DIM = 128
        HID_DIM = 128

        def _make_adj(key):
            a = jax.random.uniform(key, (N, N), dtype=jnp.float32)
            a = (a < 0.001).astype(jnp.float32)
            a = jnp.maximum(a, a.T)
            deg = jnp.sum(a, axis=1, keepdims=True)
            return a / jnp.maximum(deg, 1.0)

        def _graph_conv(x, adj, w_loop, w_neigh, b):
            loop = jnp.einsum('bnd,dh->bnh', x, w_loop)
            neigh = jnp.einsum('nm,bmh->bnh', adj, jnp.einsum('bnd,dh->bnh', x, w_neigh))
            return loop + neigh + b
        h = jax.nn.relu(_graph_conv(x, adj, w1_loop, w1_neigh, b1))
        h = jax.nn.relu(_graph_conv(h, adj, w2_loop, w2_neigh, b2))
        return (x + h) * 0.5

    def _L3_gnn_ref(x, L, adjacency, Wc, bc, g1, be1, Wq, Wk, Wv, Wo, bo, g2, be2, W1, b1, W2, b2, g3, be3):
        import jax, jax.numpy as jnp
        import numpy as np
        EPS_LN = 1e-05

        def _layernorm(x, g, b):
            mu = x.mean(-1, keepdims=True)
            var = ((x - mu) ** 2).mean(-1, keepdims=True)
            return (x - mu) / jnp.sqrt(var + EPS_LN) * g + b
        B, N, D = x.shape
        H = 4
        hd = D // H
        eig = jnp.linalg.eigvalsh(L)
        lam_max = eig[-1] + 1e-08
        L_norm = 2.0 * L / lam_max - jnp.eye(N, dtype=L.dtype)
        xp = jnp.einsum('mn,bnf->bmf', L_norm, x)
        h = xp @ Wc + bc
        h = _layernorm(h, g1, be1)
        h = jax.nn.relu(h)
        x1 = h + x
        q = (x1 @ Wq).reshape(B, N, H, hd).transpose(0, 2, 1, 3)
        k = (x1 @ Wk).reshape(B, N, H, hd).transpose(0, 2, 1, 3)
        v = (x1 @ Wv).reshape(B, N, H, hd).transpose(0, 2, 1, 3)
        scores = jnp.einsum('bhnd,bhmd->bhnm', q, k) / np.sqrt(hd).astype(np.float32)
        scores = jnp.where(adjacency[None, None] > 0, scores, jnp.float32(-1000000000.0))
        attn = jax.nn.softmax(scores, axis=-1)
        o = jnp.einsum('bhnm,bhmd->bhnd', attn, v)
        o = o.transpose(0, 2, 1, 3).reshape(B, N, D)
        o = o @ Wo + bo
        x2 = _layernorm(x1 + o, g2, be2)
        m = jax.nn.gelu(x2 @ W1 + b1, approximate=False) @ W2 + b2
        return _layernorm(x2 + m, g3, be3)
    h = jnp.maximum(_layernorm(x, axis=-1), 0.0)
    x = x + _L0_gnn_ref(h, adj, L0_gnn_W1, L0_gnn_b1, L0_gnn_g1, L0_gnn_be1, L0_gnn_W2, L0_gnn_b2, L0_gnn_g2, L0_gnn_be2)
    h = jnp.maximum(_layernorm(x, axis=-1), 0.0)
    x = x + _L1_gnn_ref(h, adj, L1_gnn_Wg0, L1_gnn_bg0, L1_gnn_Wg1, L1_gnn_bg1, L1_gnn_Wih, L1_gnn_Whh, L1_gnn_bih, L1_gnn_bhh)
    h = jnp.maximum(_layernorm(x, axis=-1), 0.0)
    x = x + _L2_gnn_ref(h, adj, L2_gnn_w1_loop, L2_gnn_w1_neigh, L2_gnn_b1, L2_gnn_w2_loop, L2_gnn_w2_neigh, L2_gnn_b2)
    h = jnp.maximum(_layernorm(x, axis=-1), 0.0)
    x = x + _L3_gnn_ref(h, adj, adj, L3_gnn_Wc, L3_gnn_bc, L3_gnn_g1, L3_gnn_be1, L3_gnn_Wq, L3_gnn_Wk, L3_gnn_Wv, L3_gnn_Wo, L3_gnn_bo, L3_gnn_g2, L3_gnn_be2, L3_gnn_W1, L3_gnn_b1, L3_gnn_W2, L3_gnn_b2, L3_gnn_g3, L3_gnn_be3)
    return x

_drawn_inputs = setup_inputs


def setup_inputs(seed=0):
    import zlib

    import numpy as np

    out = dict(_drawn_inputs(seed))
    spreads = {'L0_gnn_b1': (0.0, 2.0),
     'L0_gnn_g1': (1.0, 0.2),
     'L0_gnn_be1': (0.0, 0.1),
     'L0_gnn_b2': (0.0, 2.0),
     'L0_gnn_g2': (1.0, 0.2),
     'L0_gnn_be2': (0.0, 0.1),
     'L1_gnn_bg0': (0.0, 0.534),
     'L1_gnn_bg1': (0.0, 0.799),
     'L2_gnn_b1': (0.0, 0.274),
     'L2_gnn_b2': (0.0, 0.8),
     'L3_gnn_bc': (0.0, 0.329),
     'L3_gnn_g1': (1.0, 0.2),
     'L3_gnn_be1': (0.0, 0.36),
     'L3_gnn_bo': (0.0, 0.385),
     'L3_gnn_g2': (1.0, 0.2),
     'L3_gnn_be2': (0.0, 0.3),
     'L3_gnn_b1': (0.0, 0.55),
     'L3_gnn_b2': (0.0, 0.391),
     'L3_gnn_g3': (1.0, 0.2),
     'L3_gnn_be3': (0.0, 0.306)}
    factors = {'L1_gnn_Whh': 8.0, 'L1_gnn_bih': 6.11, 'L1_gnn_bhh': 6.081}
    for name, (base, spread) in spreads.items():
        noise = np.random.default_rng([zlib.crc32(name.encode()), seed]).standard_normal(out[name].shape)
        drawn = base * np.exp(spread * noise) if base else spread * noise
        out[name] = jnp.asarray(drawn.astype(out[name].dtype))
    for name, factor in factors.items():
        out[name] = (out[name] * factor).astype(out[name].dtype)
    return out
```

```python
import concourse.bass as bass
from concourse import mybir
from contextlib import ExitStack


P = 128
F32 = mybir.dt.float32
ALU = mybir.AluOpType
ACT = mybir.ActivationFunctionType
X_AXIS = mybir.AxisListType.X

GRAPHS, NODES, D = 16, 512, 128
NT = NODES // P
TILES = GRAPHS * NT
HID = 256
HEADS, HD = 4, 32
EPS = 1e-5
SCALE = 1.0 / (HD ** 0.5)
SQUARINGS = 12
LAST_STAGE = 3

COLS = {}
for _name, _n in (("L0_b1", 2), ("L0_g1", 2), ("L0_be1", 2), ("L0_b2", 1), ("L0_g2", 1), ("L0_be2", 1),
                  ("L1_bg1", 1), ("L2_b1", 1), ("L3_b1", 2), ("L1_bih", 16), ("L1_bhh", 16)):
    COLS[_name] = (sum(n for _, n in COLS.values()), _n)
NCOLS = sum(n for _, n in COLS.values())
ROWS = ["L1_bg0", "L2_b2", "L3_bc", "L3_g1", "L3_be1", "L3_bo", "L3_g2", "L3_be2", "L3_b2", "L3_g3", "L3_be3"]
SQUARE_WEIGHTS = ["L1_Wg0", "L1_Wg1", "L2_w1_loop", "L2_w1_neigh", "L2_w2_loop", "L2_w2_neigh",
                  "L3_Wc", "L3_Wq", "L3_Wk", "L3_Wv", "L3_Wo"]
T_W1, T_W2, T_WIH, T_WHH, T_BLOCKS = 0, 2, 4, 20, 36


def build(nc, d, out):
    with ExitStack() as ctx:
        def sb(name, shape, dt=F32):
            return ctx.enter_context(nc.sbuf_tensor(name, shape, dt))

        def sem(name):
            return ctx.enter_context(nc.semaphore(name))

        X = sb("X", [P, TILES, D])
        MV = sb("MV", [P, 2, NT, 2])
        RSTD = sb("RSTD", [P, TILES])
        NBIAS = sb("NBIAS", [P, TILES])
        ST = sb("ST", [P, 2, NT, 6])
        VE = sb("VE", [P, 2, NT])
        NMEAN = sb("NMEAN", [P, 2, NT])
        MHALF = sb("MHALF", [P, NT])
        ident = sb("ident", [P, P])
        ones = sb("ones", [P, P])
        COL = sb("COL", [P, NCOLS])
        ROW = sb("ROW", [P, len(ROWS), D])
        WSQ = sb("WSQ", [P, len(SQUARE_WEIGHTS), D])
        W3A = sb("W3A", [P, HID])
        W3B = sb("W3B", [P, 2, D])
        WT = sb("WT", [P, T_BLOCKS, P])
        adjT = sb("adjT", [P, NT, NODES])
        AhatT = sb("AhatT", [P, NT, NODES])
        LT = sb("LT", [P, NT, NODES])
        NB = sb("NB", [P, NT, NODES])
        ANYB = sb("ANYB", [P, NODES])
        BM0 = sb("BM0", [P, NT, D])
        BM1 = sb("BM1", [P, NODES])
        GB = sb("GB", [P, 16])
        AFF = sb("AFF", [P, 8])

        def col(name, j=0):
            at = COLS[name][0] + j
            return COL[:, at:at + 1]

        def cols(name):
            return COL[:, COLS[name][0]:COLS[name][0] + COLS[name][1]]

        def row4(name):
            return ROW[:, ROWS.index(name), :].unsqueeze(1).to_broadcast([P, NT, D])

        def wsq(name):
            return WSQ[:, SQUARE_WEIGHTS.index(name), :]

        x_loaded, const_ok, passed = sem("x_loaded"), sem("const_ok"), sem("passed")
        v, a, g, t = nc.vector, nc.scalar, nc.gpsimd, nc.tensor

        class LayerNormSems:
            def __init__(self, tag):
                self.stats, self.moments, self.free, self.rstd, self.bias = (
                    sem(f"{tag}_{n}") for n in ("stats", "moments", "free", "rstd", "bias"))

        def alone(eng):
            eng.sem_inc(passed, 1)

        def dve_row_stats(eng, s, b, k, src):
            for i in range(NT):
                last = v.bn_stats(ST[:, k % 2, i, :], src(i))
            last.then_inc(s.stats, 1)
            eng.wait_ge(s.stats, b + 1)
            eng.wait_ge(s.free, b + 1)
            alone(eng)
            for i in range(NT):
                last = v.bn_aggr(MV[:, k % 2, i, :], ST[:, k % 2, i, :])
            last.then_inc(s.moments, 1)

        def pool_rstd(eng, s, b, k, rstd, nbias):
            eng.wait_ge(s.moments, b + 1)
            alone(eng)
            g.tensor_scalar(NMEAN[:, k % 2, :], MV[:, k % 2, :, 0], -1.0, 0.0, ALU.mult, ALU.add)
            g.tensor_scalar(VE[:, k % 2, :], MV[:, k % 2, :, 1], 1.0, EPS, ALU.mult, ALU.add).then_inc(s.free, 1)
            eng.wait_ge(s.free, b + 3)
            alone(eng)
            g.tensor_tensor(rstd, VE[:, k % 2, :], MHALF[:], ALU.pow).then_inc(s.rstd, 1)
            eng.wait_ge(s.rstd, b + 1)
            alone(eng)
            g.tensor_tensor(nbias, NMEAN[:, k % 2, :], rstd, ALU.mult).then_inc(s.bias, 1)

        def dve_x_stats(eng, s, b, k, written=None, ahead=3):
            eng.wait_ge(x_loaded, 16)
            if written is not None:
                eng.wait_ge(written, b + ahead)
                alone(eng)
            dve_row_stats(eng, s, b, k, lambda i: X[:, 4 * b + i, :])

        def pool_x_rstd(eng, s, b, k):
            pool_rstd(eng, s, b, k, RSTD[:, bass.ds(4 * b, 4)], NBIAS[:, bass.ds(4 * b, 4)])

        def act_norm_relu(b, dst):
            for i in range(NT):
                last = a.activation(dst[:, i, :], X[:, 4 * b + i, :], ACT.Relu,
                                    bias=NBIAS[:, bass.ds(4 * b + i, 1)], scale=RSTD[:, bass.ds(4 * b + i, 1)])
            return last

        def over_nodes(ps, node_major, matT, start=True, stop=True):
            for m in range(NT):
                last = t.matmul(ps, node_major[:, m, :], matT[:, m, :],
                                start=start and m == 0, stop=stop and m == NT - 1)
            return last

        def to_node_major(ps, feat, w):
            for i in range(NT):
                last = t.matmul(ps[:, i, :], feat[:, bass.ts(i, P)], w, start=True, stop=True)
            return last

        def transposes(ps, blocks):
            for i, x in enumerate(blocks):
                last = t.transpose(ps[:, i, :], x, ident[:])
            return last

        def pairs(eng, body):
            with eng.Fori(0, GRAPHS // 4 - 1) as i:
                for slot in (0, 2):
                    body(4 * i + slot, slot, True)
            for slot in (0, 2):
                body(GRAPHS - 4 + slot, slot, slot == 0)

        def every(eng, body):
            with eng.Fori(0, GRAPHS // 2) as i:
                for slot in range(2):
                    body(2 * i + slot, slot)

        with ExitStack() as pctx:
            def psb(name, shape, dt=F32):
                return pctx.enter_context(nc.sbuf_tensor(name, shape, dt))

            adjN = psb("adjN", [P, NT, NODES])
            WR = psb("WR", [P, T_BLOCKS, P])
            VR = psb("VR", [NCOLS, P])
            S = psb("S", [P, NT, NODES])
            PA = psb("PA", [P, NT, NODES])
            PB = psb("PB", [P, NT, NODES])
            junk = psb("junk", [P, NT * NODES])
            tmp = psb("tmp", [P, NT, NODES])
            DG = psb("DG", [P, 3, NT, P])
            sm = psb("sm", [P, 64])
            c11 = psb("c11", [1, 4])
            ps4 = pctx.enter_context(nc.psum_tensor("ps4", [P, NT, NODES], F32))
            psx = pctx.enter_context(nc.psum_tensor("psx", [P, NODES], F32))
            psy = pctx.enter_context(nc.psum_tensor("psy", [P, NODES], F32))
            rowsum, colsum, diag = sm[:, 0:4], sm[:, 4:8], sm[:, 8:12]
            deg, dinv, any_ = sm[:, 12:16], sm[:, 16:20], sm[:, 20:24]
            rabs, rmax, shift = sm[:, 24:28], sm[:, 28:29], sm[:, 29:30]
            sq, isq, num_den = sm[:, 30:31], sm[:, 31:32], sm[:, 32:34]
            lam, two_over = sm[:, 34:35], sm[:, 35:36]
            dtr = sm[:, 36:40]

            d_adj, d_w, d_v = sem("d_adj"), sem("d_w"), sem("d_v")
            ident0, ident_ok = sem("ident0"), sem("ident_ok")
            tr_done, tr_copied = sem("tr_done"), sem("tr_copied")
            dv, deg_ok, dinv_ok = sem("dv"), sem("deg_ok"), sem("dinv_ok")
            diag_ok, bcast_ok = sem("diag_ok"), sem("bcast_ok")
            rmax_ok, rmaxT_ok, c11_ok, shift_ok = sem("rmax_ok"), sem("rmaxT_ok"), sem("c11_ok"), sem("shift_ok")
            m_done, sq_sum, sq_bcast, isq_ok = sem("m_done"), sem("sq_sum"), sem("sq_bcast"), sem("isq_ok")
            m_dve, m_act = sem("m_dve"), sem("m_act")
            nd_ok, nd_bcast = sem("nd_ok"), sem("nd_bcast")
            lx = LayerNormSems("lx")

            x_view = d["x"].rearrange("b (t p) d -> p (b t) d", p=P)
            N_W = 4 + len(SQUARE_WEIGHTS)
            N_V = len(COLS) + len(ROWS)

            with nc.Block() as block:
                @block.sync
                def _(sp):
                    sp.dma_start(adjN[:], d["adj"].rearrange("(t p) m -> p t m", p=P)).then_inc(d_adj, 16)
                    sp.dma_start(X[:], x_view).then_inc(x_loaded, 16)
                    for name in COLS:
                        at, w = COLS[name]
                        src = d[name]
                        src = src.rearrange("l (g p) -> (l g) p", p=P) if w == 16 else src.rearrange("(c p) -> c p", p=P)
                        sp.dma_start(VR[at:at + w, :], src).then_inc(d_v, 16)
                    for i, name in enumerate(ROWS):
                        sp.dma_start(ROW[:, i, :], d[name].partition_broadcast(P)).then_inc(d_v, 16)

                @block.scalar
                def _(act):
                    act.dma_start(WR[:, T_W1:T_W1 + 2, :], d["L0_W1"].rearrange("(h p) d -> p h d", p=P)).then_inc(d_w, 16)
                    act.dma_start(WR[:, T_W2:T_W2 + 2, :], d["L0_W2"].rearrange("o (h k) -> o h k", h=2)).then_inc(d_w, 16)
                    act.dma_start(WR[:, T_WIH:T_WIH + 16, :], d["L1_Wih"].rearrange("l (g p) d -> p (l g) d", p=P)).then_inc(d_w, 16)
                    act.dma_start(WR[:, T_WHH:T_WHH + 16, :], d["L1_Whh"].rearrange("l (g p) d -> p (l g) d", p=P)).then_inc(d_w, 16)
                    for i, name in enumerate(SQUARE_WEIGHTS):
                        act.dma_start(WSQ[:, i, :], d[name]).then_inc(d_w, 16)
                    act.dma_start(W3A[:], d["L3_W1"]).then_inc(d_v, 16)
                    act.dma_start(W3B[:], d["L3_W2"].rearrange("(h p) d -> p h d", p=P)).then_inc(d_v, 16)
                    act.wait_ge(shift_ok, 2)
                    def square(i, src, dst, k):
                        if k:
                            act.wait_ge(m_act, i * 2 + k)
                            act.wait_ge(m_dve, i * 2 + k)
                        a.activation(junk[:], src[:].rearrange("p t n -> p (t n)"), ACT.Square,
                                     accum_out=sq).then_inc(sq_sum, 1)
                        act.wait_ge(isq_ok, i * 2 + k + 1)
                        act.wait_ge(m_done, i * 2 + k + 1)
                        for r in (1, 3):
                            last = a.activation(dst[:, r, :], ps4[:, r, :], ACT.Copy, scale=isq)
                        last.then_inc(m_act, 1)
                        if not k:
                            return
                        act.wait_ge(m_act, i * 2 + k + 1)
                        act.wait_ge(m_dve, i * 2 + k + 1)
                    with act.Fori(0, SQUARINGS // 2) as i:
                        square(i, PA, PB, 0)
                        square(i, PB, PA, 1)

                @block.gpsimd
                def _(pool):
                    g.memset(ident[:], 0.0).then_inc(ident0, 1)
                    g.memset(ones[:], 1.0).then_inc(const_ok, 1)
                    g.memset(MHALF[:], -0.5).then_inc(const_ok, 1)
                    pool.wait_ge(ident0, 1)
                    g.affine_select(out=ident[:], in_=ident[:], compare_op=ALU.not_equal, fill=1.0, base=0,
                                    pattern=[[-1, P]], channel_multiplier=1).then_inc(ident_ok, 1)
                    pool.wait_ge(const_ok, 2)
                    pool.wait_ge(deg_ok, 1)
                    g.tensor_tensor(dinv, deg, MHALF[:], ALU.pow).then_inc(dinv_ok, 1)
                    pool.sem_inc(lx.free, 2)
                    every(pool, lambda b, k: pool_x_rstd(pool, lx, b, k))

                @block.vector
                def _(dve):
                    n = [0]

                    def step(ins):
                        n[0] += 1
                        ins.then_inc(dv, 1)
                        dve.wait_ge(dv, n[0])

                    for m in range(NT):
                        dve.wait_ge(tr_done, m + 1)
                        step(v.tensor_copy(adjT[:, m, :], ps4[:, m, :]))
                    v.reduce_sum(rowsum, adjN[:], X_AXIS)
                    v.reduce_sum(colsum, adjT[:], X_AXIS)
                    for m in range(NT):
                        last = v.tensor_tensor(junk[:, m * P:(m + 1) * P], adjN[:, m, m * P:(m + 1) * P], ident[:], ALU.mult)
                    step(last)
                    step(v.reduce_sum(diag, junk[:, 0:NODES].rearrange("p (t n) -> p t n", t=NT), X_AXIS))
                    step(v.tensor_tensor(deg, rowsum, colsum, ALU.add))
                    step(v.tensor_tensor(deg, deg, diag, ALU.subtract))
                    v.tensor_scalar_add(deg, deg, 1.0).then_inc(deg_ok, 1)
                    for q in range(T_BLOCKS // 4):
                        dve.wait_ge(tr_done, NT + q + 1)
                        v.tensor_copy(WT[:, 4 * q:4 * q + 4, :], (psx, psy)[q % 2][:].rearrange("p (t n) -> p t n", t=4)).then_inc(tr_copied, 1)
                    dve.wait_ge(tr_done, NT + T_BLOCKS // 4 + 1)
                    v.tensor_copy(COL[:], psy[:, 0:NCOLS]).then_inc(tr_copied, 1)
                    step(v.tensor_tensor(S[:], adjN[:], adjT[:], ALU.add))
                    step(v.tensor_scalar(S[:], S[:], 0.5, None, ALU.mult))
                    step(v.tensor_reduce(rabs, S[:], X_AXIS, ALU.add, apply_absolute_value=True))
                    v.reduce_max(rmax, rabs, X_AXIS).then_inc(rmax_ok, 1)
                    dve.wait_ge(rmaxT_ok, 1)
                    v.reduce_max(c11[:, 0:1], psx[0:1, 0:P], X_AXIS).then_inc(c11_ok, 1)
                    dve.wait_ge(rmaxT_ok, 2)
                    step(v.tensor_copy(shift, psx[:, P:P + 1]))
                    step(v.tensor_copy(PA[:], S[:]))
                    for m in range(NT):
                        blk = slice(m * P, (m + 1) * P)
                        last = v.scalar_tensor_tensor(PA[:, m, blk], ident[:], shift, S[:, m, blk], ALU.mult, ALU.add)
                    last.then_inc(shift_ok, 2)

                    step(v.tensor_scalar(tmp[:], adjN[:], 0.0, None, ALU.is_gt))
                    step(v.reduce_max(any_, tmp[:], X_AXIS))
                    step(v.tensor_scalar(tmp[:], tmp[:], 1.0, 1e9, ALU.subtract, ALU.mult))
                    for m in range(NT):
                        v.tensor_scalar(NB[:, m, :], tmp[:, m, :], any_[:, m:m + 1], None, ALU.mult)
                    dve.wait_ge(dinv_ok, 1)
                    for j, vec in enumerate((rowsum, dinv, any_)):
                        for m in range(NT):
                            last = v.tensor_scalar(DG[:, j, m, :], ident[:], vec[:, m:m + 1], None, ALU.mult)
                    last.then_inc(diag_ok, 1)
                    def square(i, dst, k):
                        dve.wait_ge(sq_bcast, i * 2 + k + 1)
                        v.reciprocal(isq, psy[:, 0:1]).then_inc(isq_ok, 1)
                        dve.wait_ge(isq_ok, i * 2 + k + 1)
                        dve.wait_ge(m_done, i * 2 + k + 1)
                        for r in (0, 2):
                            last = v.tensor_scalar(dst[:, r, :], ps4[:, r, :], isq, None, ALU.mult)
                        last.then_inc(m_dve, 1)
                    with dve.Fori(0, SQUARINGS // 2) as i:
                        square(i, PB, 0)
                        square(i, PA, 1)
                    dve.wait_ge(m_dve, SQUARINGS)
                    dve.wait_ge(m_act, SQUARINGS)
                    v.scalar_tensor_tensor(junk[:], S[:].rearrange("p t n -> p (t n)"), 1.0,
                                           PA[:].rearrange("p t n -> p (t n)"), ALU.mult, ALU.mult,
                                           accum_out=num_den[:, 0:1])
                    for m in range(NT):
                        last = v.tensor_tensor(tmp[:, 0, m * P:(m + 1) * P], PA[:, m, m * P:(m + 1) * P], ident[:], ALU.mult)
                    step(last)
                    v.reduce_sum(num_den[:, 1:2], tmp[:, 0, :], X_AXIS).then_inc(nd_ok, 1)
                    dve.wait_ge(nd_bcast, 1)
                    step(v.reciprocal(lam, psy[:, 5:6]))
                    step(v.tensor_tensor(lam, lam, psy[:, 4:5], ALU.mult))
                    step(v.tensor_scalar(lam, lam, 1e-8, None, ALU.add))
                    step(v.reciprocal(two_over, lam))
                    step(v.tensor_scalar(two_over, two_over, 2.0, None, ALU.mult))
                    step(v.tensor_scalar(LT[:], adjT[:], two_over, None, ALU.mult))
                    for m in range(NT):
                        blk = slice(m * P, (m + 1) * P)
                        v.tensor_tensor(LT[:, m, blk], LT[:, m, blk], ident[:], ALU.subtract)

                    step(v.tensor_copy(tmp[:], adjT[:]))
                    for m in range(NT):
                        blk = slice(m * P, (m + 1) * P)
                        last = v.tensor_tensor(tmp[:, m, blk], tmp[:, m, blk], ident[:], ALU.add)
                    step(last)
                    dve.wait_ge(bcast_ok, 1)
                    for m in range(NT):
                        v.scalar_tensor_tensor(AhatT[:, m, :], tmp[:, m, :], dinv[:, m:m + 1], ps4[:, 1, :], ALU.mult, ALU.mult)
                    v.tensor_copy(ANYB[:], ps4[:, 2, :])
                    dve.wait_ge(d_v, 16 * (N_V + 2))
                    v.tensor_scalar(BM1[:], ps4[:, 0, :], col("L1_bg1"), None, ALU.mult)
                    for m in range(NT):
                        v.tensor_scalar(BM0[:, m, :], ROW[:, ROWS.index("L1_bg0"), :], rowsum[:, m:m + 1], None, ALU.mult)
                    v.tensor_tensor(GB[:], cols("L1_bih"), cols("L1_bhh"), ALU.add)
                    every(dve, lambda b, k: dve_x_stats(dve, lx, b, k))

                @block.tensor
                def _(pe):
                    pe.wait_ge(ident_ok, 1)
                    pe.wait_ge(d_adj, 16)
                    for m in range(NT):
                        transposes(ps4[:, m, :].rearrange("p (t n) -> p t n", t=NT),
                                   [adjN[:, i, m * P:(m + 1) * P] for i in range(NT)]).then_inc(tr_done, 1)
                    pe.wait_ge(d_w, 16 * N_W)
                    for q in range(T_BLOCKS // 4):
                        if q >= 2:
                            pe.wait_ge(tr_copied, q - 1)
                        transposes((psx, psy)[q % 2][:].rearrange("p (t n) -> p t n", t=4),
                                   [WR[:, 4 * q + i, :] for i in range(4)]).then_inc(tr_done, 1)
                    pe.wait_ge(tr_copied, T_BLOCKS // 4)
                    pe.wait_ge(d_v, 16 * (N_V + 2))
                    t.transpose(psy[:, 0:NCOLS], VR[:], ident[0:NCOLS, 0:NCOLS]).then_inc(tr_done, 1)
                    pe.wait_ge(tr_copied, T_BLOCKS // 4 + 1)
                    pe.wait_ge(rmax_ok, 1)
                    t.transpose(psx[0:1, 0:P], rmax, ident[:]).then_inc(rmaxT_ok, 1)
                    pe.wait_ge(const_ok, 2)
                    pe.wait_ge(c11_ok, 1)
                    t.matmul(psx[:, P:P + 1], ones[0:1, :], c11[:, 0:1], start=True, stop=True).then_inc(rmaxT_ok, 1)
                    pe.wait_ge(shift_ok, 2)

                    def square(i, src, k):
                        if k:
                            pe.wait_ge(m_dve, i * 2 + k)
                            pe.wait_ge(m_act, i * 2 + k)
                        for m in range(NT):
                            for r in range(NT):
                                last = t.matmul(ps4[:, r, :], src[:, m, r * P:(r + 1) * P], src[:, m, :],
                                                start=m == 0, stop=m == NT - 1)
                        last.then_inc(m_done, 1)
                        pe.wait_ge(sq_sum, i * 2 + k + 1)
                        t.matmul(psy[:, 0:1], ones[:], sq, start=True, stop=True).then_inc(sq_bcast, 1)
                        if k:
                            pe.wait_ge(m_dve, i * 2 + k + 1)
                            pe.wait_ge(m_act, i * 2 + k + 1)
                    with pe.Fori(0, SQUARINGS // 2) as i:
                        square(i, PA, 0)
                        square(i, PB, 1)
                    pe.wait_ge(diag_ok, 1)
                    for j in range(3):
                        for m in range(NT):
                            last = t.matmul(ps4[:, j, m * P:(m + 1) * P], ones[:], DG[:, j, m, :], start=True, stop=True)
                    last.then_inc(bcast_ok, 1)
                    pe.wait_ge(nd_ok, 1)
                    t.matmul(psy[:, 4:6], ones[:], num_den, start=True, stop=True).then_inc(nd_bcast, 1)

        with ExitStack() as pctx:
            def psb(name, shape, dt=F32):
                return pctx.enter_context(nc.sbuf_tensor(name, shape, dt))

            H1 = psb("H1", [P, 2, GRAPHS, NODES])
            hn = psb("hn", [P, 4, NT, D])
            agg = psb("agg", [P, 2, NODES])
            hr = psb("hr", [P, 2, 2, NODES])
            bst = psb("bst", [P, 3, GRAPHS, 6])
            bmv = psb("bmv", [P, 3, 2])
            bve = psb("bve", [P, 3])
            Y = H1[:, 0]
            a_norm, a_agg, a_aggc, a_h, a_hc, a_st = (sem(f"s0_{n}") for n in ("norm", "agg", "aggc", "h", "hc", "st"))
            bn_mv, bn_ve, bn_rs, bn_sc, bn_d = (sem(f"s0_{n}") for n in ("bnmv", "bnve", "bnrs", "bnsc", "bnd"))
            b_hr, b_y, b_yc, b_st = (sem(f"s0_{n}") for n in ("hr", "y", "yc", "yst"))
            c_aff, c_t, c_x = (sem(f"s0_{n}") for n in ("aff", "t", "x"))
            ln = LayerNormSems("ln1")

            def dve_moments(dve, js, n):
                for j in js:
                    last = v.bn_aggr(bmv[:, j, :], bst[:, j, :, :])
                last.then_inc(bn_mv, 1)
                dve.wait_ge(bn_mv, n)
                v.tensor_scalar(bve[:, js[0]:js[-1] + 1], bmv[:, js[0]:js[-1] + 1, 1], EPS, None, ALU.add).then_inc(bn_ve, 1)

            def dve_affine(dve, js, n, scale, shift, gamma, beta):
                dve.wait_ge(bn_rs, n)
                v.tensor_tensor(scale, bve[:, js[0]:js[-1] + 1], gamma, ALU.mult).then_inc(bn_d, 1)
                dve.wait_ge(bn_d, 2 * n - 1)
                v.tensor_tensor(shift, bmv[:, js[0]:js[-1] + 1, 0], scale, ALU.mult).then_inc(bn_d, 1)
                dve.wait_ge(bn_d, 2 * n)
                v.tensor_tensor(shift, beta, shift, ALU.subtract).then_inc(bn_sc, 1)

            with ExitStack() as qctx, nc.Block() as block:
                psg = qctx.enter_context(nc.psum_tensor("s0_psg", [P, 2, NODES], F32))
                psh = qctx.enter_context(nc.psum_tensor("s0_psh", [P, 2, 2, NODES], F32))

                @block.scalar
                def _(act):
                    for k in range(2):
                        act_norm_relu(k, hn[:, k]).then_inc(a_norm, 1)

                    def body(b, slot, more):
                        if more:
                            for k in range(2):
                                act_norm_relu(b + 2 + k, hn[:, (slot + 2 + k) % 4]).then_inc(a_norm, 1)
                        for k in range(2):
                            act.wait_ge(a_agg, b + k + 1)
                            a.activation(agg[:, k, :], psg[:, k, :], ACT.Copy).then_inc(a_aggc, 1)
                    pairs(act, body)

                @block.tensor
                def _(pe):
                    def body(b, slot, more):
                        for k in range(2):
                            pe.wait_ge(a_norm, b + k + 1)
                            over_nodes(psg[:, k, :], hn[:, slot + k], AhatT).then_inc(a_agg, 1)
                        for k in range(2):
                            pe.wait_ge(a_aggc, b + k + 1)
                            pe.wait_ge(a_hc, b + k + 1)
                            for h in range(2):
                                last = t.matmul(psh[:, k, h, :], WT[:, T_W1 + h, :], agg[:, k, :], start=True, stop=True)
                            last.then_inc(a_h, 1)
                    pairs(pe, body)

                @block.vector
                def _(dve):
                    dve.sem_inc(a_hc, 2)

                    def body(b, slot):
                        dve.wait_ge(a_h, b + 1)
                        for h in range(2):
                            last = v.tensor_scalar(H1[:, h, b, :], psh[:, slot, h, :], col("L0_b1", h), None, ALU.add)
                        last.then_inc(a_hc, 1)
                        dve.wait_ge(a_hc, b + 3)
                        for h in range(2):
                            last = v.bn_stats(bst[:, h, b, :], H1[:, h, b, :])
                        last.then_inc(a_st, 1)
                    every(dve, body)
                    dve.wait_ge(a_st, GRAPHS)
                    dve_moments(dve, (0, 1), 1)
                    dve_affine(dve, (0, 1), 1, AFF[:, 0:2], AFF[:, 2:4], cols("L0_g1"), cols("L0_be1"))

                @block.gpsimd
                def _(pool):
                    pool.wait_ge(bn_ve, 1)
                    g.tensor_tensor(bve[:, 0:2], bve[:, 0:2], MHALF[:, 0:2], ALU.pow).then_inc(bn_rs, 1)

            with ExitStack() as qctx, nc.Block() as block:
                psy = qctx.enter_context(nc.psum_tensor("s0_psy", [P, 2, NODES], F32))

                @block.scalar
                def _(act):
                    def body(b, slot):
                        act.wait_ge(b_y, b + 1)
                        for h in range(2):
                            last = a.activation(hr[:, slot, h, :], H1[:, h, b, :], ACT.Relu,
                                                bias=AFF[:, 2 + h:3 + h], scale=AFF[:, h:h + 1])
                        last.then_inc(b_hr, 1)
                    every(act, body)

                @block.tensor
                def _(pe):
                    pe.sem_inc(b_y, 2)

                    def body(b, slot):
                        pe.wait_ge(b_hr, b + 1)
                        pe.wait_ge(b_yc, b + 1)
                        for h in range(2):
                            last = t.matmul(psy[:, slot, :], WT[:, T_W2 + h, :], hr[:, slot, h, :], start=h == 0, stop=h == 1)
                        last.then_inc(b_y, 1)
                    every(pe, body)

                @block.vector
                def _(dve):
                    dve.sem_inc(b_yc, 2)

                    def body(b, slot):
                        dve.wait_ge(b_y, b + 3)
                        v.tensor_scalar(Y[:, b, :], psy[:, slot, :], col("L0_b2"), None, ALU.add).then_inc(b_yc, 1)
                        dve.wait_ge(b_yc, b + 3)
                        v.bn_stats(bst[:, 2, b, :], Y[:, b, :]).then_inc(b_st, 1)
                    every(dve, body)
                    dve.wait_ge(b_st, GRAPHS)
                    dve_moments(dve, (2,), 2)
                    dve_affine(dve, (2,), 2, AFF[:, 4:5], AFF[:, 5:6], cols("L0_g2"), cols("L0_be2"))

                @block.gpsimd
                def _(pool):
                    pool.wait_ge(bn_ve, 2)
                    g.tensor_tensor(bve[:, 2:3], bve[:, 2:3], MHALF[:, 0:1], ALU.pow).then_inc(bn_rs, 1)

            with ExitStack() as qctx, nc.Block() as block:
                pst = qctx.enter_context(nc.psum_tensor("s0_pst", [P, 2, NT, P], F32))

                @block.scalar
                def _(act):
                    def body(b, slot):
                        act.wait_ge(c_t, b + 1)
                        a.activation(agg[:, slot, :], Y[:, b, :], ACT.Identity, bias=AFF[:, 5:6], scale=AFF[:, 4:5]).then_inc(c_aff, 1)
                    every(act, body)

                @block.tensor
                def _(pe):
                    pe.sem_inc(c_t, 2)

                    def body(b, slot):
                        pe.wait_ge(c_aff, b + 1)
                        pe.wait_ge(c_x, b + 1)
                        transposes(pst[:, slot], [agg[:, slot, i * P:(i + 1) * P] for i in range(NT)]).then_inc(c_t, 1)
                    every(pe, body)

                @block.vector
                def _(dve):
                    dve.sem_inc(c_x, 2)

                    def body(b, slot):
                        dve.wait_ge(c_t, b + 3)
                        xb = X[:, bass.ds(4 * b, 4), :]
                        v.tensor_tensor(xb, xb, pst[:, slot], ALU.add).then_inc(c_x, 1)
                        dve_x_stats(dve, ln, b, slot, c_x)
                    every(dve, body)

                @block.gpsimd
                def _(pool):
                    pool.sem_inc(ln.free, 2)
                    every(pool, lambda b, slot: pool_x_rstd(pool, ln, b, slot))

        with ExitStack() as pctx:
            def psb(name, shape, dt=F32):
                return pctx.enter_context(nc.sbuf_tensor(name, shape, dt))

            HF = psb("HF", [P, GRAPHS, NODES])
            g_norm, g_agg, g_aggc, g_w, g_add, g_relu = (
                sem(f"s1_{n}") for n in ("norm", "agg", "aggc", "w", "add", "relu"))

            with ExitStack() as qctx, nc.Block() as block:
                hn = qctx.enter_context(nc.sbuf_tensor("s1_hn", [P, 4, NT, D], F32))
                agg = qctx.enter_context(nc.sbuf_tensor("s1_agg", [P, 2, NODES], F32))
                pre = qctx.enter_context(nc.sbuf_tensor("s1_pre", [P, 2, 2, NODES], F32))
                h1 = qctx.enter_context(nc.sbuf_tensor("s1_h1", [P, 2, NT, D], F32))
                psa = qctx.enter_context(nc.psum_tensor("s1_psa", [P, 2, NODES], F32))
                psw = qctx.enter_context(nc.psum_tensor("s1_psw", [P, 2, NODES], F32))


                @block.scalar
                def _(act):
                    for k in range(2):
                        act_norm_relu(k, hn[:, k]).then_inc(g_norm, 1)

                    def body(b, slot, more):
                        if more:
                            for k in range(2):
                                act_norm_relu(b + 2 + k, hn[:, (slot + 2 + k) % 4]).then_inc(g_norm, 1)
                        for layer in range(2):
                            for k in range(2):
                                act.wait_ge(g_agg, 2 * b + 2 * layer + k + 1)
                                a.activation(agg[:, k, :], psa[:, k, :], ACT.Copy).then_inc(g_aggc, 1)
                            for k in range(2):
                                act.wait_ge(g_add, 2 * b + 2 * layer + k + 3)
                                dst = h1[:, k].rearrange("p t d -> p (t d)") if layer == 0 else HF[:, b + k, :]
                                a.activation(dst, pre[:, layer, k, :], ACT.Relu).then_inc(g_relu, 1)
                    pairs(act, body)

                @block.tensor
                def _(pe):
                    def body(b, slot, more):
                        for layer in range(2):
                            for k in range(2):
                                if layer == 0:
                                    pe.wait_ge(g_norm, b + k + 1)
                                    over_nodes(psa[:, k, :], hn[:, slot + k], adjT).then_inc(g_agg, 1)
                                else:
                                    pe.wait_ge(g_relu, 2 * b + k + 1)
                                    over_nodes(psa[:, k, :], h1[:, k], adjT).then_inc(g_agg, 1)
                            for k in range(2):
                                pe.wait_ge(g_aggc, 2 * b + 2 * layer + k + 1)
                                pe.wait_ge(g_add, 2 * b + 2 * layer + k + 1)
                                if layer == 0:
                                    to_node_major(psw[:, k, :].rearrange("p (t d) -> p t d", t=NT), agg[:, k, :],
                                                  wsq("L1_Wg0")).then_inc(g_w, 1)
                                else:
                                    t.matmul(psw[:, k, :], wsq("L1_Wg1"), agg[:, k, :], start=True, stop=True).then_inc(g_w, 1)
                    pairs(pe, body)

                @block.vector
                def _(dve):
                    dve.sem_inc(g_add, 2)

                    def body(b, slot, more):
                        for layer in range(2):
                            bias = BM0[:].rearrange("p t d -> p (t d)") if layer == 0 else BM1[:]
                            for k in range(2):
                                dve.wait_ge(g_w, 2 * b + 2 * layer + k + 1)
                                v.tensor_tensor(pre[:, layer, k, :], psw[:, k, :], bias, ALU.add).then_inc(g_add, 1)
                    pairs(dve, body)

            cells = []
            for p in range(1, 5):
                chunk_graphs = {1: 1, 2: 2, 3: 2, 4: 4}[p]
                chunks = 4 // chunk_graphs
                if p == 1:
                    cells += [(1, c, c, 1, 0, None) for c in range(4)]
                    continue
                base = len(cells)
                for step_t in range(p):
                    for c in range(chunks):
                        need = {2: 1 + 2 * c, 3: base - 2 + c, 4: base - 1}[p]
                        cells.append((p, c, c * chunk_graphs, chunk_graphs, step_t, need))
            NCELL = len(cells)
            GATES = [(0, 2, 3) if c[4] == 0 else (0, 2, 1, 3) for c in cells]
            gate_no = []
            for gs in GATES:
                gate_no.append({x: sum(map(len, gate_no)) + j + 1 for j, x in enumerate(gs)})
            GATES_GROUP = sum(map(len, GATES))

            def bank_reader(n, gate):
                m = n - 2
                while True:
                    if gate in gate_no[m % NCELL]:
                        return gate_no[m % NCELL][gate] + (0 if m >= 0 else -GATES_GROUP)
                    m -= 2

            l_gate, l_act, l_prod, l_c, l_tc, l_h, l_t, l_x = (
                sem(f"s1_{n}") for n in ("gate", "act", "prod", "c", "tc", "hid", "tr", "xadd"))
            ln = LayerNormSems("ln2")

            with ExitStack() as qctx, nc.Block() as block:
                LG = qctx.enter_context(nc.sbuf_tensor("LG", [P, 2, 4, NODES], F32))
                GA = qctx.enter_context(nc.sbuf_tensor("GA", [P, 2, 4, NODES], F32))
                CC = qctx.enter_context(nc.sbuf_tensor("CC", [P, 2, NODES], F32))
                HB = qctx.enter_context(nc.sbuf_tensor("HB", [P, 2, NODES], F32))
                IG = qctx.enter_context(nc.sbuf_tensor("IG", [P, NODES], F32))
                FC = qctx.enter_context(nc.sbuf_tensor("FC", [P, NODES], F32))
                TC = qctx.enter_context(nc.sbuf_tensor("TC", [P, 2, NODES], F32))
                psl = qctx.enter_context(nc.psum_tensor("psl", [P, 2, 4, NODES], F32))

                def windows(p, tensor, b0, nb, step_t):
                    nw = NODES // p
                    return tensor[:, b0:b0 + nb, step_t:(nw - 1) * p + step_t + 1:p]

                def flat(p, ap, nb):
                    nw = NODES // p
                    return ap[:, 0:nb * nw].rearrange("q (b j) -> q b j", b=nb)

                def groups(eng, body):
                    with eng.Fori(0, GRAPHS // 8) as i:
                        for par in range(2):
                            body(2 * i + par, par)

                def before(n):
                    return max(m for m in range(n) if cells[m][0:2] == cells[n][0:2])

                @block.tensor
                def _(pe):
                    def x_part(q, par, n):
                        p, c, b0, nb, step_t, need = cells[n]
                        if need is not None:
                            pe.wait_ge(l_h, NCELL * q + need + 1)
                        if n < 2:
                            pe.wait_ge(l_x, 4 * q + 4)
                        for gate in GATES[n]:
                            pe.wait_ge(l_act, GATES_GROUP * (q + 1) + bank_reader(n, gate))
                            src = HF[:, bass.ds(4 * q + b0, 1), :] if p == 1 else windows(p, LG[:, par], b0, nb, step_t)
                            last = t.matmul(flat(p, psl[:, n % 2, gate, :], nb), WT[:, T_WIH + 4 * (p - 1) + gate, :], src,
                                            start=True, stop=step_t == 0)
                            if step_t == 0:
                                last.then_inc(l_gate, 1)

                    def h_part(q, n):
                        p, c, b0, nb, step_t, need = cells[n]
                        pe.wait_ge(l_h, NCELL * q + before(n) + 1)
                        for gate in GATES[n]:
                            t.matmul(flat(p, psl[:, n % 2, gate, :], nb), WT[:, T_WHH + 4 * (p - 1) + gate, :],
                                     flat(p, HB[:, c, :], nb), start=False, stop=True).then_inc(l_gate, 1)

                    def body(q, par):
                        ahead = False
                        for n in range(NCELL):
                            if not ahead:
                                x_part(q, par, n)
                            ahead = False
                            if cells[n][4] > 0:
                                if n + 1 < NCELL and cells[n + 1][4] > 0 and cells[n + 1][5] < before(n):
                                    x_part(q, par, n + 1)
                                    ahead = True
                                h_part(q, n)
                        pe.wait_ge(l_h, NCELL * q + NCELL)
                        for b in range(4):
                            transposes(psl[:, 0, b, :].rearrange("p (t d) -> p t d", t=NT),
                                       [LG[:, par, b, i * P:(i + 1) * P] for i in range(NT)]).then_inc(l_t, 1)
                    groups(pe, body)

                @block.scalar
                def _(act):
                    act.sem_inc(l_act, GATES_GROUP)

                    def body(q, par):
                        for n in range(NCELL):
                            p, c, b0, nb, step_t, need = cells[n]
                            w = nb * (NODES // p)
                            for gate in GATES[n]:
                                act.wait_ge(l_gate, GATES_GROUP * q + gate_no[n][gate])
                                a.activation(GA[:, n % 2, gate, 0:w], psl[:, n % 2, gate, 0:w],
                                             ACT.Tanh if gate == 2 else ACT.Sigmoid,
                                             bias=GB[:, 4 * (p - 1) + gate:4 * (p - 1) + gate + 1]).then_inc(l_act, 1)
                            act.wait_ge(l_c, NCELL * q + n + 1)
                            a.activation(TC[:, n % 2, 0:w], CC[:, (c if p > 1 else n) % 2, 0:w], ACT.Tanh).then_inc(l_tc, 1)
                    groups(act, body)

                @block.vector
                def _(dve):
                    dve.sem_inc(l_x, 4)
                    PRODS = sum(c[4] > 0 for c in cells)

                    def body(q, par):
                        prods = 0
                        for n in range(NCELL):
                            p, c, b0, nb, step_t, need = cells[n]
                            w = nb * (NODES // p)
                            gates = GA[:, n % 2, :, 0:w]
                            cc = CC[:, (c if p > 1 else n) % 2, 0:w]
                            dve.wait_ge(l_act, GATES_GROUP * (q + 1) + gate_no[n][1 if step_t else 2])
                            if step_t == 0:
                                v.tensor_tensor(cc, gates[:, 0], gates[:, 2], ALU.mult).then_inc(l_c, 1)
                            else:
                                v.tensor_tensor(IG[:, 0:w], gates[:, 0], gates[:, 2], ALU.mult)
                                v.tensor_tensor(FC[:, 0:w], gates[:, 1], cc, ALU.mult).then_inc(l_prod, 1)
                                prods += 1
                                dve.wait_ge(l_prod, PRODS * q + prods)
                                v.tensor_tensor(cc, IG[:, 0:w], FC[:, 0:w], ALU.add).then_inc(l_c, 1)
                            dve.wait_ge(l_tc, NCELL * q + n + 1)
                            dst = windows(p, LG[:, par], b0, nb, step_t) if step_t == p - 1 else flat(p, HB[:, c, :], nb)
                            v.tensor_tensor(dst, flat(p, gates[:, 3], nb), flat(p, TC[:, n % 2, :], nb), ALU.mult).then_inc(l_h, 1)
                        for b in range(4):
                            dve.wait_ge(l_t, 4 * q + b + 1)
                            xb = X[:, bass.ds(16 * q + 4 * b, 4), :]
                            v.tensor_tensor(xb, xb, psl[:, 0, b, :].rearrange("p (t d) -> p t d", t=NT), ALU.add).then_inc(l_x, 1)
                        for b in range(4):
                            dve_x_stats(dve, ln, 4 * q + b, b, l_x, 5)
                    groups(dve, body)

                @block.gpsimd
                def _(pool):
                    pool.sem_inc(ln.free, 2)
                    every(pool, lambda b, slot: pool_x_rstd(pool, ln, b, slot))

        if LAST_STAGE >= 2:
            f_norm, f_t, f_tc, f_z, f_zc, f_f, f_fc, f_o, f_u, f_w, f_x, f_free = (
                sem(f"s2_{n}") for n in ("norm", "t", "tc", "z", "zc", "f", "fc", "o", "u", "w", "x", "free"))
            ln = LayerNormSems("ln3")
            with ExitStack() as qctx, nc.Block() as block:
                hn = qctx.enter_context(nc.sbuf_tensor("s2_hn", [P, 4, NT, D], F32))
                hF = qctx.enter_context(nc.sbuf_tensor("s2_hF", [P, 2, NODES], F32))
                h1F = qctx.enter_context(nc.sbuf_tensor("s2_h1F", [P, 2, NODES], F32))
                z = qctx.enter_context(nc.sbuf_tensor("s2_z", [P, 2, NT, D], F32))
                u = qctx.enter_context(nc.sbuf_tensor("s2_u", [P, 2, NT, D], F32))
                w = qctx.enter_context(nc.sbuf_tensor("s2_w", [P, 2, NT, D], F32))
                psa = qctx.enter_context(nc.psum_tensor("s2_psa", [P, 2, NODES], F32))
                psz = qctx.enter_context(nc.psum_tensor("s2_psz", [P, 2, NT, D], F32))
                pso = qctx.enter_context(nc.psum_tensor("s2_pso", [P, 2, NT, D], F32))

                @block.scalar
                def _(act):
                    for k in range(2):
                        act_norm_relu(k, hn[:, k]).then_inc(f_norm, 1)

                    def body(b, slot, more):
                        for k in range(2):
                            act.wait_ge(f_t, b + k + 1)
                            a.activation(hF[:, k, :], psa[:, k, :], ACT.Copy).then_inc(f_tc, 1)
                        for k in range(2):
                            act.wait_ge(f_f, b + k + 1)
                            a.activation(h1F[:, k, :], psa[:, k, :], ACT.Relu, bias=col("L2_b1")).then_inc(f_fc, 1)
                        if more:
                            for k in range(2):
                                act.wait_ge(f_free, b + k + 3)
                                alone(act)
                                act_norm_relu(b + 2 + k, hn[:, (slot + 2 + k) % 4]).then_inc(f_norm, 1)
                    pairs(act, body)

                @block.tensor
                def _(pe):
                    def body(b, slot, more):
                        for k in range(2):
                            pe.wait_ge(f_norm, b + k + 1)
                            transposes(psa[:, k, :].rearrange("p (t d) -> p t d", t=NT),
                                       [hn[:, slot + k, i, :] for i in range(NT)]).then_inc(f_t, 1)
                        for k in range(2):
                            pe.wait_ge(f_tc, b + k + 1)
                            to_node_major(psz[:, k], hF[:, k, :], wsq("L2_w1_neigh")).then_inc(f_z, 1)
                        for k in range(2):
                            pe.wait_ge(f_zc, 2 * b + k + 1)
                            over_nodes(psa[:, k, :], z[:, k], adjT, stop=False)
                            t.matmul(psa[:, k, :], wsq("L2_w1_loop"), hF[:, k, :], start=False, stop=True).then_inc(f_f, 1)
                        for k in range(2):
                            pe.wait_ge(f_fc, b + k + 1)
                            to_node_major(psz[:, k], h1F[:, k, :], wsq("L2_w2_neigh")).then_inc(f_z, 1)
                        for k in range(2):
                            pe.wait_ge(f_zc, 2 * b + 2 + k + 1)
                            pe.wait_ge(f_u, b + k + 1)
                            for i in range(NT):
                                for m in range(NT):
                                    t.matmul(pso[:, k, i, :], adjT[:, m, i * P:(i + 1) * P], z[:, k, m, :], start=m == 0, stop=False)
                                last = t.matmul(pso[:, k, i, :], h1F[:, k, i * P:(i + 1) * P], wsq("L2_w2_loop"), start=False, stop=True)
                            last.then_inc(f_o, 1)
                    pairs(pe, body)

                @block.vector
                def _(dve):
                    dve.sem_inc(f_u, 2)
                    dve.sem_inc(f_x, 2)
                    dve.sem_inc(f_free, 4)

                    def body(b, slot, more):
                        for layer in range(2):
                            for k in range(2):
                                dve.wait_ge(f_z, 2 * b + 2 * layer + k + 1)
                                v.tensor_copy(z[:, k], psz[:, k]).then_inc(f_zc, 1)
                        for k in range(2):
                            dve.wait_ge(f_o, b + k + 1)
                            v.tensor_tensor(u[:, k], pso[:, k], row4("L2_b2"), ALU.add).then_inc(f_u, 1)
                            dve.wait_ge(f_u, b + k + 3)
                            v.scalar_tensor_tensor(w[:, k], u[:, k], 0.0, hn[:, slot + k], ALU.max, ALU.add).then_inc(f_w, 1)
                            dve.wait_ge(f_w, b + k + 1)
                            v.tensor_scalar(u[:, k], w[:, k], 0.5, None, ALU.mult).then_inc(f_free, 1)
                            dve.wait_ge(f_free, b + k + 5)
                            xb = X[:, bass.ds(4 * b + 4 * k, 4), :]
                            v.tensor_tensor(xb, xb, u[:, k], ALU.add).then_inc(f_x, 1)
                            dve_x_stats(dve, ln, b + k, k, f_x)
                    pairs(dve, body)

                @block.gpsimd
                def _(pool):
                    pool.sem_inc(ln.free, 2)
                    every(pool, lambda b, slot: pool_x_rstd(pool, ln, b, slot))

        if LAST_STAGE >= 3:
            with ExitStack() as pctx:
                X2 = pctx.enter_context(nc.sbuf_tensor("X2", [P, TILES, D], F32))

                p_norm, p_xp, p_xpc, p_wc, p_y, p_aff, p_mul, p_add, p_max, p_x1 = (
                    sem(f"s3_{n}") for n in ("norm", "xp", "xpc", "wc", "y", "aff", "mul", "add", "max", "x1"))
                p_t, p_tc, p_q, p_qc, p_k, p_kc, p_v, p_vc = (
                    sem(f"s3_{n}") for n in ("t", "tc", "q", "qc", "k", "kc", "v", "vc"))
                at_s, at_m, at_e, at_t, at_pd, at_pa, at_pv, at_r, at_o = (
                    sem(f"at_{n}") for n in ("s", "m", "e", "t", "pd", "pa", "pv", "r", "o"))
                q_t, q_tc, q_wo, q_z, q_zz, q_aff, q_mul, q_x2 = (
                    sem(f"s3q_{n}") for n in ("t", "tc", "wo", "z", "zz", "aff", "mul", "x2"))
                ln1, ln2 = LayerNormSems("ln4"), LayerNormSems("ln5")

                with ExitStack() as qctx, nc.Block() as block:
                    def qsb(name, shape):
                        return qctx.enter_context(nc.sbuf_tensor("s3_" + name, shape, F32))

                    hn = qsb("hn", [P, 2, NT, D])
                    xpF = qsb("xpF", [P, NODES])
                    Y = qsb("Y", [P, NT, D])
                    Y1 = qsb("Y1", [P, NT, D])
                    x1 = qsb("x1", [P, 2, NT, D])
                    x1F = qsb("x1F", [P, NODES])
                    qF = qsb("qF", [P, 2, NODES])
                    kF = qsb("kF", [P, 2, NODES])
                    vT = qsb("vT", [P, 2, NT, D])
                    SM = qsb("SM", [P, 2, HEADS, NODES])
                    MN = qsb("MN", [P, 2, HEADS])
                    SUM = qsb("SUM", [P, 2, HEADS])
                    RS = qsb("RS", [P, 2, HEADS])
                    PT = qsb("PT", [P, 2, NT, P])
                    oT = qsb("oT", [P, 2, NT, D])
                    oF = qsb("oF", [P, NODES])
                    Z = qsb("Z", [P, NT, D])
                    Z1 = qsb("Z1", [P, NT, D])
                    rstd1 = qsb("rstd1", [P, NT])
                    nb1 = qsb("nb1", [P, NT])
                    rstd2 = qsb("rstd2", [P, NT])
                    nb2 = qsb("nb2", [P, NT])
                    pss = qctx.enter_context(nc.psum_tensor("s3_pss", [P, HEADS, NODES], F32))
                    pst = qctx.enter_context(nc.psum_tensor("s3_pst", [P, 2, NT, P], F32))
                    pso = qctx.enter_context(nc.psum_tensor("s3_pso", [P, D], F32))
                    ps1 = qctx.enter_context(nc.psum_tensor("s3_ps1", [P, NODES], F32))
                    ps1t = ps1[:].rearrange("p (t d) -> p t d", t=NT)


                    def run(eng, first, unit, last):
                        first()
                        def graph(b, s, tail, head):
                            for nt in range(NT):
                                unit(b, s, nt, tail, head, head or nt < NT - 1)
                        graph(0, 0, False, True)
                        with eng.Fori(0, GRAPHS // 2 - 1) as i:
                            graph(2 * i + 1, 1, True, True)
                            graph(2 * i + 2, 0, True, True)
                        graph(GRAPHS - 1, 1, True, False)
                        last()

                    @block.tensor
                    def _(pe):
                        def head_step(place, c, s):
                            if place == 1:
                                pe.wait_ge(p_norm, c + 1)
                                over_nodes(ps1[:], hn[:, s], LT).then_inc(p_xp, 1)
                            if place == 2:
                                pe.wait_ge(p_xpc, c + 1)
                                to_node_major(ps1t, xpF[:], wsq("L3_Wc")).then_inc(p_wc, 1)
                            if place == 4:
                                pe.wait_ge(p_x1, c + 1)
                                transposes(ps1t, [x1[:, s, i, :] for i in range(NT)]).then_inc(p_t, 1)
                            if place == 5:
                                pe.wait_ge(p_tc, c + 1)
                                t.matmul(ps1[:], wsq("L3_Wq"), x1F[:], start=True, stop=True).then_inc(p_q, 1)
                                pe.wait_ge(p_qc, c + 1)
                                t.matmul(ps1[:], wsq("L3_Wk"), x1F[:], start=True, stop=True).then_inc(p_k, 1)
                            if place == 6:
                                pe.wait_ge(p_kc, c + 1)
                                to_node_major(ps1t, x1F[:], wsq("L3_Wv")).then_inc(p_v, 1)

                        def tail_step(place, c, s):
                            if place == 0:
                                pe.wait_ge(at_o, 4 * c + 5)
                                transposes(ps1t, [oT[:, s, i, :] for i in range(NT)]).then_inc(q_t, 1)
                            if place == 3:
                                pe.wait_ge(q_tc, c + 1)
                                to_node_major(ps1t, oF[:], wsq("L3_Wo")).then_inc(q_wo, 1)

                        def scores(u, s, nt, h):
                            rows = slice(HD * h, HD * h + HD)
                            t.matmul(pss[:, h, :], qF[rows, s, nt * P:(nt + 1) * P], kF[rows, s, :], start=True, stop=True).then_inc(at_s, 1)

                        def side(place, b, s, tail, head):
                            if tail and place in (0, 3):
                                if place == 0:
                                    pe.wait_ge(p_vc, b + 1)
                                else:
                                    pe.wait_ge(p_y, b + 1 + (1 if head else 0))
                                tail_step(place, b - 1, 1 - s)
                            if head:
                                if place == 1:
                                    pe.wait_ge(p_vc, b + 1)
                                    if tail:
                                        pe.wait_ge(q_tc, b)
                                if place == 4 and tail:
                                    pe.wait_ge(q_z, b)
                                head_step(place, b + 1, 1 - s)

                        def unit(b, s, nt, tail, head, more):
                            u = 4 * b + nt
                            for h in range(HEADS):
                                if more:
                                    if nt == NT - 1 and h == 0:
                                        pe.wait_ge(p_kc, b + 2)
                                    pe.wait_ge(at_m, 4 * u + h + 1)
                                    scores(u + 1, s if nt < NT - 1 else 1 - s, (nt + 1) % NT, h)
                                pe.wait_ge(at_e, 4 * u + h + 1)
                                transposes(pst[:, h % 2], [SM[:, nt % 2, h, m * P:(m + 1) * P] for m in range(NT)]).then_inc(at_t, 1)
                                if h:
                                    weighted(u, b, s, h - 1)
                                if h % 2:
                                    side(2 * nt + h // 2, b, s, tail, head)
                            weighted(u, b, s, HEADS - 1)

                        def weighted(u, b, s, h):
                            pe.wait_ge(at_pa if h % 2 else at_pd, 2 * u + h // 2 + 1)
                            if h == 0:
                                pe.wait_ge(at_o, u + 1)
                                pe.wait_ge(p_vc, b + 1)
                            for m in range(NT):
                                last = t.matmul(pso[:, HD * h:HD * h + HD], PT[:, h % 2, m, :], vT[:, s, m, HD * h:HD * h + HD],
                                                start=m == 0, stop=m == NT - 1)
                            if h == HEADS - 1:
                                last.then_inc(at_pv, 1)

                        def first():
                            for place in (1, 2, 4, 5, 6):
                                head_step(place, 0, 0)
                            for h in range(HEADS):
                                scores(0, 0, 0, h)

                        def last():
                            for place in (0, 3):
                                if place == 0:
                                    pe.wait_ge(q_z, GRAPHS - 1)
                                tail_step(place, GRAPHS - 1, 1)
                        run(pe, first, unit, last)

                    @block.scalar
                    def _(act):
                        def normalize(c, s):
                            act_norm_relu(c, hn[:, s]).then_inc(p_norm, 1)

                        def affine(dst, src, rstd, nb):
                            for i in range(NT):
                                last = a.activation(dst[:, i, :], src[:, i, :], ACT.Identity, bias=nb[:, i:i + 1], scale=rstd[:, i:i + 1])
                            return last

                        def head_step(place, c, s):
                            if place == 1:
                                act.wait_ge(p_xp, c + 1)
                                a.activation(xpF[:], ps1[:], ACT.Copy).then_inc(p_xpc, 1)
                            if place == 3:
                                act.wait_ge(ln1.bias, c + 1)
                                affine(Y1, Y, rstd1, nb1).then_inc(p_aff, 1)
                            if place == 4:
                                act.wait_ge(p_t, c + 1)
                                a.activation(x1F[:], ps1[:], ACT.Copy).then_inc(p_tc, 1)
                            if place == 5:
                                act.wait_ge(p_k, c + 1)
                                a.activation(kF[:, s, :], ps1[:], ACT.Copy).then_inc(p_kc, 1)
                            if place == 6:
                                act.wait_ge(p_v, c + 1)
                                a.activation(vT[:, s], ps1t, ACT.Copy).then_inc(p_vc, 1)

                        def tail_step(place, c, s):
                            if place == 0:
                                act.wait_ge(q_t, c + 1)
                                a.activation(oF[:], ps1[:], ACT.Copy).then_inc(q_tc, 1)
                            if place == 5:
                                act.wait_ge(ln2.bias, c + 1)
                                affine(Z1, Z, rstd2, nb2).then_inc(q_aff, 1)

                        def exps(u, nt, h):
                            act.wait_ge(at_m, 4 * u + h + 1)
                            a.activation(SM[:, nt % 2, h, :], SM[:, nt % 2, h, :], ACT.Exp, bias=MN[:, nt % 2, h:h + 1], scale=-1.0,
                                         accum_out=SUM[:, nt % 2, h:h + 1]).then_inc(at_e, 1)

                        def unit(b, s, nt, tail, head, more):
                            u = 4 * b + nt
                            for h in range(HEADS):
                                if more:
                                    exps(u + 1, (nt + 1) % NT, h)
                                if nt == 0 and h == 0 and head:
                                    normalize(b + 1, 1 - s)
                                if h % 2:
                                    act.wait_ge(at_t, 4 * u + h + 1)
                                    a.activation(PT[:, 1], pst[:, 1], ACT.Copy).then_inc(at_pa, 1)
                                    if tail:
                                        tail_step(2 * nt + h // 2, b - 1, 1 - s)
                                    if head:
                                        head_step(2 * nt + h // 2, b + 1, 1 - s)

                        def first():
                            normalize(0, 0)
                            for place in (1, 3, 4, 5, 6):
                                head_step(place, 0, 0)
                            for h in range(HEADS):
                                exps(0, 0, h)

                        def last():
                            for place in (0, 5):
                                tail_step(place, GRAPHS - 1, 1)
                        run(act, first, unit, last)

                    @block.vector
                    def _(dve):
                        dve.sem_inc(at_o, 1)

                        def head_step(place, c, s):
                            if place == 2:
                                dve.wait_ge(p_wc, c + 1)
                                v.tensor_tensor(Y[:], ps1t, row4("L3_bc"), ALU.add).then_inc(p_y, 1)
                                dve.wait_ge(p_y, c + 1)
                                dve_row_stats(dve, ln1, c, 0, lambda i: Y[:, i, :])
                            if place == 3:
                                dve.wait_ge(p_aff, c + 1)
                                v.tensor_tensor(Y1[:], Y1[:], row4("L3_g1"), ALU.mult).then_inc(p_mul, 1)
                                dve.wait_ge(p_mul, c + 1)
                                v.tensor_tensor(Y1[:], Y1[:], row4("L3_be1"), ALU.add).then_inc(p_add, 1)
                                dve.wait_ge(p_add, c + 1)
                                v.scalar_tensor_tensor(x1[:, s], Y1[:], 0.0, hn[:, s], ALU.max, ALU.add).then_inc(p_x1, 1)
                            if place == 5:
                                dve.wait_ge(p_q, c + 1)
                                v.tensor_tensor(qF[:, s, :], ps1[:], ANYB[:], ALU.mult).then_inc(p_qc, 1)

                        def tail_step(place, c, s):
                            if place == 3:
                                dve.wait_ge(q_wo, c + 1)
                                v.tensor_tensor(Z[:], ps1t, row4("L3_bo"), ALU.add).then_inc(q_z, 1)
                                dve.wait_ge(q_z, c + 1)
                                v.tensor_tensor(Z[:], Z[:], x1[:, s], ALU.add).then_inc(q_zz, 1)
                                dve.wait_ge(q_zz, c + 1)
                                dve_row_stats(dve, ln2, c, 1, lambda i: Z[:, i, :])
                            if place == 6:
                                dve.wait_ge(q_aff, c + 1)
                                v.tensor_tensor(Z1[:], Z1[:], row4("L3_g2"), ALU.mult).then_inc(q_mul, 1)
                                dve.wait_ge(q_mul, c + 1)
                                v.tensor_tensor(X2[:, bass.ds(4 * c, 4), :], Z1[:], row4("L3_be2"), ALU.add).then_inc(q_x2, 1)

                        def mask(u, nt, h):
                            dve.wait_ge(at_s, 4 * u + h + 1)
                            alone(dve)
                            v.tensor_tensor_reduce(out=SM[:, nt % 2, h, :], in0=pss[:, h, :], in1=NB[:, nt, :], scale=-SCALE,
                                                   scalar=3e38, op0=ALU.add, op1=ALU.min,
                                                   accum_out=MN[:, nt % 2, h:h + 1]).then_inc(at_m, 1)

                        def unit(b, s, nt, tail, head, more):
                            u = 4 * b + nt
                            for h in range(HEADS):
                                if more:
                                    mask(u + 1, (nt + 1) % NT, h)
                                if h % 2 == 0:
                                    dve.wait_ge(at_t, 4 * u + h + 1)
                                    v.tensor_copy(PT[:, 0], pst[:, 0]).then_inc(at_pd, 1)
                                else:
                                    if tail:
                                        tail_step(2 * nt + h // 2, b - 1, 1 - s)
                                    if head:
                                        head_step(2 * nt + h // 2, b + 1, 1 - s)
                            dve.wait_ge(at_pv, u + 1)
                            v.reciprocal(RS[:, nt % 2, :], SUM[:, nt % 2, :]).then_inc(at_r, 1)
                            dve.wait_ge(at_r, u + 1)
                            v.tensor_tensor(oT[:, s, nt, :].rearrange("p (h e) -> p h e", h=HEADS),
                                            pso[:].rearrange("p (h e) -> p h e", h=HEADS),
                                            RS[:, nt % 2, :].unsqueeze(2).to_broadcast([P, HEADS, HD]), ALU.mult).then_inc(at_o, 1)

                        def first():
                            for place in (2, 3, 5):
                                head_step(place, 0, 0)
                            for h in range(HEADS):
                                mask(0, 0, h)

                        def last():
                            for place in (3, 6):
                                tail_step(place, GRAPHS - 1, 1)
                        run(dve, first, unit, last)

                    @block.gpsimd
                    def _(pool):
                        pool.sem_inc(ln1.free, 2)
                        pool.sem_inc(ln2.free, 2)

                        def head_step(c):
                            pool_rstd(pool, ln1, c, 0, rstd1[:], nb1[:])

                        def tail_step(c):
                            pool_rstd(pool, ln2, c, 1, rstd2[:], nb2[:])
                        head_step(0)
                        head_step(1)
                        with pool.Fori(1, GRAPHS - 1) as b:
                            head_step(b + 1)
                            tail_step(b - 1)
                        tail_step(GRAPHS - 2)
                        tail_step(GRAPHS - 1)

                m_x, m_free, m_t, m_tc, m_w1, m_g, m_w2, m_z, m_zz, m_aff, m_mul, m_add, m_out = (
                    sem(f"s4_{n}") for n in ("x", "free", "t", "tc", "w1", "g", "w2", "z", "zz", "aff", "mul", "add", "out"))
                m_st = [sem(f"s4_st{n}") for n in range(2)]
                ln = LayerNormSems("ln6")
                with ExitStack() as qctx, nc.Block() as block:
                    def qsb(name, shape):
                        return qctx.enter_context(nc.sbuf_tensor("s4_" + name, shape, F32))

                    xs = qsb("xs", [P, 4, NT, D])
                    xF = qsb("xF", [P, 2, NODES])
                    gF = qsb("gF", [P, 2, 2, NODES])
                    Z = qsb("Z", [P, 2, NT, D])
                    Z1 = qsb("Z1", [P, 2, NT, D])
                    O = qsb("O", [P, 2, NT, D])
                    rs = qsb("rs", [P, 2, NT])
                    nb = qsb("nb", [P, 2, NT])
                    pst = qctx.enter_context(nc.psum_tensor("s4_pst", [P, 2, NT, P], F32))
                    psh = qctx.enter_context(nc.psum_tensor("s4_psh", [P, 2, 2, NODES], F32))
                    psw = qctx.enter_context(nc.psum_tensor("s4_psw", [P, 2, NT, D], F32))

                    @block.scalar
                    def _(act):
                        def fetch(b, k, slot):
                            a.activation(xs[:, slot], X2[:, bass.ds(4 * (b + k), 4), :], ACT.Copy).then_inc(m_x, 1)
                        for k in range(2):
                            fetch(0, k, k)

                        def body(b, slot, more):
                            for k in range(2):
                                act.wait_ge(m_t, b + k + 1)
                                a.activation(xF[:, k, :], pst[:, k].rearrange("p t d -> p (t d)"), ACT.Copy).then_inc(m_tc, 1)
                            for k in range(2):
                                act.wait_ge(m_w1, b + k + 1)
                                for h in range(2):
                                    last = a.activation(gF[:, k, h, :], psh[:, k, h, :], ACT.Gelu, bias=col("L3_b1", h))
                                last.then_inc(m_g, 1)
                            if more:
                                for k in range(2):
                                    act.wait_ge(m_free, b + k + 3)
                                    alone(act)
                                    fetch(b + 2, k, (slot + 2 + k) % 4)
                            for k in range(2):
                                act.wait_ge(ln.bias, b + k + 1)
                                for i in range(NT):
                                    last = a.activation(Z1[:, k, i, :], Z[:, k, i, :], ACT.Identity, bias=nb[:, k, i:i + 1], scale=rs[:, k, i:i + 1])
                                last.then_inc(m_aff, 1)
                        pairs(act, body)

                    @block.tensor
                    def _(pe):
                        def body(b, slot, more):
                            for k in range(2):
                                pe.wait_ge(m_x, b + k + 1)
                                transposes(pst[:, k], [xs[:, slot + k, i, :] for i in range(NT)]).then_inc(m_t, 1)
                            for k in range(2):
                                pe.wait_ge(m_tc, b + k + 1)
                                for h in range(2):
                                    last = t.matmul(psh[:, k, h, :], W3A[:, h * P:(h + 1) * P], xF[:, k, :], start=True, stop=True)
                                last.then_inc(m_w1, 1)
                            for k in range(2):
                                pe.wait_ge(m_g, b + k + 1)
                                pe.wait_ge(m_z, b + k + 1)
                                for i in range(NT):
                                    for h in range(2):
                                        last = t.matmul(psw[:, k, i, :], gF[:, k, h, i * P:(i + 1) * P], W3B[:, h, :], start=h == 0, stop=h == 1)
                                last.then_inc(m_w2, 1)
                        pairs(pe, body)

                    @block.vector
                    def _(dve):
                        dve.sem_inc(m_z, 2)
                        dve.sem_inc(m_free, 4)

                        def body(b, slot, more):
                            for k in range(2):
                                dve.wait_ge(m_w2, b + k + 1)
                                v.tensor_tensor(Z[:, k], psw[:, k], row4("L3_b2"), ALU.add).then_inc(m_z, 1)
                                dve.wait_ge(m_z, b + k + 3)
                                v.tensor_tensor(Z[:, k], Z[:, k], xs[:, slot + k], ALU.add).then_inc(m_free, 1)
                                dve.wait_ge(m_free, b + k + 5)
                                dve_row_stats(dve, ln, b + k, k, lambda i: Z[:, k, i, :])
                            for k in range(2):
                                dve.wait_ge(m_aff, b + k + 1)
                                v.tensor_tensor(Z1[:, k], Z1[:, k], row4("L3_g3"), ALU.mult).then_inc(m_mul, 1)
                                dve.wait_ge(m_mul, b + k + 1)
                                v.tensor_tensor(Z1[:, k], Z1[:, k], row4("L3_be3"), ALU.add).then_inc(m_add, 1)
                                dve.wait_ge(m_add, b + k + 1)
                                dve.wait_ge(m_st[k], 8 * b + 16)
                                v.tensor_tensor(O[:, k], Z1[:, k], X[:, bass.ds(4 * (b + k), 4), :], ALU.add).then_inc(m_out, 1)
                        pairs(dve, body)

                    @block.gpsimd
                    def _(pool):
                        pool.sem_inc(ln.free, 2)
                        every(pool, lambda b, slot: pool_rstd(pool, ln, b, slot, rs[:, slot, :], nb[:, slot, :]))

                    @block.sync
                    def _(sp):
                        for slot in range(2):
                            sp.sem_inc(m_st[slot], 16)
                        o_view = out.rearrange("b (t p) d -> b p t d", p=P)

                        def body(b, slot):
                            sp.wait_ge(m_out, b + 1)
                            sp.dma_start(o_view[bass.ds(b, 1), :, :, :].rearrange("b p t d -> p (b t) d"), O[:, slot]).then_inc(m_st[slot], 16)
                        every(sp, body)
                        for slot in range(2):
                            sp.wait_ge(m_st[slot], 8 * GRAPHS + 16)
        if LAST_STAGE < 3:
            stored = sem("stored")
            with nc.Block() as block:
                @block.sync
                def _(sp):
                    o_view = out.rearrange("b (t p) d -> p (b t) d", p=P)
                    for q in range(4):
                        sp.dma_start(o_view[:, 16 * q:16 * q + 16, :], X[:, 16 * q:16 * q + 16, :]).then_inc(stored, 16)
                    sp.wait_ge(stored, 64)


_INS = ['x', 'adj', 'L0_gnn_W1', 'L0_gnn_b1', 'L0_gnn_g1', 'L0_gnn_be1', 'L0_gnn_W2', 'L0_gnn_b2', 'L0_gnn_g2',
        'L0_gnn_be2', 'L1_gnn_Wg0', 'L1_gnn_bg0', 'L1_gnn_Wg1', 'L1_gnn_bg1', 'L1_gnn_Wih', 'L1_gnn_Whh',
        'L1_gnn_bih', 'L1_gnn_bhh', 'L2_gnn_w1_loop', 'L2_gnn_w1_neigh', 'L2_gnn_b1', 'L2_gnn_w2_loop',
        'L2_gnn_w2_neigh', 'L2_gnn_b2', 'L3_gnn_Wc', 'L3_gnn_bc', 'L3_gnn_g1', 'L3_gnn_be1', 'L3_gnn_Wq',
        'L3_gnn_Wk', 'L3_gnn_Wv', 'L3_gnn_Wo', 'L3_gnn_bo', 'L3_gnn_g2', 'L3_gnn_be2', 'L3_gnn_W1', 'L3_gnn_b1',
        'L3_gnn_W2', 'L3_gnn_b2', 'L3_gnn_g3', 'L3_gnn_be3']


def kernel(**inputs):
    import numpy as _np
    import concourse.bacc as _bacc
    from concourse import mybir as _mybir
    from concourse.bass_utils import run_bass_kernel_spmd as _run

    nc = _bacc.Bacc("TRN2", target_bir_lowering=False, num_devices=1)
    arrays, handles = {}, {}
    for name in _INS:
        a = _np.ascontiguousarray(inputs[name])
        arrays[f"in_{name}_dram"] = a
        handles[name.replace("_gnn", "")] = nc.dram_tensor(f"in_{name}_dram", a.shape, _mybir.dt.from_np(a.dtype),
                                                           kind="ExternalInput").ap()
    out = nc.dram_tensor("out_0_dram", (GRAPHS, NODES, D), _mybir.dt.float32, kind="ExternalOutput").ap()
    build(nc, handles, out)
    r = _run(nc, [arrays], core_ids=[0])
    return r.results[0]["out_0_dram"]
```

```python
import concourse.bass as bass
from concourse import mybir
from contextlib import ExitStack


P = 128
F32 = mybir.dt.float32
F32R = mybir.dt.float32r
ALU = mybir.AluOpType
ACT = mybir.ActivationFunctionType
X_AXIS = mybir.AxisListType.X

GRAPHS, NODES, D = 16, 512, 128
NT = NODES // P
TILES = GRAPHS * NT
HID = 256
HEADS, HD = 4, 32
EPS = 1e-5
SCALE = 1.0 / (HD ** 0.5)
SQUARINGS = 12
LAST_STAGE = 3

COLS = {}
for _name, _n in (("L0_b1", 2), ("L0_g1", 2), ("L0_be1", 2), ("L0_b2", 1), ("L0_g2", 1), ("L0_be2", 1),
                  ("L1_bg1", 1), ("L2_b1", 1), ("L3_b1", 2), ("L1_bih", 16), ("L1_bhh", 16)):
    COLS[_name] = (sum(n for _, n in COLS.values()), _n)
NCOLS = sum(n for _, n in COLS.values())
ROWS = ["L1_bg0", "L2_b2", "L3_bc", "L3_g1", "L3_be1", "L3_bo", "L3_g2", "L3_be2", "L3_b2", "L3_g3", "L3_be3"]
SQUARE_WEIGHTS = ["L1_Wg0", "L1_Wg1", "L2_w1_loop", "L2_w1_neigh", "L2_w2_loop", "L2_w2_neigh",
                  "L3_Wc", "L3_Wq", "L3_Wk", "L3_Wv", "L3_Wo"]
T_W1, T_W2, T_WIH, T_WHH, T_BLOCKS = 0, 2, 4, 20, 36


def build(nc, d, out):
    with ExitStack() as ctx:
        def sb(name, shape, dt=F32):
            return ctx.enter_context(nc.sbuf_tensor(name, shape, dt))

        def sem(name):
            return ctx.enter_context(nc.semaphore(name))

        X = sb("X", [P, TILES, D])
        MV = sb("MV", [P, 2, NT, 2])
        RSTD = sb("RSTD", [P, TILES])
        NBIAS = sb("NBIAS", [P, TILES])
        ST = sb("ST", [P, 2, NT, 6])
        VE = sb("VE", [P, 2, NT])
        NMEAN = sb("NMEAN", [P, 2, NT])
        MHALF = sb("MHALF", [P, NT])
        ident = sb("ident", [P, P])
        ones = sb("ones", [P, P])
        COL = sb("COL", [P, NCOLS])
        ROW = sb("ROW", [P, len(ROWS), D])
        WSQ = sb("WSQ", [P, len(SQUARE_WEIGHTS), D])
        W3A = sb("W3A", [P, HID])
        W3B = sb("W3B", [P, 2, D])
        adjT = sb("adjT", [P, NT, NODES])
        LT = sb("LT", [P, NT, NODES])
        NB = sb("NB", [P, NT, NODES])
        NS = sb("NS", [P, NT])
        two_over = sb("two_over", [P, 1])
        AFF = sb("AFF", [P, 8])

        early = ctx.enter_context(ExitStack())

        def early_sb(name, shape, dt=F32):
            return early.enter_context(nc.sbuf_tensor(name, shape, dt))

        WT = early_sb("WT", [P, T_BLOCKS, P])
        AhatT = early_sb("AhatT", [P, NT, NODES])
        BM0 = early_sb("BM0", [P, NT, D])
        BM1 = early_sb("BM1", [P, NODES])
        GB = early_sb("GB", [P, 16])

        def col(name, j=0):
            at = COLS[name][0] + j
            return COL[:, at:at + 1]

        def cols(name):
            return COL[:, COLS[name][0]:COLS[name][0] + COLS[name][1]]

        def row4(name):
            return ROW[:, ROWS.index(name), :].unsqueeze(1).to_broadcast([P, NT, D])

        def wsq(name):
            return WSQ[:, SQUARE_WEIGHTS.index(name), :]

        x_loaded, const_ok, passed = sem("x_loaded"), sem("const_ok"), sem("passed")
        v, a, g, t = nc.vector, nc.scalar, nc.gpsimd, nc.tensor

        class LayerNormSems:
            def __init__(self, tag):
                self.stats, self.moments, self.free, self.rstd, self.bias = (
                    sem(f"{tag}_{n}") for n in ("stats", "moments", "free", "rstd", "bias"))
                self.base = 0

            def next(self):
                self.base += GRAPHS

        ln = LayerNormSems("ln")

        def alone(eng):
            eng.sem_inc(passed, 1)

        def dve_row_stats(eng, s, b, k, src):
            for i in range(NT):
                last = v.bn_stats(ST[:, k % 2, i, :], src(i))
            last.then_inc(s.stats, 1)
            eng.wait_ge(s.stats, s.base + b + 1)
            eng.wait_ge(s.free, s.base + b + 1)
            alone(eng)
            for i in range(NT):
                last = v.bn_aggr(MV[:, k % 2, i, :], ST[:, k % 2, i, :])
            last.then_inc(s.moments, 1)

        def pool_rstd(eng, s, b, k, rstd, nbias):
            eng.wait_ge(s.moments, s.base + b + 1)
            alone(eng)
            if nbias is not None:
                g.tensor_scalar(NMEAN[:, k % 2, :], MV[:, k % 2, :, 0], -1.0, 0.0, ALU.mult, ALU.add)
            g.tensor_scalar(VE[:, k % 2, :], MV[:, k % 2, :, 1], 1.0, EPS, ALU.mult, ALU.add).then_inc(s.free, 1)
            eng.wait_ge(s.free, s.base + b + 3)
            alone(eng)
            g.tensor_tensor(rstd, VE[:, k % 2, :], MHALF[:], ALU.pow).then_inc(s.rstd, 1)
            eng.wait_ge(s.rstd, s.base + b + 1)
            alone(eng)
            if nbias is None:
                eng.sem_inc(s.bias, 1)
            else:
                g.tensor_tensor(nbias, NMEAN[:, k % 2, :], rstd, ALU.mult).then_inc(s.bias, 1)

        def dve_x_stats(eng, s, b, k, written=None, ahead=3):
            eng.wait_ge(x_loaded, 16)
            if written is not None:
                eng.wait_ge(written, b + ahead)
                alone(eng)
            dve_row_stats(eng, s, b, k, lambda i: X[:, 4 * b + i, :])

        def pool_x_rstd(eng, s, b, k):
            pool_rstd(eng, s, b, k, RSTD[:, bass.ds(4 * b, 4)], NBIAS[:, bass.ds(4 * b, 4)])

        def act_norm_relu(b, dst):
            for i in range(NT):
                last = a.activation(dst[:, i, :], X[:, 4 * b + i, :], ACT.Relu,
                                    bias=NBIAS[:, bass.ds(4 * b + i, 1)], scale=RSTD[:, bass.ds(4 * b + i, 1)])
            return last

        def over_nodes(ps, node_major, matT, start=True, stop=True):
            for m in range(NT):
                last = t.matmul(ps, node_major[:, m, :], matT[:, m, :],
                                start=start and m == 0, stop=stop and m == NT - 1)
            return last

        def to_node_major(ps, feat, w):
            for i in range(NT):
                last = t.matmul(ps[:, i, :], feat[:, bass.ts(i, P)], w, start=True, stop=True)
            return last

        def transposes(ps, blocks):
            for i, x in enumerate(blocks):
                last = t.transpose(ps[:, i, :], x, ident[:])
            return last

        def pairs(eng, body):
            with eng.Fori(0, GRAPHS // 4 - 1) as i:
                for slot in (0, 2):
                    body(4 * i + slot, slot, True)
            for slot in (0, 2):
                body(GRAPHS - 4 + slot, slot, slot == 0)

        def every(eng, body):
            with eng.Fori(0, GRAPHS // 2) as i:
                for slot in range(2):
                    body(2 * i + slot, slot)

        with ExitStack() as pctx:
            def psb(name, shape, dt=F32):
                return pctx.enter_context(nc.sbuf_tensor(name, shape, dt))

            adjN = psb("adjN", [P, NT, NODES])
            WR = psb("WR", [P, T_BLOCKS, P])
            VR = psb("VR", [NCOLS, P])
            S = psb("S", [P, NT, NODES])
            SH = psb("SH", [P, NT, NODES], F32R)
            SL = psb("SL", [P, NT, NODES], F32R)
            PA = psb("PA", [P, NT, NODES], F32R)
            PB = psb("PB", [P, NT, NODES], F32R)
            junk = psb("junk", [P, NT * NODES])
            tmp = psb("tmp", [P, NT, NODES])
            DG = psb("DG", [P, 2, NT, P])
            sm = psb("sm", [P, 64])
            c11 = psb("c11", [1, 4])
            ps4 = pctx.enter_context(nc.psum_tensor("ps4", [P, NT, NODES], F32))
            psx = pctx.enter_context(nc.psum_tensor("psx", [P, NODES], F32))
            psy = pctx.enter_context(nc.psum_tensor("psy", [P, NODES], F32))
            psb2 = pctx.enter_context(nc.psum_tensor("psb2", [P, 2, NODES], F32))
            rowsum, colsum, diag = sm[:, 0:4], sm[:, 4:8], sm[:, 8:12]
            deg, dinv, any_ = sm[:, 12:16], sm[:, 16:20], sm[:, 20:24]
            rabs, rmax, shift = sm[:, 24:28], sm[:, 28:29], sm[:, 29:30]
            sq, isq, num_den = sm[:, 30:31], sm[:, 31:32], sm[:, 32:34]
            lam, rshift = sm[:, 34:35], sm[:, 35:36]

            d_adj, d_w, d_v = sem("d_adj"), sem("d_w"), sem("d_v")
            ident0, ident_ok = sem("ident0"), sem("ident_ok")
            tr_done, tr_copied = sem("tr_done"), sem("tr_copied")
            dv, deg_ok, dinv_ok = sem("dv"), sem("deg_ok"), sem("dinv_ok")
            diag_ok, bcast_ok = sem("diag_ok"), sem("bcast_ok")
            rmax_ok, rmaxT_ok, c11_ok, shift_ok = sem("rmax_ok"), sem("rmaxT_ok"), sem("c11_ok"), sem("shift_ok")
            m_done, sq_sum, sq_bcast, isq_ok = sem("m_done"), sem("sq_sum"), sem("sq_bcast"), sem("isq_ok")
            m_act = sem("m_act")
            split_ok, sm_ok, nd_ok, nd_bcast = sem("split_ok"), sem("sm_ok"), sem("nd_ok"), sem("nd_bcast")
            lx = ln

            x_view = d["x"].rearrange("b (t p) d -> p (b t) d", p=P)
            N_W = 4 + len(SQUARE_WEIGHTS)
            N_V = len(COLS) + len(ROWS)

            with nc.Block() as block:
                @block.sync
                def _(sp):
                    sp.dma_start(adjN[:], d["adj"].rearrange("(t p) m -> p t m", p=P)).then_inc(d_adj, 16)
                    sp.dma_start(X[:], x_view).then_inc(x_loaded, 16)
                    for name in COLS:
                        at, w = COLS[name]
                        src = d[name]
                        src = src.rearrange("l (g p) -> (l g) p", p=P) if w == 16 else src.rearrange("(c p) -> c p", p=P)
                        sp.dma_start(VR[at:at + w, :], src).then_inc(d_v, 16)
                    for i, name in enumerate(ROWS):
                        sp.dma_start(ROW[:, i, :], d[name].partition_broadcast(P)).then_inc(d_v, 16)

                @block.scalar
                def _(act):
                    act.dma_start(WR[:, T_W1:T_W1 + 2, :], d["L0_W1"].rearrange("(h p) d -> p h d", p=P)).then_inc(d_w, 16)
                    act.dma_start(WR[:, T_W2:T_W2 + 2, :], d["L0_W2"].rearrange("o (h k) -> o h k", h=2)).then_inc(d_w, 16)
                    act.dma_start(WR[:, T_WIH:T_WIH + 16, :], d["L1_Wih"].rearrange("l (g p) d -> p (l g) d", p=P)).then_inc(d_w, 16)
                    act.dma_start(WR[:, T_WHH:T_WHH + 16, :], d["L1_Whh"].rearrange("l (g p) d -> p (l g) d", p=P)).then_inc(d_w, 16)
                    for i, name in enumerate(SQUARE_WEIGHTS):
                        act.dma_start(WSQ[:, i, :], d[name]).then_inc(d_w, 16)
                    act.dma_start(W3A[:], d["L3_W1"]).then_inc(d_v, 16)
                    act.dma_start(W3B[:], d["L3_W2"].rearrange("(h p) d -> p h d", p=P)).then_inc(d_v, 16)
                    def square(i, src, dst, k):
                        if k:
                            act.wait_ge(m_act, 2 * i + 1)
                            a.activation(junk[:], src[:].bitcast(F32).rearrange("p t n -> p (t n)"), ACT.Square,
                                         accum_out=sq).then_inc(sq_sum, 1)
                            act.wait_ge(isq_ok, i + 1)
                            alone(act)
                        for r in range(NT):
                            act.wait_ge(m_done, NT * (2 * i + k) + r + 1)
                            last = a.activation(dst[:, r, :], ps4[:, r, :], ACT.Copy, scale=isq if k else 1.0)
                        last.then_inc(m_act, 1)
                    with act.Fori(0, SQUARINGS // 2) as i:
                        square(i, PA, PB, 0)
                        square(i, PB, PA, 1)
                    act.wait_ge(m_act, SQUARINGS)
                    a.activation(junk[:], PA[:].bitcast(F32).rearrange("p t n -> p (t n)"), ACT.Square,
                                 accum_out=num_den[:, 1:2]).then_inc(nd_ok, 1)

                @block.gpsimd
                def _(pool):
                    g.memset(ident[:], 0.0).then_inc(ident0, 1)
                    g.memset(ones[:], 1.0).then_inc(const_ok, 1)
                    g.memset(MHALF[:], -0.5).then_inc(const_ok, 1)
                    pool.wait_ge(ident0, 1)
                    g.affine_select(out=ident[:], in_=ident[:], compare_op=ALU.not_equal, fill=1.0, base=0,
                                    pattern=[[-1, P]], channel_multiplier=1).then_inc(ident_ok, 1)
                    pool.wait_ge(const_ok, 2)
                    pool.wait_ge(deg_ok, 1)
                    g.tensor_tensor(dinv, deg, MHALF[:], ALU.pow).then_inc(dinv_ok, 1)
                    pool.sem_inc(ln.free, 2)
                    every(pool, lambda b, k: pool_x_rstd(pool, lx, b, k))

                @block.vector
                def _(dve):
                    n = [0]

                    def step(ins):
                        n[0] += 1
                        ins.then_inc(dv, 1)
                        dve.wait_ge(dv, n[0])

                    for m in range(NT):
                        dve.wait_ge(tr_done, m + 1)
                        step(v.tensor_copy(adjT[:, m, :], ps4[:, m, :]))
                    v.reduce_sum(rowsum, adjN[:], X_AXIS)
                    v.reduce_sum(colsum, adjT[:], X_AXIS)
                    for m in range(NT):
                        last = v.tensor_tensor(junk[:, m * P:(m + 1) * P], adjN[:, m, m * P:(m + 1) * P], ident[:], ALU.mult)
                    step(last)
                    step(v.reduce_sum(diag, junk[:, 0:NODES].rearrange("p (t n) -> p t n", t=NT), X_AXIS))
                    step(v.tensor_tensor(deg, rowsum, colsum, ALU.add))
                    step(v.tensor_tensor(deg, deg, diag, ALU.subtract))
                    v.tensor_scalar_add(deg, deg, 1.0).then_inc(deg_ok, 1)
                    for q in range(T_BLOCKS // 4):
                        dve.wait_ge(tr_done, NT + q + 1)
                        v.tensor_copy(WT[:, 4 * q:4 * q + 4, :], (psx, psy)[q % 2][:].rearrange("p (t n) -> p t n", t=4)).then_inc(tr_copied, 1)
                    dve.wait_ge(tr_done, NT + T_BLOCKS // 4 + 1)
                    v.tensor_copy(COL[:], psy[:, 0:NCOLS]).then_inc(tr_copied, 1)
                    step(v.tensor_tensor(S[:], adjN[:], adjT[:], ALU.add))
                    step(v.tensor_scalar(S[:], S[:], 0.5, None, ALU.mult))
                    step(v.tensor_reduce(rabs, S[:], X_AXIS, ALU.add, apply_absolute_value=True))
                    v.reduce_max(rmax, rabs, X_AXIS).then_inc(rmax_ok, 1)
                    dve.wait_ge(rmaxT_ok, 1)
                    v.reduce_max(c11[:, 0:1], psx[0:1, 0:P], X_AXIS).then_inc(c11_ok, 1)
                    dve.wait_ge(rmaxT_ok, 2)
                    step(v.tensor_scalar(shift, psx[:, P:P + 1], 1e-30, None, ALU.max))
                    step(v.reciprocal(rshift, shift))
                    step(v.tensor_scalar(PA[:], S[:], rshift, None, ALU.mult))
                    for m in range(NT):
                        blk = slice(m * P, (m + 1) * P)
                        last = v.scalar_tensor_tensor(PA[:, m, blk], S[:, m, blk], rshift, ident[:], ALU.mult, ALU.add)
                    last.then_inc(shift_ok, 2)

                    def isq_step(i):
                        dve.wait_ge(sq_bcast, i + 1)
                        v.reciprocal(isq, psy[:, 0:1]).then_inc(isq_ok, 1)

                    def x_stats(b0, n):
                        with dve.Fori(0, n // 2) as i:
                            for k in range(2):
                                dve_x_stats(dve, lx, 2 * i + (b0 + k), k)

                    dve.wait_ge(dinv_ok, 1)
                    for j, vec in enumerate((rowsum, dinv)):
                        for m in range(NT):
                            last = v.tensor_scalar(DG[:, j, m, :], ident[:], vec[:, m:m + 1], None, ALU.mult)
                    last.then_inc(diag_ok, 1)
                    step(v.tensor_copy(tmp[:], adjT[:]))
                    for m in range(NT):
                        blk = slice(m * P, (m + 1) * P)
                        last = v.tensor_tensor(tmp[:, m, blk], tmp[:, m, blk], ident[:], ALU.add)
                    step(last)
                    isq_step(0)
                    dve.wait_ge(bcast_ok, 1)
                    for m in range(NT):
                        last = v.scalar_tensor_tensor(AhatT[:, m, :], tmp[:, m, :], dinv[:, m:m + 1], psb2[:, 1, :], ALU.mult, ALU.mult)
                    step(last)
                    dve.wait_ge(d_v, 16 * (N_V + 2))
                    v.tensor_scalar(BM1[:], psb2[:, 0, :], col("L1_bg1"), None, ALU.mult)
                    for m in range(NT):
                        v.tensor_scalar(BM0[:, m, :], ROW[:, ROWS.index("L1_bg0"), :], rowsum[:, m:m + 1], None, ALU.mult)
                    v.tensor_tensor(GB[:], cols("L1_bih"), cols("L1_bhh"), ALU.add)
                    isq_step(1)
                    step(v.tensor_scalar(tmp[:], adjN[:], 0.0, None, ALU.is_gt))
                    step(v.reduce_max(any_, tmp[:], X_AXIS))
                    isq_step(2)
                    step(v.tensor_scalar(tmp[:], tmp[:], 1.0, 1e9, ALU.subtract, ALU.mult))
                    for m in range(NT):
                        v.tensor_scalar(NB[:, m, :], tmp[:, m, :], any_[:, m:m + 1], None, ALU.mult)
                    v.tensor_scalar(NS[:], any_, -SCALE, None, ALU.mult)
                    isq_step(3)
                    step(v.tensor_copy(SH[:], S[:]))
                    v.tensor_tensor(SL[:], S[:], SH[:].bitcast(F32), ALU.subtract).then_inc(split_ok, 1)
                    isq_step(4)
                    x_stats(0, 6)
                    isq_step(5)
                    x_stats(6, 10)
                    dve.wait_ge(sm_ok, 1)
                    v.scalar_tensor_tensor(tmp[:], ps4[:], 1.0, PA[:].bitcast(F32), ALU.mult, ALU.mult,
                                           accum_out=num_den[:, 0:1]).then_inc(nd_ok, 1)
                    dve.wait_ge(nd_bcast, 1)
                    step(v.reciprocal(lam, psy[:, 5:6]))
                    step(v.tensor_tensor(lam, lam, psy[:, 4:5], ALU.mult))
                    step(v.tensor_scalar(lam, lam, 1e-8, None, ALU.add))
                    step(v.reciprocal(two_over[:], lam))
                    v.tensor_scalar(two_over[:], two_over[:], 2.0, None, ALU.mult)

                @block.tensor
                def _(pe):
                    pe.wait_ge(ident_ok, 1)
                    pe.wait_ge(d_adj, 16)
                    for m in range(NT):
                        transposes(ps4[:, m, :].rearrange("p (t n) -> p t n", t=NT),
                                   [adjN[:, i, m * P:(m + 1) * P] for i in range(NT)]).then_inc(tr_done, 1)
                    pe.wait_ge(d_w, 16 * N_W)
                    for q in range(T_BLOCKS // 4):
                        if q >= 2:
                            pe.wait_ge(tr_copied, q - 1)
                        transposes((psx, psy)[q % 2][:].rearrange("p (t n) -> p t n", t=4),
                                   [WR[:, 4 * q + i, :] for i in range(4)]).then_inc(tr_done, 1)
                    pe.wait_ge(tr_copied, T_BLOCKS // 4)
                    pe.wait_ge(d_v, 16 * (N_V + 2))
                    t.transpose(psy[:, 0:NCOLS], VR[:], ident[0:NCOLS, 0:NCOLS]).then_inc(tr_done, 1)
                    pe.wait_ge(tr_copied, T_BLOCKS // 4 + 1)
                    pe.wait_ge(rmax_ok, 1)
                    t.transpose(psx[0:1, 0:P], rmax, ident[:]).then_inc(rmaxT_ok, 1)
                    pe.wait_ge(const_ok, 2)
                    pe.wait_ge(c11_ok, 1)
                    t.matmul(psx[:, P:P + 1], ones[0:1, :], c11[:, 0:1], start=True, stop=True).then_inc(rmaxT_ok, 1)
                    pe.wait_ge(shift_ok, 2)

                    def square(i, src, k):
                        for r in range(NT):
                            for m in range(NT):
                                last = t.matmul(ps4[:, r, :], src[:, m, r * P:(r + 1) * P], src[:, m, :],
                                                start=m == 0, stop=m == NT - 1)
                            last.then_inc(m_done, 1)
                        if k:
                            pe.wait_ge(sq_sum, i + 1)
                            t.matmul(psy[:, 0:1], ones[:], sq, start=True, stop=True).then_inc(sq_bcast, 1)
                        pe.wait_ge(m_act, 2 * i + k + 1)
                        alone(pe)
                    square(0, PA, 0)
                    square(0, PB, 1)
                    pe.wait_ge(diag_ok, 1)
                    for j in range(2):
                        for m in range(NT):
                            last = t.matmul(psb2[:, j, m * P:(m + 1) * P], ones[:], DG[:, j, m, :], start=True, stop=True)
                    last.then_inc(bcast_ok, 1)
                    with pe.Fori(1, SQUARINGS // 2) as i:
                        square(i, PA, 0)
                        square(i, PB, 1)
                    pe.wait_ge(split_ok, 1)
                    for r in range(NT):
                        for part in (SL, SH):
                            for m in range(NT):
                                last = t.matmul(ps4[:, r, :], part[:, m, r * P:(r + 1) * P], PA[:, m, :],
                                                start=part is SL and m == 0, stop=part is SH and m == NT - 1)
                    last.then_inc(sm_ok, 1)
                    pe.wait_ge(nd_ok, 2)
                    t.matmul(psy[:, 4:6], ones[:], num_den, start=True, stop=True).then_inc(nd_bcast, 1)

        with ExitStack() as pctx:
            def psb(name, shape, dt=F32):
                return pctx.enter_context(nc.sbuf_tensor(name, shape, dt))

            H1 = psb("H1", [P, 2, GRAPHS, NODES])
            hn = psb("hn", [P, 4, NT, D])
            agg = psb("agg", [P, 2, NODES])
            hr = psb("hr", [P, 2, 2, NODES])
            bst = psb("bst", [P, 3, GRAPHS, 6])
            bmv = psb("bmv", [P, 3, 2])
            bve = psb("bve", [P, 3])
            Y = H1[:, 0]
            a_norm, a_agg, a_aggc, a_h, a_hc, a_st = (sem(f"s0_{n}") for n in ("norm", "agg", "aggc", "h", "hc", "st"))
            bn_mv, bn_ve, bn_rs, bn_sc, bn_d = (sem(f"s0_{n}") for n in ("bnmv", "bnve", "bnrs", "bnsc", "bnd"))
            b_hr, b_y, b_yc, b_st = (sem(f"s0_{n}") for n in ("hr", "y", "yc", "yst"))
            c_aff, c_t, c_x = (sem(f"s0_{n}") for n in ("aff", "t", "x"))
            ln.next()

            def dve_moments(dve, js, n):
                for j in js:
                    last = v.bn_aggr(bmv[:, j, :], bst[:, j, :, :])
                last.then_inc(bn_mv, 1)
                dve.wait_ge(bn_mv, n)
                v.tensor_scalar(bve[:, js[0]:js[-1] + 1], bmv[:, js[0]:js[-1] + 1, 1], EPS, None, ALU.add).then_inc(bn_ve, 1)

            def dve_affine(dve, js, n, scale, shift, gamma, beta):
                dve.wait_ge(bn_rs, n)
                v.tensor_tensor(scale, bve[:, js[0]:js[-1] + 1], gamma, ALU.mult).then_inc(bn_d, 1)
                dve.wait_ge(bn_d, 2 * n - 1)
                v.tensor_tensor(shift, bmv[:, js[0]:js[-1] + 1, 0], scale, ALU.mult).then_inc(bn_d, 1)
                dve.wait_ge(bn_d, 2 * n)
                v.tensor_tensor(shift, beta, shift, ALU.subtract).then_inc(bn_sc, 1)

            lt_ok = sem("lt_ok")

            with ExitStack() as qctx, nc.Block() as block:
                psg = qctx.enter_context(nc.psum_tensor("s0_psg", [P, 2, NODES], F32))
                psh = qctx.enter_context(nc.psum_tensor("s0_psh", [P, 2, 2, NODES], F32))

                @block.scalar
                def _(act):
                    for k in range(2):
                        act_norm_relu(k, hn[:, k]).then_inc(a_norm, 1)

                    def body(b, slot, more):
                        if more:
                            for k in range(2):
                                act_norm_relu(b + 2 + k, hn[:, (slot + 2 + k) % 4]).then_inc(a_norm, 1)
                        for k in range(2):
                            act.wait_ge(a_agg, b + k + 1)
                            a.activation(agg[:, k, :], psg[:, k, :], ACT.Copy).then_inc(a_aggc, 1)
                    pairs(act, body)

                @block.tensor
                def _(pe):
                    def body(b, slot, more):
                        for k in range(2):
                            pe.wait_ge(a_norm, b + k + 1)
                            over_nodes(psg[:, k, :], hn[:, slot + k], AhatT).then_inc(a_agg, 1)
                        for k in range(2):
                            pe.wait_ge(a_aggc, b + k + 1)
                            pe.wait_ge(a_hc, b + k + 1)
                            for h in range(2):
                                last = t.matmul(psh[:, k, h, :], WT[:, T_W1 + h, :], agg[:, k, :], start=True, stop=True)
                            last.then_inc(a_h, 1)
                    pairs(pe, body)

                @block.gpsimd
                def _(pool):
                    g.tensor_scalar(LT[:], adjT[:], two_over[:], 0.0, ALU.mult, ALU.add).then_inc(lt_ok, 1)
                    pool.wait_ge(lt_ok, 1)
                    alone(pool)
                    for m in range(NT):
                        blk = slice(m * P, (m + 1) * P)
                        g.tensor_tensor(LT[:, m, blk], LT[:, m, blk], ident[:], ALU.subtract)

                @block.vector
                def _(dve):
                    dve.sem_inc(a_hc, 2)

                    def body(b, slot):
                        dve.wait_ge(a_h, b + 1)
                        for h in range(2):
                            last = v.tensor_scalar(H1[:, h, b, :], psh[:, slot, h, :], col("L0_b1", h), None, ALU.add)
                        last.then_inc(a_hc, 1)
                        dve.wait_ge(a_hc, b + 3)
                        for h in range(2):
                            last = v.bn_stats(bst[:, h, b, :], H1[:, h, b, :])
                        last.then_inc(a_st, 1)
                    every(dve, body)
                    dve.wait_ge(a_st, GRAPHS)
                    dve_moments(dve, (0, 1), 1)
                    dve_affine(dve, (0, 1), 1, AFF[:, 0:2], AFF[:, 2:4], cols("L0_g1"), cols("L0_be1"))

                @block.gpsimd
                def _(pool):
                    pool.wait_ge(bn_ve, 1)
                    g.tensor_tensor(bve[:, 0:2], bve[:, 0:2], MHALF[:, 0:2], ALU.pow).then_inc(bn_rs, 1)

            with ExitStack() as qctx, nc.Block() as block:
                psy = qctx.enter_context(nc.psum_tensor("s0_psy", [P, 2, NODES], F32))

                @block.scalar
                def _(act):
                    def body(b, slot):
                        act.wait_ge(b_y, b + 1)
                        for h in range(2):
                            last = a.activation(hr[:, slot, h, :], H1[:, h, b, :], ACT.Relu,
                                                bias=AFF[:, 2 + h:3 + h], scale=AFF[:, h:h + 1])
                        last.then_inc(b_hr, 1)
                    every(act, body)

                @block.tensor
                def _(pe):
                    pe.sem_inc(b_y, 2)

                    def body(b, slot):
                        pe.wait_ge(b_hr, b + 1)
                        pe.wait_ge(b_yc, b + 1)
                        for h in range(2):
                            last = t.matmul(psy[:, slot, :], WT[:, T_W2 + h, :], hr[:, slot, h, :], start=h == 0, stop=h == 1)
                        last.then_inc(b_y, 1)
                    every(pe, body)

                @block.vector
                def _(dve):
                    dve.sem_inc(b_yc, 2)

                    def body(b, slot):
                        dve.wait_ge(b_y, b + 3)
                        v.tensor_scalar(Y[:, b, :], psy[:, slot, :], col("L0_b2"), None, ALU.add).then_inc(b_yc, 1)
                        dve.wait_ge(b_yc, b + 3)
                        v.bn_stats(bst[:, 2, b, :], Y[:, b, :]).then_inc(b_st, 1)
                    every(dve, body)
                    dve.wait_ge(b_st, GRAPHS)
                    dve_moments(dve, (2,), 2)
                    dve_affine(dve, (2,), 2, AFF[:, 4:5], AFF[:, 5:6], cols("L0_g2"), cols("L0_be2"))

                @block.gpsimd
                def _(pool):
                    pool.wait_ge(bn_ve, 2)
                    g.tensor_tensor(bve[:, 2:3], bve[:, 2:3], MHALF[:, 0:1], ALU.pow).then_inc(bn_rs, 1)

            with ExitStack() as qctx, nc.Block() as block:
                pst = qctx.enter_context(nc.psum_tensor("s0_pst", [P, 2, NT, P], F32))

                @block.scalar
                def _(act):
                    def body(b, slot):
                        act.wait_ge(c_t, b + 1)
                        a.activation(agg[:, slot, :], Y[:, b, :], ACT.Identity, bias=AFF[:, 5:6], scale=AFF[:, 4:5]).then_inc(c_aff, 1)
                    every(act, body)

                @block.tensor
                def _(pe):
                    pe.sem_inc(c_t, 2)

                    def body(b, slot):
                        pe.wait_ge(c_aff, b + 1)
                        pe.wait_ge(c_x, b + 1)
                        transposes(pst[:, slot], [agg[:, slot, i * P:(i + 1) * P] for i in range(NT)]).then_inc(c_t, 1)
                    every(pe, body)

                @block.vector
                def _(dve):
                    dve.sem_inc(c_x, 2)

                    def body(b, slot):
                        dve.wait_ge(c_t, b + 3)
                        xb = X[:, bass.ds(4 * b, 4), :]
                        v.tensor_tensor(xb, xb, pst[:, slot], ALU.add).then_inc(c_x, 1)
                        dve_x_stats(dve, ln, b, slot, c_x)
                    every(dve, body)

                @block.gpsimd
                def _(pool):
                    every(pool, lambda b, slot: pool_x_rstd(pool, ln, b, slot))

        with ExitStack() as pctx:
            def psb(name, shape, dt=F32):
                return pctx.enter_context(nc.sbuf_tensor(name, shape, dt))

            HF = psb("HF", [P, GRAPHS, NODES])
            g_norm, g_agg, g_aggc, g_w, g_add, g_relu = (
                sem(f"s1_{n}") for n in ("norm", "agg", "aggc", "w", "add", "relu"))

            with ExitStack() as qctx, nc.Block() as block:
                hn = qctx.enter_context(nc.sbuf_tensor("s1_hn", [P, 4, NT, D], F32))
                agg = qctx.enter_context(nc.sbuf_tensor("s1_agg", [P, 2, NODES], F32))
                pre = qctx.enter_context(nc.sbuf_tensor("s1_pre", [P, 2, 2, NODES], F32))
                h1 = qctx.enter_context(nc.sbuf_tensor("s1_h1", [P, 2, NT, D], F32))
                psa = qctx.enter_context(nc.psum_tensor("s1_psa", [P, 2, NODES], F32))
                psw = qctx.enter_context(nc.psum_tensor("s1_psw", [P, 2, NODES], F32))


                @block.scalar
                def _(act):
                    for k in range(2):
                        act_norm_relu(k, hn[:, k]).then_inc(g_norm, 1)

                    def body(b, slot, more):
                        if more:
                            for k in range(2):
                                act_norm_relu(b + 2 + k, hn[:, (slot + 2 + k) % 4]).then_inc(g_norm, 1)
                        for layer in range(2):
                            for k in range(2):
                                act.wait_ge(g_agg, 2 * b + 2 * layer + k + 1)
                                a.activation(agg[:, k, :], psa[:, k, :], ACT.Copy).then_inc(g_aggc, 1)
                            for k in range(2):
                                act.wait_ge(g_add, 2 * b + 2 * layer + k + 3)
                                dst = h1[:, k].rearrange("p t d -> p (t d)") if layer == 0 else HF[:, b + k, :]
                                a.activation(dst, pre[:, layer, k, :], ACT.Relu).then_inc(g_relu, 1)
                    pairs(act, body)

                @block.tensor
                def _(pe):
                    def body(b, slot, more):
                        for layer in range(2):
                            for k in range(2):
                                if layer == 0:
                                    pe.wait_ge(g_norm, b + k + 1)
                                    over_nodes(psa[:, k, :], hn[:, slot + k], adjT).then_inc(g_agg, 1)
                                else:
                                    pe.wait_ge(g_relu, 2 * b + k + 1)
                                    over_nodes(psa[:, k, :], h1[:, k], adjT).then_inc(g_agg, 1)
                            for k in range(2):
                                pe.wait_ge(g_aggc, 2 * b + 2 * layer + k + 1)
                                pe.wait_ge(g_add, 2 * b + 2 * layer + k + 1)
                                if layer == 0:
                                    to_node_major(psw[:, k, :].rearrange("p (t d) -> p t d", t=NT), agg[:, k, :],
                                                  wsq("L1_Wg0")).then_inc(g_w, 1)
                                else:
                                    t.matmul(psw[:, k, :], wsq("L1_Wg1"), agg[:, k, :], start=True, stop=True).then_inc(g_w, 1)
                    pairs(pe, body)

                @block.vector
                def _(dve):
                    dve.sem_inc(g_add, 2)

                    def body(b, slot, more):
                        for layer in range(2):
                            bias = BM0[:].rearrange("p t d -> p (t d)") if layer == 0 else BM1[:]
                            for k in range(2):
                                dve.wait_ge(g_w, 2 * b + 2 * layer + k + 1)
                                v.tensor_tensor(pre[:, layer, k, :], psw[:, k, :], bias, ALU.add).then_inc(g_add, 1)
                    pairs(dve, body)

            cells = []
            for p in range(1, 5):
                chunk_graphs = {1: 1, 2: 2, 3: 2, 4: 4}[p]
                chunks = 4 // chunk_graphs
                if p == 1:
                    cells += [(1, c, c, 1, 0, None) for c in range(4)]
                    continue
                base = len(cells)
                for step_t in range(p):
                    for c in range(chunks):
                        need = {2: 1 + 2 * c, 3: base - 2 + c, 4: base - 1}[p]
                        cells.append((p, c, c * chunk_graphs, chunk_graphs, step_t, need))
            NCELL = len(cells)
            GATES = [(0, 2, 3) if c[4] == 0 else (0, 2, 1, 3) for c in cells]
            gate_no = []
            for gs in GATES:
                gate_no.append({x: sum(map(len, gate_no)) + j + 1 for j, x in enumerate(gs)})
            GATES_GROUP = sum(map(len, GATES))

            def bank_reader(n, gate):
                m = n - 2
                while True:
                    if gate in gate_no[m % NCELL]:
                        return gate_no[m % NCELL][gate] + (0 if m >= 0 else -GATES_GROUP)
                    m -= 2

            l_gate, l_act, l_prod, l_c, l_tc, l_h, l_t, l_x = (
                sem(f"s1_{n}") for n in ("gate", "act", "prod", "c", "tc", "hid", "tr", "xadd"))
            ln.next()

            with ExitStack() as qctx, nc.Block() as block:
                LG = qctx.enter_context(nc.sbuf_tensor("LG", [P, 2, 4, NODES], F32))
                GA = qctx.enter_context(nc.sbuf_tensor("GA", [P, 2, 4, NODES], F32))
                CC = qctx.enter_context(nc.sbuf_tensor("CC", [P, 2, NODES], F32))
                HB = qctx.enter_context(nc.sbuf_tensor("HB", [P, 2, NODES], F32))
                IG = qctx.enter_context(nc.sbuf_tensor("IG", [P, NODES], F32))
                FC = qctx.enter_context(nc.sbuf_tensor("FC", [P, NODES], F32))
                TC = qctx.enter_context(nc.sbuf_tensor("TC", [P, 2, NODES], F32))
                psl = qctx.enter_context(nc.psum_tensor("psl", [P, 2, 4, NODES], F32))

                def windows(p, tensor, b0, nb, step_t):
                    nw = NODES // p
                    return tensor[:, b0:b0 + nb, step_t:(nw - 1) * p + step_t + 1:p]

                def flat(p, ap, nb):
                    nw = NODES // p
                    return ap[:, 0:nb * nw].rearrange("q (b j) -> q b j", b=nb)

                def groups(eng, body):
                    with eng.Fori(0, GRAPHS // 8) as i:
                        for par in range(2):
                            body(2 * i + par, par)

                def before(n):
                    return max(m for m in range(n) if cells[m][0:2] == cells[n][0:2])

                @block.tensor
                def _(pe):
                    def x_part(q, par, n):
                        p, c, b0, nb, step_t, need = cells[n]
                        if need is not None:
                            pe.wait_ge(l_h, NCELL * q + need + 1)
                        if n < 2:
                            pe.wait_ge(l_x, 4 * q + 4)
                        for gate in GATES[n]:
                            pe.wait_ge(l_act, GATES_GROUP * (q + 1) + bank_reader(n, gate))
                            src = HF[:, bass.ds(4 * q + b0, 1), :] if p == 1 else windows(p, LG[:, par], b0, nb, step_t)
                            last = t.matmul(flat(p, psl[:, n % 2, gate, :], nb), WT[:, T_WIH + 4 * (p - 1) + gate, :], src,
                                            start=True, stop=step_t == 0)
                            if step_t == 0:
                                last.then_inc(l_gate, 1)

                    def h_part(q, n):
                        p, c, b0, nb, step_t, need = cells[n]
                        pe.wait_ge(l_h, NCELL * q + before(n) + 1)
                        for gate in GATES[n]:
                            t.matmul(flat(p, psl[:, n % 2, gate, :], nb), WT[:, T_WHH + 4 * (p - 1) + gate, :],
                                     flat(p, HB[:, c, :], nb), start=False, stop=True).then_inc(l_gate, 1)

                    def body(q, par):
                        ahead = False
                        for n in range(NCELL):
                            if not ahead:
                                x_part(q, par, n)
                            ahead = False
                            if cells[n][4] > 0:
                                if n + 1 < NCELL and cells[n + 1][4] > 0 and cells[n + 1][5] < before(n):
                                    x_part(q, par, n + 1)
                                    ahead = True
                                h_part(q, n)
                        pe.wait_ge(l_h, NCELL * q + NCELL)
                        for b in range(4):
                            transposes(psl[:, 0, b, :].rearrange("p (t d) -> p t d", t=NT),
                                       [LG[:, par, b, i * P:(i + 1) * P] for i in range(NT)]).then_inc(l_t, 1)
                    groups(pe, body)

                @block.scalar
                def _(act):
                    act.sem_inc(l_act, GATES_GROUP)

                    def body(q, par):
                        for n in range(NCELL):
                            p, c, b0, nb, step_t, need = cells[n]
                            w = nb * (NODES // p)
                            for gate in GATES[n]:
                                act.wait_ge(l_gate, GATES_GROUP * q + gate_no[n][gate])
                                a.activation(GA[:, n % 2, gate, 0:w], psl[:, n % 2, gate, 0:w],
                                             ACT.Tanh if gate == 2 else ACT.Sigmoid,
                                             bias=GB[:, 4 * (p - 1) + gate:4 * (p - 1) + gate + 1]).then_inc(l_act, 1)
                            act.wait_ge(l_c, NCELL * q + n + 1)
                            a.activation(TC[:, n % 2, 0:w], CC[:, (c if p > 1 else n) % 2, 0:w], ACT.Tanh).then_inc(l_tc, 1)
                    groups(act, body)

                @block.vector
                def _(dve):
                    dve.sem_inc(l_x, 4)
                    PRODS = sum(c[4] > 0 for c in cells)

                    def body(q, par):
                        prods = 0
                        for n in range(NCELL):
                            p, c, b0, nb, step_t, need = cells[n]
                            w = nb * (NODES // p)
                            gates = GA[:, n % 2, :, 0:w]
                            cc = CC[:, (c if p > 1 else n) % 2, 0:w]
                            dve.wait_ge(l_act, GATES_GROUP * (q + 1) + gate_no[n][1 if step_t else 2])
                            if step_t == 0:
                                v.tensor_tensor(cc, gates[:, 0], gates[:, 2], ALU.mult).then_inc(l_c, 1)
                            else:
                                v.tensor_tensor(IG[:, 0:w], gates[:, 0], gates[:, 2], ALU.mult)
                                v.tensor_tensor(FC[:, 0:w], gates[:, 1], cc, ALU.mult).then_inc(l_prod, 1)
                                prods += 1
                                dve.wait_ge(l_prod, PRODS * q + prods)
                                v.tensor_tensor(cc, IG[:, 0:w], FC[:, 0:w], ALU.add).then_inc(l_c, 1)
                            dve.wait_ge(l_tc, NCELL * q + n + 1)
                            dst = windows(p, LG[:, par], b0, nb, step_t) if step_t == p - 1 else flat(p, HB[:, c, :], nb)
                            v.tensor_tensor(dst, flat(p, gates[:, 3], nb), flat(p, TC[:, n % 2, :], nb), ALU.mult).then_inc(l_h, 1)
                        for b in range(4):
                            dve.wait_ge(l_t, 4 * q + b + 1)
                            xb = X[:, bass.ds(16 * q + 4 * b, 4), :]
                            v.tensor_tensor(xb, xb, psl[:, 0, b, :].rearrange("p (t d) -> p t d", t=NT), ALU.add).then_inc(l_x, 1)
                        for b in range(4):
                            dve_x_stats(dve, ln, 4 * q + b, b, l_x, 5)
                    groups(dve, body)

                @block.gpsimd
                def _(pool):
                    every(pool, lambda b, slot: pool_x_rstd(pool, ln, b, slot))

        early.close()
        if LAST_STAGE >= 2:
            f_norm, f_t, f_tc, f_z, f_zc, f_f, f_fc, f_o, f_u, f_w, f_x, f_free = (
                sem(f"s2_{n}") for n in ("norm", "t", "tc", "z", "zc", "f", "fc", "o", "u", "w", "x", "free"))
            ln.next()
            with ExitStack() as qctx, nc.Block() as block:
                hn = qctx.enter_context(nc.sbuf_tensor("s2_hn", [P, 4, NT, D], F32))
                hF = qctx.enter_context(nc.sbuf_tensor("s2_hF", [P, 2, NODES], F32))
                h1F = qctx.enter_context(nc.sbuf_tensor("s2_h1F", [P, 2, NODES], F32))
                z = qctx.enter_context(nc.sbuf_tensor("s2_z", [P, 2, NT, D], F32))
                u = qctx.enter_context(nc.sbuf_tensor("s2_u", [P, 2, NT, D], F32))
                w = qctx.enter_context(nc.sbuf_tensor("s2_w", [P, 2, NT, D], F32))
                psa = qctx.enter_context(nc.psum_tensor("s2_psa", [P, 2, NODES], F32))
                psz = qctx.enter_context(nc.psum_tensor("s2_psz", [P, 2, NT, D], F32))
                pso = qctx.enter_context(nc.psum_tensor("s2_pso", [P, 2, NT, D], F32))

                @block.scalar
                def _(act):
                    for k in range(2):
                        act_norm_relu(k, hn[:, k]).then_inc(f_norm, 1)

                    def body(b, slot, more):
                        for k in range(2):
                            act.wait_ge(f_t, b + k + 1)
                            a.activation(hF[:, k, :], psa[:, k, :], ACT.Copy).then_inc(f_tc, 1)
                        for k in range(2):
                            act.wait_ge(f_f, b + k + 1)
                            a.activation(h1F[:, k, :], psa[:, k, :], ACT.Relu, bias=col("L2_b1")).then_inc(f_fc, 1)
                        if more:
                            for k in range(2):
                                act.wait_ge(f_free, b + k + 3)
                                alone(act)
                                act_norm_relu(b + 2 + k, hn[:, (slot + 2 + k) % 4]).then_inc(f_norm, 1)
                    pairs(act, body)

                @block.tensor
                def _(pe):
                    def body(b, slot, more):
                        for k in range(2):
                            pe.wait_ge(f_norm, b + k + 1)
                            transposes(psa[:, k, :].rearrange("p (t d) -> p t d", t=NT),
                                       [hn[:, slot + k, i, :] for i in range(NT)]).then_inc(f_t, 1)
                        for k in range(2):
                            pe.wait_ge(f_tc, b + k + 1)
                            to_node_major(psz[:, k], hF[:, k, :], wsq("L2_w1_neigh")).then_inc(f_z, 1)
                        for k in range(2):
                            pe.wait_ge(f_zc, 2 * b + k + 1)
                            over_nodes(psa[:, k, :], z[:, k], adjT, stop=False)
                            t.matmul(psa[:, k, :], wsq("L2_w1_loop"), hF[:, k, :], start=False, stop=True).then_inc(f_f, 1)
                        for k in range(2):
                            pe.wait_ge(f_fc, b + k + 1)
                            to_node_major(psz[:, k], h1F[:, k, :], wsq("L2_w2_neigh")).then_inc(f_z, 1)
                        for k in range(2):
                            pe.wait_ge(f_zc, 2 * b + 2 + k + 1)
                            pe.wait_ge(f_u, b + k + 1)
                            for i in range(NT):
                                for m in range(NT):
                                    t.matmul(pso[:, k, i, :], adjT[:, m, i * P:(i + 1) * P], z[:, k, m, :], start=m == 0, stop=False)
                                last = t.matmul(pso[:, k, i, :], h1F[:, k, i * P:(i + 1) * P], wsq("L2_w2_loop"), start=False, stop=True)
                            last.then_inc(f_o, 1)
                    pairs(pe, body)

                @block.vector
                def _(dve):
                    dve.sem_inc(f_u, 2)
                    dve.sem_inc(f_x, 2)
                    dve.sem_inc(f_free, 4)

                    def body(b, slot, more):
                        for layer in range(2):
                            for k in range(2):
                                dve.wait_ge(f_z, 2 * b + 2 * layer + k + 1)
                                v.tensor_copy(z[:, k], psz[:, k]).then_inc(f_zc, 1)
                        for k in range(2):
                            dve.wait_ge(f_o, b + k + 1)
                            v.tensor_tensor(u[:, k], pso[:, k], row4("L2_b2"), ALU.add).then_inc(f_u, 1)
                            dve.wait_ge(f_u, b + k + 3)
                            v.scalar_tensor_tensor(w[:, k], u[:, k], 0.0, hn[:, slot + k], ALU.max, ALU.add).then_inc(f_w, 1)
                            dve.wait_ge(f_w, b + k + 1)
                            v.tensor_scalar(u[:, k], w[:, k], 0.5, None, ALU.mult).then_inc(f_free, 1)
                            dve.wait_ge(f_free, b + k + 5)
                            xb = X[:, bass.ds(4 * b + 4 * k, 4), :]
                            v.tensor_tensor(xb, xb, u[:, k], ALU.add).then_inc(f_x, 1)
                            dve_x_stats(dve, ln, b + k, k, f_x)
                    pairs(dve, body)

                @block.gpsimd
                def _(pool):
                    every(pool, lambda b, slot: pool_x_rstd(pool, ln, b, slot))

        if LAST_STAGE >= 3:
            with ExitStack() as pctx:
                X2 = pctx.enter_context(nc.sbuf_tensor("X2", [P, TILES, D], F32))

                p_norm, p_xp, p_xpc, p_wc, p_y, p_aff, p_mul, p_add, p_max, p_x1 = (
                    sem(f"s3_{n}") for n in ("norm", "xp", "xpc", "wc", "y", "aff", "mul", "add", "max", "x1"))
                p_t, p_tc, p_q, p_qh, p_ql, p_k, p_kh, p_kl, p_v, p_vc = (
                    sem(f"s3_{n}") for n in ("t", "tc", "q", "qh", "ql", "k", "kh", "kl", "v", "vc"))
                stacked, p_keep, at_x = sem("s3_stacked"), sem("s3_keep"), sem("at_x")
                STACK = 2 * HEADS * 4 * 16
                at_s, at_m, at_e, at_t, at_pd, at_pa, at_pv, at_r, at_rb, at_rt, at_rc, at_o = (
                    sem(f"at_{n}") for n in ("s", "m", "e", "t", "pd", "pa", "pv", "r", "rb", "rt", "rc", "o"))
                q_wo, q_z, q_zz, q_aff, q_mul, q_x2 = (
                    sem(f"s3q_{n}") for n in ("wo", "z", "zz", "aff", "mul", "x2"))
                ln.next()
                ln1, ln2 = ln, LayerNormSems("ln_out")

                with ExitStack() as qctx, nc.Block() as block:
                    def qsb(name, shape, dt=F32):
                        return qctx.enter_context(nc.sbuf_tensor("s3_" + name, shape, dt))

                    hn = qsb("hn", [P, NT, D])
                    xpF = qsb("xpF", [P, NODES])
                    Y = qsb("Y", [P, NT, D])
                    Y1 = qsb("Y1", [P, NT, D])
                    x1 = qsb("x1", [P, NT, D])
                    x1F = qsb("x1F", [P, NODES])
                    qk = qsb("qk", [P, 2, 2, NODES], F32R)
                    QS = qsb("QS", [P, 2, HEADS, NODES], F32R)
                    KS = qsb("KS", [P, 2, HEADS, NODES], F32R)
                    vT = qsb("vT", [P, 2, NT, D])
                    SM = qsb("SM", [P, 2, NT, NODES])
                    MN = qsb("MN", [P, 2, NT])
                    SUM = qsb("SUM", [P, HEADS, NT])
                    RS = qsb("RS", [P, HEADS, NT])
                    RB = qsb("RB", [P, NT, HEADS, HD])
                    RF = qsb("RF", [P, NODES])
                    PT = qsb("PT", [P, 2, NODES])
                    oF = qsb("oF", [P, NODES])
                    Z = qsb("Z", [P, NT, D])
                    Z1 = qsb("Z1", [P, NT, D])
                    rstd1 = qsb("rstd1", [P, NT])
                    rstd2 = qsb("rstd2", [P, NT])
                    nb2 = qsb("nb2", [P, NT])
                    pss = qctx.enter_context(nc.psum_tensor("s3_pss", [P, NT, NODES], F32))
                    pst = qctx.enter_context(nc.psum_tensor("s3_pst", [P, 2, NODES], F32))
                    pso = qctx.enter_context(nc.psum_tensor("s3_pso", [P, NODES], F32))
                    ps1 = qctx.enter_context(nc.psum_tensor("s3_ps1", [P, NODES], F32))
                    ps1t = ps1[:].rearrange("p (t d) -> p t d", t=NT)

                    AHEAD = 5
                    STEPS = HEADS * NT

                    def run(first, round_, last):
                        def loop(eng):
                            first()
                            round_(0, 0, False, True, True, True)
                            with eng.Fori(0, GRAPHS // 2 - 2) as i:
                                round_(2 * i + 1, 1, True, True, True, True)
                                round_(2 * i + 2, 0, True, True, True, True)
                            round_(GRAPHS - 3, 1, True, True, True, False)
                            round_(GRAPHS - 2, 0, True, True, False, False)
                            round_(GRAPHS - 1, 1, True, False, False, False)
                            last()
                        return loop

                    def ahead(s, value):
                        n = s + AHEAD
                        return (n, n // NT % HEADS, n % NT) if value or n < STEPS else None

                    @block.tensor
                    def _(pe):
                        def convolution(c, m):
                            if m == 0:
                                pe.wait_ge(p_norm, c + 1)
                                pe.wait_ge(at_rc, c + 1)
                            last = t.matmul(ps1[:], hn[:, m, :], LT[:, m, :], start=m == 0, stop=m == NT - 1)
                            if m == NT - 1:
                                last.then_inc(p_xp, 1)

                        def head_step(s, c):
                            if s < 4:
                                convolution(c, s)
                            if s == 4:
                                pe.wait_ge(p_xpc, c + 1)
                                to_node_major(ps1t, xpF[:], wsq("L3_Wc")).then_inc(p_wc, 1)
                            if s == 9:
                                pe.wait_ge(p_vc, c)
                                pe.wait_ge(p_x1, c + 1)
                                transposes(ps1t, [x1[:, i, :] for i in range(NT)]).then_inc(p_t, 1)
                            if s == 10:
                                pe.wait_ge(p_tc, c + 1)
                                t.matmul(ps1[:], wsq("L3_Wq"), x1F[:], start=True, stop=True).then_inc(p_q, 1)
                            if s == 12:
                                pe.wait_ge(p_ql, c + 1)
                                t.matmul(ps1[:], wsq("L3_Wk"), x1F[:], start=True, stop=True).then_inc(p_k, 1)

                        def value_step(c):
                            to_node_major(ps1t, x1F[:], wsq("L3_Wv")).then_inc(p_v, 1)

                        def tail_step(c):
                            pe.wait_ge(at_o, c + 2)
                            to_node_major(ps1t, oF[:], wsq("L3_Wo")).then_inc(q_wo, 1)

                        def scores(slot, h, j):
                            t.matmul(pss[:, j, :], QS[:, slot, h, j * P:(j + 1) * P], KS[:, slot, h, :], start=True, stop=True).then_inc(at_s, 1)

                        def weighted(b, slot, h, m):
                            pe.wait_ge(at_pa if m % 2 else at_pd, 2 * (HEADS * b + h) + m // 2 + 1)
                            if m == 0 and h == 0:
                                pe.wait_ge(at_o, b + 1)
                                pe.wait_ge(p_vc, b + 1)
                            last = t.matmul(pso[HD * h:HD * h + HD, :], vT[:, slot, m, HD * h:HD * h + HD], PT[:, m % 2, :],
                                            start=m == 0, stop=m == NT - 1)
                            if m == NT - 1 and h == HEADS - 1:
                                last.then_inc(at_pv, 1)

                        def round_(b, slot, tail, value, head, norm):
                            for s in range(STEPS):
                                h, j = s // NT, s % NT
                                u = HEADS * b + h
                                tile = ahead(s, value)
                                if tile:
                                    n, sh, sj = tile
                                    if n == STEPS:
                                        pe.wait_ge(stacked, STACK * (b + 3))
                                    pe.wait_ge(at_m, STEPS * b + n - NT + 1)
                                    scores(slot if n < STEPS else 1 - slot, sh, sj)
                                if j == 0:
                                    pe.wait_ge(at_e, NT * u + NT)
                                transposes(pst[:, j % 2, :].rearrange("p (t n) -> p t n", t=NT),
                                           [SM[:, h % 2, i, j * P:(j + 1) * P] for i in range(NT)]).then_inc(at_t, 1)
                                if s:
                                    weighted(b, slot, (s - 1) // NT, (s - 1) % NT)
                                elif tail:
                                    weighted(b - 1, 1 - slot, HEADS - 1, NT - 1)
                                if tail and s == 6:
                                    if head:
                                        pe.wait_ge(p_y, b + 3)
                                    tail_step(b - 1)
                                if value and s == 7:
                                    if tail:
                                        pe.wait_ge(q_z, b)
                                    else:
                                        pe.wait_ge(p_y, b + 3)
                                    value_step(b + 1)
                                if head:
                                    head_step(s, b + 2)
                                if s == 14:
                                    if head:
                                        pe.wait_ge(p_kl, b + 3)
                                    elif value:
                                        pe.wait_ge(p_vc, b + 2)
                                    pe.wait_ge(at_rb, b + 1)
                                    transposes(ps1t, [RB[:, i].rearrange("p h e -> p (h e)") for i in range(NT)]).then_inc(at_rt, 1)

                        def first():
                            for c in range(2):
                                for s in range(14):
                                    if s == 0 and c:
                                        pe.wait_ge(p_vc, 1)
                                    if s == 9 and c == 0:
                                        pe.wait_ge(p_x1, 1)
                                        transposes(ps1t, [x1[:, i, :] for i in range(NT)]).then_inc(p_t, 1)
                                    else:
                                        head_step(s, c)
                                if c == 0:
                                    pe.wait_ge(p_kl, 1)
                                    value_step(0)
                            pe.wait_ge(p_kl, 2)
                            pe.wait_ge(stacked, 2 * STACK)
                            for n in range(AHEAD):
                                if n >= NT:
                                    pe.wait_ge(at_m, n - NT + 1)
                                scores(0, n // NT, n % NT)

                        def last():
                            weighted(GRAPHS - 1, 1, HEADS - 1, NT - 1)
                            pe.wait_ge(at_rc, GRAPHS + 3)
                            tail_step(GRAPHS - 1)
                        run(first, round_, last)(pe)

                    @block.sync
                    def _(sp):
                        sp.sem_inc(stacked, STACK)

                        def stack(c, s):
                            for part, (made, dst, order) in enumerate(((p_ql, QS, (0, 0, 1, 1)), (p_kl, KS, (0, 1, 0, 1)))):
                                sp.wait_ge(made, c + 1)
                                if part == 0:
                                    sp.wait_ge(at_x, c + 1)
                                for h in range(HEADS):
                                    for r in range(4):
                                        sp.dma_start(dst[HD * r:HD * r + HD, s, h, :].bitcast(F32),
                                                     qk[HD * h:HD * h + HD, part, order[r], :].bitcast(F32)).then_inc(stacked, 16)
                        every(sp, stack)

                    @block.scalar
                    def _(act):
                        act.sem_inc(at_rc, 3)

                        def head_evacuation(s, c):
                            if s == 4:
                                act.wait_ge(p_xp, c + 1)
                                a.activation(xpF[:], ps1[:], ACT.Copy).then_inc(p_xpc, 1)
                            if s == 10:
                                act.wait_ge(p_t, c + 1)
                                a.activation(x1F[:], ps1[:], ACT.Copy).then_inc(p_tc, 1)
                            if s in (11, 13):
                                part = (s - 11) // 2
                                made, high = ((p_q, p_qh), (p_k, p_kh))[part]
                                act.wait_ge(made, c + 1)
                                act.wait_ge(stacked, STACK * c + STACK)
                                a.activation(qk[:, part, 0, :], ps1[:], ACT.Copy).then_inc(high, 1)

                        def keep(c):
                            a.activation(X2[:, bass.ds(4 * c, 4), :], x1[:], ACT.Copy).then_inc(p_keep, 1)

                        def value_evacuation(c, slot):
                            act.wait_ge(p_v, c + 1)
                            a.activation(vT[:, slot], ps1t, ACT.Copy).then_inc(p_vc, 1)

                        def exps(number, h, j):
                            act.wait_ge(at_m, number + 1)
                            a.activation(SM[:, h % 2, j, :], SM[:, h % 2, j, :], ACT.Exp, bias=MN[:, h % 2, j:j + 1], scale=-1.0,
                                         accum_out=SUM[:, h, j:j + 1]).then_inc(at_e, 1)

                        def normalize(c, i):
                            ins = a.activation(hn[:, i, :], X[:, 4 * c + i, :], ACT.Relu,
                                               bias=NBIAS[:, bass.ds(4 * c + i, 1)], scale=RSTD[:, bass.ds(4 * c + i, 1)])
                            if i == NT - 1:
                                ins.then_inc(p_norm, 1)

                        def round_(b, slot, tail, value, head, norm):
                            for s in range(STEPS):
                                j = s % NT
                                if value and s == 8:
                                    value_evacuation(b + 1, 1 - slot)
                                if head:
                                    head_evacuation(s, b + 2)
                                if s == 15:
                                    act.wait_ge(at_rt, b + 1)
                                    a.activation(RF[:], ps1[:], ACT.Copy).then_inc(at_rc, 1)
                                if j % 2:
                                    act.wait_ge(at_t, STEPS * b + s + 1)
                                    a.activation(PT[:, 1, :], pst[:, 1, :], ACT.Copy).then_inc(at_pa, 1)
                                tile = ahead(s, value)
                                if tile:
                                    n, sh, sj = tile
                                    if n == STEPS:
                                        act.wait_ge(at_r, b + 1)
                                        alone(act)
                                    exps(STEPS * b + n, sh, sj)
                                if head and s == 10:
                                    keep(b + 2)
                                if norm and s > 10 and s < 15:
                                    normalize(b + 3, s - 11)

                        def first():
                            for c in range(2):
                                for i in range(NT):
                                    normalize(c, i)
                                for s in range(15):
                                    head_evacuation(s, c)
                                    if s == 10:
                                        keep(c)
                                if c == 0:
                                    value_evacuation(0, 0)
                            for i in range(NT):
                                normalize(2, i)
                            for n in range(AHEAD):
                                exps(n, n // NT, n % NT)

                        run(first, round_, lambda: None)(act)

                    @block.vector
                    def _(dve):
                        dve.sem_inc(at_o, 1)
                        dve.sem_inc(at_x, 2)

                        def head_evacuation(s, c):
                            if s == 5:
                                dve.wait_ge(p_wc, c + 1)
                                v.tensor_tensor(Y[:], ps1t, row4("L3_bc"), ALU.add).then_inc(p_y, 1)

                        def head_step(s, c):
                            if s == 5:
                                dve.wait_ge(p_y, c + 1)
                                dve_row_stats(dve, ln1, c, 0, lambda i: Y[:, i, :])
                            if s == 6:
                                dve.wait_ge(ln1.moments, ln1.base + c + 1)
                                for i in range(NT):
                                    last = v.scalar_tensor_tensor(Y1[:, i, :], Y[:, i, :], MV[:, 0, i, 0:1], ROW[:, ROWS.index("L3_g1"), :],
                                                                  ALU.subtract, ALU.mult)
                                last.then_inc(p_mul, 1)
                            if s == 7:
                                dve.wait_ge(p_mul, c + 1)
                                dve.wait_ge(ln1.rstd, ln1.base + c + 1)
                                for i in range(NT):
                                    last = v.scalar_tensor_tensor(Y1[:, i, :], Y1[:, i, :], rstd1[:, i:i + 1], ROW[:, ROWS.index("L3_be1"), :],
                                                                  ALU.mult, ALU.add)
                                last.then_inc(p_add, 1)
                            if s == 8:
                                dve.wait_ge(p_add, c + 1)
                                dve.wait_ge(p_keep, c + 1)
                                v.scalar_tensor_tensor(x1[:], Y1[:], 0.0, hn[:], ALU.max, ALU.add).then_inc(p_x1, 1)
                            if s in (11, 13):
                                part = (s - 11) // 2
                                high, low = ((p_qh, p_ql), (p_kh, p_kl))[part]
                                dve.wait_ge(high, c + 1)
                                v.tensor_tensor(qk[:, part, 1, :], ps1[:], qk[:, part, 0, :].bitcast(F32), ALU.subtract).then_inc(low, 1)

                        def mask(number, h, j):
                            dve.wait_ge(at_s, number + 1)
                            alone(dve)
                            v.tensor_tensor_reduce(out=SM[:, h % 2, j, :], in0=pss[:, j, :], in1=NB[:, j, :], scale=NS[:, j:j + 1],
                                                   scalar=3e38, op0=ALU.add, op1=ALU.min,
                                                   accum_out=MN[:, h % 2, j:j + 1]).then_inc(at_m, 1)

                        def projection_evacuation(c):
                            dve.wait_ge(q_aff, c + 1)
                            dve.wait_ge(q_wo, c + 1)
                            v.tensor_tensor(Z[:], ps1t, row4("L3_bo"), ALU.add).then_inc(q_z, 1)

                        def output_stats(c):
                            dve.wait_ge(q_z, c + 1)
                            v.tensor_tensor(Z[:], Z[:], X2[:, bass.ds(4 * c, 4), :], ALU.add).then_inc(q_zz, 1)
                            dve.wait_ge(q_zz, c + 1)
                            dve_row_stats(dve, ln2, c, 1, lambda i: Z[:, i, :])

                        def output(c):
                            dve.wait_ge(at_pv, c + 1)
                            dve.wait_ge(at_rc, c + 4)
                            v.tensor_tensor(oF[:], pso[:], RF[:], ALU.mult).then_inc(at_o, 1)

                        def round_(b, slot, tail, value, head, norm):
                            for s in range(STEPS):
                                h, j = s // NT, s % NT
                                if tail and s == 7:
                                    projection_evacuation(b - 1)
                                if head:
                                    head_evacuation(s, b + 2)
                                if j % 2 == 0:
                                    dve.wait_ge(at_t, STEPS * b + s + 1)
                                    v.tensor_copy(PT[:, 0, :], pst[:, 0, :]).then_inc(at_pd, 1)
                                if tail and s == 0:
                                    output(b - 1)
                                if s == 11:
                                    dve.wait_ge(at_e, STEPS * b + STEPS)
                                    v.reciprocal(RS[:], SUM[:]).then_inc(at_r, 1)
                                tile = ahead(s, value)
                                if tile:
                                    n, sh, sj = tile
                                    if sj == 0:
                                        dve.wait_ge(at_t, STEPS * b + s + 1)
                                    mask(STEPS * b + n, sh, sj)
                                if s + AHEAD == STEPS - 1:
                                    dve.sem_inc(at_x, 1)
                                if s == 12:
                                    dve.wait_ge(at_r, b + 1)
                                    for i in range(NT):
                                        last = v.tensor_copy(RB[:, i], RS[:, :, i].unsqueeze(2).to_broadcast([P, HEADS, HD]))
                                    last.then_inc(at_rb, 1)
                                if tail and s == 7:
                                    output_stats(b - 1)
                                if head:
                                    head_step(s, b + 2)

                        def first():
                            dve.sem_inc(p_keep, 1)
                            for c in range(2):
                                for s in range(15):
                                    head_evacuation(s, c)
                                    head_step(s, c)
                            for n in range(AHEAD):
                                mask(n, n // NT, n % NT)

                        def last():
                            output(GRAPHS - 1)
                            projection_evacuation(GRAPHS - 1)
                            output_stats(GRAPHS - 1)
                        run(first, round_, last)(dve)

                    @block.gpsimd
                    def _(pool):
                        pool.sem_inc(ln2.free, 2)
                        pool.sem_inc(q_aff, 1)

                        def tail_rows(c):
                            pool.wait_ge(ln2.bias, c + 1)
                            alone(pool)
                            for i in range(NT):
                                last = g.tensor_scalar(Z1[:, i, :], Z[:, i, :], rstd2[:, i:i + 1], nb2[:, i:i + 1], ALU.mult, ALU.add)
                            last.then_inc(q_aff, 1)
                            pool.wait_ge(q_aff, c + 2)
                            alone(pool)
                            g.tensor_tensor(Z1[:], Z1[:], row4("L3_g2"), ALU.mult).then_inc(q_mul, 1)
                            pool.wait_ge(q_mul, c + 1)
                            alone(pool)
                            g.tensor_tensor(X2[:, bass.ds(4 * c, 4), :], Z1[:], row4("L3_be2"), ALU.add).then_inc(q_x2, 1)

                        def round_(b, slot, tail, value, head, norm):
                            if head:
                                pool_rstd(pool, ln1, b + 2, 0, rstd1[:], None)
                            if tail:
                                pool_rstd(pool, ln2, b - 1, 1, rstd2[:], nb2[:])
                                tail_rows(b - 1)

                        def first():
                            for c in range(2):
                                pool_rstd(pool, ln1, c, 0, rstd1[:], None)

                        def last():
                            pool_rstd(pool, ln2, GRAPHS - 1, 1, rstd2[:], nb2[:])
                            tail_rows(GRAPHS - 1)
                        run(first, round_, last)(pool)

                m_x, m_free, m_t, m_tc, m_w1, m_g, m_w2, m_z, m_zz, m_aff, m_mul, m_add, m_out = (
                    sem(f"s4_{n}") for n in ("x", "free", "t", "tc", "w1", "g", "w2", "z", "zz", "aff", "mul", "add", "out"))
                m_st = [sem(f"s4_st{n}") for n in range(2)]
                ln.next()
                with ExitStack() as qctx, nc.Block() as block:
                    def qsb(name, shape):
                        return qctx.enter_context(nc.sbuf_tensor("s4_" + name, shape, F32))

                    xs = qsb("xs", [P, 4, NT, D])
                    xF = qsb("xF", [P, 2, NODES])
                    gF = qsb("gF", [P, 2, 2, NODES])
                    Z = qsb("Z", [P, 2, NT, D])
                    Z1 = qsb("Z1", [P, 2, NT, D])
                    O = qsb("O", [P, 2, NT, D])
                    rs = qsb("rs", [P, 2, NT])
                    nb = qsb("nb", [P, 2, NT])
                    pst = qctx.enter_context(nc.psum_tensor("s4_pst", [P, 2, NT, P], F32))
                    psh = qctx.enter_context(nc.psum_tensor("s4_psh", [P, 2, 2, NODES], F32))
                    psw = qctx.enter_context(nc.psum_tensor("s4_psw", [P, 2, NT, D], F32))

                    @block.scalar
                    def _(act):
                        def fetch(b, k, slot):
                            a.activation(xs[:, slot], X2[:, bass.ds(4 * (b + k), 4), :], ACT.Copy).then_inc(m_x, 1)
                        for k in range(2):
                            fetch(0, k, k)

                        def body(b, slot, more):
                            for k in range(2):
                                act.wait_ge(m_t, b + k + 1)
                                a.activation(xF[:, k, :], pst[:, k].rearrange("p t d -> p (t d)"), ACT.Copy).then_inc(m_tc, 1)
                            for k in range(2):
                                act.wait_ge(m_w1, b + k + 1)
                                for h in range(2):
                                    last = a.activation(gF[:, k, h, :], psh[:, k, h, :], ACT.Gelu, bias=col("L3_b1", h))
                                last.then_inc(m_g, 1)
                            if more:
                                for k in range(2):
                                    act.wait_ge(m_free, b + k + 3)
                                    alone(act)
                                    fetch(b + 2, k, (slot + 2 + k) % 4)
                            for k in range(2):
                                act.wait_ge(ln.bias, ln.base + b + k + 1)
                                for i in range(NT):
                                    last = a.activation(Z1[:, k, i, :], Z[:, k, i, :], ACT.Identity, bias=nb[:, k, i:i + 1], scale=rs[:, k, i:i + 1])
                                last.then_inc(m_aff, 1)
                        pairs(act, body)

                    @block.tensor
                    def _(pe):
                        def body(b, slot, more):
                            for k in range(2):
                                pe.wait_ge(m_x, b + k + 1)
                                transposes(pst[:, k], [xs[:, slot + k, i, :] for i in range(NT)]).then_inc(m_t, 1)
                            for k in range(2):
                                pe.wait_ge(m_tc, b + k + 1)
                                for h in range(2):
                                    last = t.matmul(psh[:, k, h, :], W3A[:, h * P:(h + 1) * P], xF[:, k, :], start=True, stop=True)
                                last.then_inc(m_w1, 1)
                            for k in range(2):
                                pe.wait_ge(m_g, b + k + 1)
                                pe.wait_ge(m_z, b + k + 1)
                                for i in range(NT):
                                    for h in range(2):
                                        last = t.matmul(psw[:, k, i, :], gF[:, k, h, i * P:(i + 1) * P], W3B[:, h, :], start=h == 0, stop=h == 1)
                                last.then_inc(m_w2, 1)
                        pairs(pe, body)

                    @block.vector
                    def _(dve):
                        dve.sem_inc(m_z, 2)
                        dve.sem_inc(m_free, 4)

                        def body(b, slot, more):
                            for k in range(2):
                                dve.wait_ge(m_w2, b + k + 1)
                                v.tensor_tensor(Z[:, k], psw[:, k], row4("L3_b2"), ALU.add).then_inc(m_z, 1)
                                dve.wait_ge(m_z, b + k + 3)
                                v.tensor_tensor(Z[:, k], Z[:, k], xs[:, slot + k], ALU.add).then_inc(m_free, 1)
                                dve.wait_ge(m_free, b + k + 5)
                                dve_row_stats(dve, ln, b + k, k, lambda i: Z[:, k, i, :])
                            for k in range(2):
                                dve.wait_ge(m_aff, b + k + 1)
                                v.tensor_tensor(Z1[:, k], Z1[:, k], row4("L3_g3"), ALU.mult).then_inc(m_mul, 1)
                                dve.wait_ge(m_mul, b + k + 1)
                                v.tensor_tensor(Z1[:, k], Z1[:, k], row4("L3_be3"), ALU.add).then_inc(m_add, 1)
                                dve.wait_ge(m_add, b + k + 1)
                                dve.wait_ge(m_st[k], 8 * b + 16)
                                v.tensor_tensor(O[:, k], Z1[:, k], X[:, bass.ds(4 * (b + k), 4), :], ALU.add).then_inc(m_out, 1)
                        pairs(dve, body)

                    @block.gpsimd
                    def _(pool):
                        every(pool, lambda b, slot: pool_rstd(pool, ln, b, slot, rs[:, slot, :], nb[:, slot, :]))

                    @block.sync
                    def _(sp):
                        for slot in range(2):
                            sp.sem_inc(m_st[slot], 16)
                        o_view = out.rearrange("b (t p) d -> b p t d", p=P)

                        def body(b, slot):
                            sp.wait_ge(m_out, b + 1)
                            sp.dma_start(o_view[bass.ds(b, 1), :, :, :].rearrange("b p t d -> p (b t) d"), O[:, slot]).then_inc(m_st[slot], 16)
                        every(sp, body)
                        for slot in range(2):
                            sp.wait_ge(m_st[slot], 8 * GRAPHS + 16)
        if LAST_STAGE < 3:
            stored = sem("stored")
            with nc.Block() as block:
                @block.sync
                def _(sp):
                    o_view = out.rearrange("b (t p) d -> p (b t) d", p=P)
                    for q in range(4):
                        sp.dma_start(o_view[:, 16 * q:16 * q + 16, :], X[:, 16 * q:16 * q + 16, :]).then_inc(stored, 16)
                    sp.wait_ge(stored, 64)


_INS = ['x', 'adj', 'L0_gnn_W1', 'L0_gnn_b1', 'L0_gnn_g1', 'L0_gnn_be1', 'L0_gnn_W2', 'L0_gnn_b2', 'L0_gnn_g2',
        'L0_gnn_be2', 'L1_gnn_Wg0', 'L1_gnn_bg0', 'L1_gnn_Wg1', 'L1_gnn_bg1', 'L1_gnn_Wih', 'L1_gnn_Whh',
        'L1_gnn_bih', 'L1_gnn_bhh', 'L2_gnn_w1_loop', 'L2_gnn_w1_neigh', 'L2_gnn_b1', 'L2_gnn_w2_loop',
        'L2_gnn_w2_neigh', 'L2_gnn_b2', 'L3_gnn_Wc', 'L3_gnn_bc', 'L3_gnn_g1', 'L3_gnn_be1', 'L3_gnn_Wq',
        'L3_gnn_Wk', 'L3_gnn_Wv', 'L3_gnn_Wo', 'L3_gnn_bo', 'L3_gnn_g2', 'L3_gnn_be2', 'L3_gnn_W1', 'L3_gnn_b1',
        'L3_gnn_W2', 'L3_gnn_b2', 'L3_gnn_g3', 'L3_gnn_be3']


def kernel(**inputs):
    import numpy as _np
    import concourse.bacc as _bacc
    from concourse import mybir as _mybir
    from concourse.bass_utils import run_bass_kernel_spmd as _run

    nc = _bacc.Bacc("TRN2", target_bir_lowering=False, num_devices=1)
    arrays, handles = {}, {}
    for name in _INS:
        a = _np.ascontiguousarray(inputs[name])
        arrays[f"in_{name}_dram"] = a
        handles[name.replace("_gnn", "")] = nc.dram_tensor(f"in_{name}_dram", a.shape, _mybir.dt.from_np(a.dtype),
                                                           kind="ExternalInput").ap()
    out = nc.dram_tensor("out_0_dram", (GRAPHS, NODES, D), _mybir.dt.float32, kind="ExternalOutput").ap()
    build(nc, handles, out)
    r = _run(nc, [arrays], core_ids=[0])
    return r.results[0]["out_0_dram"]
```

```python
import concourse.bass as bass
from concourse import mybir
from contextlib import ExitStack


P = 128
F32 = mybir.dt.float32
F32R = mybir.dt.float32r
ALU = mybir.AluOpType
ACT = mybir.ActivationFunctionType
X_AXIS = mybir.AxisListType.X

GRAPHS, NODES, D = 16, 512, 128
NT = NODES // P
TILES = GRAPHS * NT
HID = 256
HEADS, HD = 4, 32
EPS = 1e-5
SCALE = 1.0 / (HD ** 0.5)
SQUARINGS = 12

COLS = {}
for _name, _n in (("L0_b1", 2), ("L0_g1", 2), ("L0_be1", 2), ("L0_b2", 1), ("L0_g2", 1), ("L0_be2", 1),
                  ("L1_bg1", 1), ("L2_b1", 1), ("L2_b2", 1), ("L3_b1", 2), ("L1_bih", 16), ("L1_bhh", 16)):
    COLS[_name] = (sum(n for _, n in COLS.values()), _n)
NCOLS = sum(n for _, n in COLS.values())
ROWS = ["L1_bg0", "L3_bc", "L3_g1", "L3_be1", "L3_bo", "L3_g2", "L3_be2", "L3_b2", "L3_g3", "L3_be3"]
SQUARE_WEIGHTS = ["L1_Wg0", "L1_Wg1", "L2_w1_loop", "L2_w1_neigh", "L2_w2_loop", "L2_w2_neigh",
                  "L3_Wc", "L3_Wq", "L3_Wk", "L3_Wv", "L3_Wo"]
SPLIT_WEIGHTS = ["L1_Wg1", "L2_w1_loop", "L2_w2_loop"]
T_W1, T_W2, T_WIH, T_WHH, T_BLOCKS = 0, 2, 4, 20, 36


def build(nc, d, out):
    with ExitStack() as ctx:
        def sb(name, shape, dt=F32):
            return ctx.enter_context(nc.sbuf_tensor(name, shape, dt))

        def sem(name):
            return ctx.enter_context(nc.semaphore(name))

        X = sb("X", [P, TILES, D])
        MV = sb("MV", [P, 2, NT, 2])
        RSTD = sb("RSTD", [P, TILES])
        NBIAS = sb("NBIAS", [P, TILES])
        ST = sb("ST", [P, 2, NT, 6])
        VE = sb("VE", [P, 2, NT])
        NMEAN = sb("NMEAN", [P, 2, NT])
        MHALF = sb("MHALF", [P, NT])
        ident = sb("ident", [P, P])
        ones = sb("ones", [P, P])
        COL = sb("COL", [P, NCOLS])
        ROW = sb("ROW", [P, len(ROWS), D])
        WSQ = sb("WSQ", [P, len(SQUARE_WEIGHTS), D])
        W3A = sb("W3A", [P, HID])
        W3B = sb("W3B", [P, 2, D])
        adjT = sb("adjT", [P, NT, NODES])
        LT = sb("LT", [P, NT, NODES])
        NB = sb("NB", [P, NT, NODES])
        NS = sb("NS", [P, NT])
        two_over = sb("two_over", [P, 1])
        AFF = sb("AFF", [P, 8])

        until2 = ctx.enter_context(ExitStack())
        adjH = until2.enter_context(nc.sbuf_tensor("adjH", [P, NT, NODES], F32R))
        adjL = until2.enter_context(nc.sbuf_tensor("adjL", [P, NT, NODES], F32R))
        WH = until2.enter_context(nc.sbuf_tensor("WH", [P, len(SPLIT_WEIGHTS), D], F32R))
        WL = until2.enter_context(nc.sbuf_tensor("WL", [P, len(SPLIT_WEIGHTS), D], F32R))

        early = ctx.enter_context(ExitStack())

        def early_sb(name, shape, dt=F32):
            return early.enter_context(nc.sbuf_tensor(name, shape, dt))

        WT = early_sb("WT", [P, T_BLOCKS, P])
        AhatT = early_sb("AhatT", [P, NT, NODES])
        BM0 = early_sb("BM0", [P, NT, D])
        BM1 = early_sb("BM1", [P, NODES])
        GB = early_sb("GB", [P, 16])

        def col(name, j=0):
            at = COLS[name][0] + j
            return COL[:, at:at + 1]

        def cols(name):
            return COL[:, COLS[name][0]:COLS[name][0] + COLS[name][1]]

        def row4(name):
            return ROW[:, ROWS.index(name), :].unsqueeze(1).to_broadcast([P, NT, D])

        def wsq(name):
            return WSQ[:, SQUARE_WEIGHTS.index(name), :]

        x_loaded, const_ok, passed = sem("x_loaded"), sem("const_ok"), sem("passed")
        v, a, g, t = nc.vector, nc.scalar, nc.gpsimd, nc.tensor

        class LayerNormSems:
            def __init__(self, tag):
                self.stats, self.moments, self.free, self.rstd, self.bias = (
                    sem(f"{tag}_{n}") for n in ("stats", "moments", "free", "rstd", "bias"))
                self.base = 0

            def next(self):
                self.base += GRAPHS

            def before(self):
                other = LayerNormSems.__new__(LayerNormSems)
                other.stats, other.moments, other.free, other.rstd, other.bias = (
                    self.stats, self.moments, self.free, self.rstd, self.bias)
                other.base = self.base - GRAPHS
                return other

        ln = LayerNormSems("ln")

        def alone(eng):
            eng.sem_inc(passed, 1)

        def dve_row_stats(eng, s, b, k, src):
            for i in range(NT):
                last = v.bn_stats(ST[:, k % 2, i, :], src(i))
            last.then_inc(s.stats, 1)
            eng.wait_ge(s.stats, s.base + b + 1)
            eng.wait_ge(s.free, s.base + b + 1)
            alone(eng)
            for i in range(NT):
                last = v.bn_aggr(MV[:, k % 2, i, :], ST[:, k % 2, i, :])
            last.then_inc(s.moments, 1)

        def pool_rstd(eng, s, b, k, rstd, nbias):
            eng.wait_ge(s.moments, s.base + b + 1)
            alone(eng)
            if nbias is not None:
                g.tensor_scalar(NMEAN[:, k % 2, :], MV[:, k % 2, :, 0], -1.0, 0.0, ALU.mult, ALU.add)
            g.tensor_scalar(VE[:, k % 2, :], MV[:, k % 2, :, 1], 1.0, EPS, ALU.mult, ALU.add).then_inc(s.free, 1)
            eng.wait_ge(s.free, s.base + b + 3)
            alone(eng)
            g.tensor_tensor(rstd, VE[:, k % 2, :], MHALF[:], ALU.pow).then_inc(s.rstd, 1)
            eng.wait_ge(s.rstd, s.base + b + 1)
            alone(eng)
            if nbias is None:
                eng.sem_inc(s.bias, 1)
            else:
                g.tensor_tensor(nbias, NMEAN[:, k % 2, :], rstd, ALU.mult).then_inc(s.bias, 1)

        def dve_x_stats(eng, s, b, k, written=None, ahead=3):
            eng.wait_ge(x_loaded, 16)
            if written is not None:
                eng.wait_ge(written, b + ahead)
                alone(eng)
            dve_row_stats(eng, s, b, k, lambda i: X[:, 4 * b + i, :])

        def pool_x_rstd(eng, s, b, k):
            pool_rstd(eng, s, b, k, RSTD[:, bass.ds(4 * b, 4)], NBIAS[:, bass.ds(4 * b, 4)])

        def act_norm_relu(b, dst):
            for i in range(NT):
                last = a.activation(dst[:, i, :], X[:, 4 * b + i, :], ACT.Relu,
                                    bias=NBIAS[:, bass.ds(4 * b + i, 1)], scale=RSTD[:, bass.ds(4 * b + i, 1)])
            return last

        def over_nodes(ps, node_major, matT, start=True, stop=True):
            for m in range(NT):
                last = t.matmul(ps, node_major[:, m, :], matT[:, m, :],
                                start=start and m == 0, stop=stop and m == NT - 1)
            return last

        def over_nodes_split(ps, high, low, mat_high, mat_low, stop=True):
            for m in range(NT):
                t.matmul(ps, low[:, m, :], mat_high[:, m, :], start=m == 0, stop=False)
                t.matmul(ps, high[:, m, :], mat_low[:, m, :], start=False, stop=False)
                last = t.matmul(ps, high[:, m, :], mat_high[:, m, :], start=False, stop=stop and m == NT - 1)
            return last

        def weights_split(ps, w_high, w_low, high, low, start=True):
            t.matmul(ps, w_low, high, start=start, stop=False)
            t.matmul(ps, w_high, low, start=False, stop=False)
            return t.matmul(ps, w_high, high, start=False, stop=True)

        def to_node_major(ps, feat, w, bias=None):
            for i in range(NT):
                last = t.matmul(ps[:, i, :], feat[:, bass.ts(i, P)], w, start=True, stop=bias is None)
                if bias is not None:
                    last = t.matmul(ps[:, i, :], ones[0:1, :], ROW[0:1, ROWS.index(bias), :], start=False, stop=True)
            return last

        def transposes(ps, blocks):
            for i, x in enumerate(blocks):
                last = t.transpose(ps[:, i, :], x, ident[:])
            return last

        def pairs(eng, body):
            with eng.Fori(0, GRAPHS // 4 - 1) as i:
                for slot in (0, 2):
                    body(4 * i + slot, slot, True)
            for slot in (0, 2):
                body(GRAPHS - 4 + slot, slot, slot == 0)

        PAIRS = GRAPHS // 2

        def there(n, count=PAIRS):
            return not isinstance(n, int) or 0 <= n < count

        def skewed(eng, before, after, body):
            for n in range(-after, before):
                body(n)
            with eng.Fori(before, PAIRS - after) as n:
                body(n)
            for n in range(PAIRS - after, PAIRS + before):
                body(n)

        def every(eng, body):
            with eng.Fori(0, GRAPHS // 2) as i:
                for slot in range(2):
                    body(2 * i + slot, slot)

        with ExitStack() as pctx:
            def psb(name, shape, dt=F32):
                return pctx.enter_context(nc.sbuf_tensor(name, shape, dt))

            adjN = psb("adjN", [P, NT, NODES])
            WR = psb("WR", [P, T_BLOCKS, P])
            VR = psb("VR", [NCOLS, P])
            S = psb("S", [P, NT, NODES])
            SH = psb("SH", [P, NT, NODES], F32R)
            SL = psb("SL", [P, NT, NODES], F32R)
            PA = psb("PA", [P, NT, NODES], F32R)
            PB = psb("PB", [P, NT, NODES], F32R)
            junk = psb("junk", [P, NT * NODES])
            tmp = psb("tmp", [P, NT, NODES])
            DG = psb("DG", [P, 2, NT, P])
            sm = psb("sm", [P, 64])
            c11 = psb("c11", [1, 4])
            ps4 = pctx.enter_context(nc.psum_tensor("ps4", [P, NT, NODES], F32))
            psx = pctx.enter_context(nc.psum_tensor("psx", [P, NODES], F32))
            psy = pctx.enter_context(nc.psum_tensor("psy", [P, NODES], F32))
            psb2 = pctx.enter_context(nc.psum_tensor("psb2", [P, 2, NODES], F32))
            rowsum, colsum, diag = sm[:, 0:4], sm[:, 4:8], sm[:, 8:12]
            deg, dinv, any_ = sm[:, 12:16], sm[:, 16:20], sm[:, 20:24]
            rabs, rmax, shift = sm[:, 24:28], sm[:, 28:29], sm[:, 29:30]
            sq, isq, num_den = sm[:, 30:31], sm[:, 31:32], sm[:, 32:34]
            lam, rshift = sm[:, 34:35], sm[:, 35:36]

            d_adj, d_w, d_v = sem("d_adj"), sem("d_w"), sem("d_v")
            ident0, ident_ok = sem("ident0"), sem("ident_ok")
            tr_done, tr_copied = sem("tr_done"), sem("tr_copied")
            dv, deg_ok, dinv_ok = sem("dv"), sem("deg_ok"), sem("dinv_ok")
            diag_ok, bcast_ok = sem("diag_ok"), sem("bcast_ok")
            rmax_ok, rmaxT_ok, c11_ok, shift_ok = sem("rmax_ok"), sem("rmaxT_ok"), sem("c11_ok"), sem("shift_ok")
            m_done, sq_sum, sq_bcast, isq_ok = sem("m_done"), sem("sq_sum"), sem("sq_bcast"), sem("isq_ok")
            m_act = sem("m_act")
            split_ok, sm_ok, nd_ok, nd_bcast = sem("split_ok"), sem("sm_ok"), sem("nd_ok"), sem("nd_bcast")
            lx = ln

            x_view = d["x"].rearrange("b (t p) d -> p (b t) d", p=P)
            N_W = 4 + len(SQUARE_WEIGHTS)
            N_V = len(COLS) + len(ROWS)

            with nc.Block() as block:
                @block.sync
                def _(sp):
                    sp.dma_start(adjN[:], d["adj"].rearrange("(t p) m -> p t m", p=P)).then_inc(d_adj, 16)
                    sp.dma_start(X[:], x_view).then_inc(x_loaded, 16)
                    for name in COLS:
                        at, w = COLS[name]
                        src = d[name]
                        src = src.rearrange("l (g p) -> (l g) p", p=P) if w == 16 else src.rearrange("(c p) -> c p", p=P)
                        sp.dma_start(VR[at:at + w, :], src).then_inc(d_v, 16)
                    for i, name in enumerate(ROWS):
                        sp.dma_start(ROW[:, i, :], d[name].partition_broadcast(P)).then_inc(d_v, 16)

                @block.scalar
                def _(act):
                    act.dma_start(WR[:, T_W1:T_W1 + 2, :], d["L0_W1"].rearrange("(h p) d -> p h d", p=P)).then_inc(d_w, 16)
                    act.dma_start(WR[:, T_W2:T_W2 + 2, :], d["L0_W2"].rearrange("o (h k) -> o h k", h=2)).then_inc(d_w, 16)
                    act.dma_start(WR[:, T_WIH:T_WIH + 16, :], d["L1_Wih"].rearrange("l (g p) d -> p (l g) d", p=P)).then_inc(d_w, 16)
                    act.dma_start(WR[:, T_WHH:T_WHH + 16, :], d["L1_Whh"].rearrange("l (g p) d -> p (l g) d", p=P)).then_inc(d_w, 16)
                    for i, name in enumerate(SQUARE_WEIGHTS):
                        act.dma_start(WSQ[:, i, :], d[name]).then_inc(d_w, 16)
                    act.dma_start(W3A[:], d["L3_W1"]).then_inc(d_v, 16)
                    act.dma_start(W3B[:], d["L3_W2"].rearrange("(h p) d -> p h d", p=P)).then_inc(d_v, 16)
                    def square(i, src, dst, k):
                        if k:
                            act.wait_ge(m_act, 2 * i + 1)
                            a.activation(junk[:], src[:].bitcast(F32).rearrange("p t n -> p (t n)"), ACT.Square,
                                         accum_out=sq).then_inc(sq_sum, 1)
                            act.wait_ge(isq_ok, i + 1)
                            alone(act)
                        for r in range(NT):
                            act.wait_ge(m_done, NT * (2 * i + k) + r + 1)
                            last = a.activation(dst[:, r, :], ps4[:, r, :], ACT.Copy, scale=isq if k else 1.0)
                        last.then_inc(m_act, 1)
                    square(0, PA, PB, 0)
                    square(0, PB, PA, 1)
                    for q in range(T_BLOCKS // 4):
                        act.wait_ge(tr_done, NT + q + 1)
                        a.activation(WT[:, 4 * q:4 * q + 4, :], (psx, psy)[q % 2][:].rearrange("p (t n) -> p t n", t=4),
                                     ACT.Copy).then_inc(tr_copied, 1)
                    act.wait_ge(tr_done, NT + T_BLOCKS // 4 + 1)
                    a.activation(COL[:], psy[:, 0:NCOLS], ACT.Copy).then_inc(tr_copied, 1)
                    with act.Fori(1, SQUARINGS // 2) as i:
                        square(i, PA, PB, 0)
                        square(i, PB, PA, 1)
                    act.wait_ge(m_act, SQUARINGS)
                    a.activation(junk[:], PA[:].bitcast(F32).rearrange("p t n -> p (t n)"), ACT.Square,
                                 accum_out=num_den[:, 1:2]).then_inc(nd_ok, 1)

                @block.gpsimd
                def _(pool):
                    g.memset(ident[:], 0.0).then_inc(ident0, 1)
                    g.memset(ones[:], 1.0).then_inc(const_ok, 1)
                    g.memset(MHALF[:], -0.5).then_inc(const_ok, 1)
                    pool.wait_ge(ident0, 1)
                    g.affine_select(out=ident[:], in_=ident[:], compare_op=ALU.not_equal, fill=1.0, base=0,
                                    pattern=[[-1, P]], channel_multiplier=1).then_inc(ident_ok, 1)
                    pool.wait_ge(const_ok, 2)
                    pool.wait_ge(deg_ok, 1)
                    g.tensor_tensor(dinv, deg, MHALF[:], ALU.pow).then_inc(dinv_ok, 1)
                    pool.sem_inc(ln.free, 2)
                    every(pool, lambda b, k: pool_x_rstd(pool, lx, b, k))

                @block.vector
                def _(dve):
                    n = [0]

                    def step(ins):
                        n[0] += 1
                        ins.then_inc(dv, 1)
                        dve.wait_ge(dv, n[0])

                    for m in range(NT):
                        dve.wait_ge(tr_done, m + 1)
                        step(v.tensor_copy(adjT[:, m, :], ps4[:, m, :]))
                    v.reduce_sum(rowsum, adjN[:], X_AXIS)
                    v.reduce_sum(colsum, adjT[:], X_AXIS)
                    for m in range(NT):
                        last = v.tensor_tensor(junk[:, m * P:(m + 1) * P], adjN[:, m, m * P:(m + 1) * P], ident[:], ALU.mult)
                    step(last)
                    step(v.reduce_sum(diag, junk[:, 0:NODES].rearrange("p (t n) -> p t n", t=NT), X_AXIS))
                    step(v.tensor_tensor(deg, rowsum, colsum, ALU.add))
                    step(v.tensor_tensor(deg, deg, diag, ALU.subtract))
                    v.tensor_scalar_add(deg, deg, 1.0).then_inc(deg_ok, 1)
                    step(v.tensor_tensor(S[:], adjN[:], adjT[:], ALU.add))
                    step(v.tensor_reduce(rabs, S[:], X_AXIS, ALU.add, apply_absolute_value=True))
                    v.reduce_max(rmax, rabs, X_AXIS).then_inc(rmax_ok, 1)
                    dve.wait_ge(rmaxT_ok, 1)
                    v.reduce_max(c11[:, 0:1], psx[0:1, 0:P], X_AXIS).then_inc(c11_ok, 1)
                    dve.wait_ge(rmaxT_ok, 2)
                    step(v.tensor_scalar(shift, psx[:, P:P + 1], 1e-30, None, ALU.max))
                    step(v.reciprocal(rshift, shift))
                    step(v.tensor_scalar(PA[:], S[:], rshift, None, ALU.mult))
                    for m in range(NT):
                        blk = slice(m * P, (m + 1) * P)
                        last = v.scalar_tensor_tensor(PA[:, m, blk], S[:, m, blk], rshift, ident[:], ALU.mult, ALU.add)
                    last.then_inc(shift_ok, 2)

                    def isq_step(i):
                        dve.wait_ge(sq_bcast, i + 1)
                        v.reciprocal(isq, psy[:, 0:1]).then_inc(isq_ok, 1)

                    def x_stats(b0, n):
                        with dve.Fori(0, n // 2) as i:
                            for k in range(2):
                                dve_x_stats(dve, lx, 2 * i + (b0 + k), k)

                    dve.wait_ge(dinv_ok, 1)
                    for j, vec in enumerate((rowsum, dinv)):
                        for m in range(NT):
                            last = v.tensor_scalar(DG[:, j, m, :], ident[:], vec[:, m:m + 1], None, ALU.mult)
                    last.then_inc(diag_ok, 1)
                    step(v.tensor_copy(tmp[:], adjT[:]))
                    for m in range(NT):
                        blk = slice(m * P, (m + 1) * P)
                        last = v.tensor_tensor(tmp[:, m, blk], tmp[:, m, blk], ident[:], ALU.add)
                    step(last)
                    isq_step(0)
                    dve.wait_ge(bcast_ok, 1)
                    for m in range(NT):
                        last = v.scalar_tensor_tensor(AhatT[:, m, :], tmp[:, m, :], dinv[:, m:m + 1], psb2[:, 1, :], ALU.mult, ALU.mult)
                    step(last)
                    dve.wait_ge(d_v, 16 * (N_V + 2))
                    dve.wait_ge(tr_copied, T_BLOCKS // 4 + 1)
                    v.tensor_scalar(BM1[:], psb2[:, 0, :], col("L1_bg1"), None, ALU.mult)
                    for m in range(NT):
                        v.tensor_scalar(BM0[:, m, :], ROW[:, ROWS.index("L1_bg0"), :], rowsum[:, m:m + 1], None, ALU.mult)
                    v.tensor_tensor(GB[:], cols("L1_bih"), cols("L1_bhh"), ALU.add)
                    isq_step(1)
                    step(v.tensor_scalar(tmp[:], adjN[:], 0.0, None, ALU.is_gt))
                    step(v.reduce_max(any_, tmp[:], X_AXIS))
                    isq_step(2)
                    step(v.tensor_scalar(tmp[:], tmp[:], 1.0, 1e9, ALU.subtract, ALU.mult))
                    for m in range(NT):
                        v.tensor_scalar(NB[:, m, :], tmp[:, m, :], any_[:, m:m + 1], None, ALU.mult)
                    v.tensor_scalar(NS[:], any_, -SCALE, None, ALU.mult)
                    isq_step(3)
                    step(v.tensor_copy(SH[:], S[:]))
                    v.tensor_tensor(SL[:], S[:], SH[:].bitcast(F32), ALU.subtract).then_inc(split_ok, 1)
                    x_stats(0, 2)
                    isq_step(4)
                    x_stats(2, 8)
                    isq_step(5)
                    x_stats(10, 6)
                    dve.wait_ge(sm_ok, 1)
                    v.scalar_tensor_tensor(tmp[:], ps4[:], 1.0, PA[:].bitcast(F32), ALU.mult, ALU.mult,
                                           accum_out=num_den[:, 0:1]).then_inc(nd_ok, 1)
                    dve.wait_ge(nd_bcast, 1)
                    step(v.reciprocal(lam, psy[:, 5:6]))
                    step(v.tensor_tensor(lam, lam, psy[:, 4:5], ALU.mult))
                    step(v.tensor_scalar(lam, lam, 0.5, 1e-8, ALU.mult, ALU.add))
                    step(v.reciprocal(two_over[:], lam))
                    v.tensor_scalar(two_over[:], two_over[:], 2.0, None, ALU.mult)

                @block.tensor
                def _(pe):
                    pe.wait_ge(ident_ok, 1)
                    pe.wait_ge(d_adj, 16)
                    for m in range(NT):
                        transposes(ps4[:, m, :].rearrange("p (t n) -> p t n", t=NT),
                                   [adjN[:, i, m * P:(m + 1) * P] for i in range(NT)]).then_inc(tr_done, 1)
                    pe.wait_ge(rmax_ok, 1)
                    t.transpose(psx[0:1, 0:P], rmax, ident[:]).then_inc(rmaxT_ok, 1)
                    pe.wait_ge(const_ok, 2)
                    pe.wait_ge(c11_ok, 1)
                    t.matmul(psx[:, P:P + 1], ones[0:1, :], c11[:, 0:1], start=True, stop=True).then_inc(rmaxT_ok, 1)
                    pe.wait_ge(shift_ok, 2)

                    def square(i, src, k):
                        for r in range(NT):
                            for m in range(NT):
                                last = t.matmul(ps4[:, r, :], src[:, m, r * P:(r + 1) * P], src[:, m, :],
                                                start=m == 0, stop=m == NT - 1)
                            last.then_inc(m_done, 1)
                            if k and r == NT - 2:
                                pe.wait_ge(sq_sum, i + 1)
                                t.matmul(psy[:, 0:1], ones[:], sq, start=True, stop=True).then_inc(sq_bcast, 1)
                        pe.wait_ge(m_act, 2 * i + k + 1)
                        alone(pe)
                    square(0, PA, 0)
                    square(0, PB, 1)
                    pe.wait_ge(diag_ok, 1)
                    for j in range(2):
                        for m in range(NT):
                            last = t.matmul(psb2[:, j, m * P:(m + 1) * P], ones[:], DG[:, j, m, :], start=True, stop=True)
                    last.then_inc(bcast_ok, 1)
                    pe.wait_ge(isq_ok, 1)
                    pe.wait_ge(d_w, 16 * N_W)
                    for q in range(T_BLOCKS // 4):
                        if q >= 2:
                            pe.wait_ge(tr_copied, q - 1)
                        transposes((psx, psy)[q % 2][:].rearrange("p (t n) -> p t n", t=4),
                                   [WR[:, 4 * q + i, :] for i in range(4)]).then_inc(tr_done, 1)
                    pe.wait_ge(tr_copied, T_BLOCKS // 4)
                    pe.wait_ge(d_v, 16 * (N_V + 2))
                    t.transpose(psy[:, 0:NCOLS], VR[:], ident[0:NCOLS, 0:NCOLS]).then_inc(tr_done, 1)
                    pe.wait_ge(tr_copied, T_BLOCKS // 4 + 1)
                    with pe.Fori(1, SQUARINGS // 2) as i:
                        square(i, PA, 0)
                        square(i, PB, 1)
                    pe.wait_ge(split_ok, 1)
                    for r in range(NT):
                        for part in (SL, SH):
                            for m in range(NT):
                                last = t.matmul(ps4[:, r, :], part[:, m, r * P:(r + 1) * P], PA[:, m, :],
                                                start=part is SL and m == 0, stop=part is SH and m == NT - 1)
                    last.then_inc(sm_ok, 1)
                    pe.wait_ge(nd_ok, 2)
                    t.matmul(psy[:, 4:6], ones[:], num_den, start=True, stop=True).then_inc(nd_bcast, 1)

        with ExitStack() as pctx:
            def psb(name, shape, dt=F32):
                return pctx.enter_context(nc.sbuf_tensor(name, shape, dt))

            H1 = psb("H1", [P, 2, GRAPHS, NODES])
            hn = psb("hn", [P, 4, NT, D])
            agg = psb("agg", [P, 2, NODES])
            hr = psb("hr", [P, 2, 2, NODES])
            bst = psb("bst", [P, 3, GRAPHS, 6])
            bmv = psb("bmv", [P, 3, 2])
            bve = psb("bve", [P, 3])
            Y = H1[:, 0]
            a_norm, a_agg, a_aggc, a_h, a_hc, a_st = (sem(f"s0_{n}") for n in ("norm", "agg", "aggc", "h", "hc", "st"))
            bn_mv, bn_ve, bn_rs, bn_sc, bn_d = (sem(f"s0_{n}") for n in ("bnmv", "bnve", "bnrs", "bnsc", "bnd"))
            b_hr, b_y, b_yc, b_st = (sem(f"s0_{n}") for n in ("hr", "y", "yc", "yst"))
            c_aff, c_t, c_x = (sem(f"s0_{n}") for n in ("aff", "t", "x"))
            ln.next()

            def dve_moments(dve, js, n):
                for j in js:
                    last = v.bn_aggr(bmv[:, j, :], bst[:, j, :, :])
                last.then_inc(bn_mv, 1)
                dve.wait_ge(bn_mv, n)
                v.tensor_scalar(bve[:, js[0]:js[-1] + 1], bmv[:, js[0]:js[-1] + 1, 1], EPS, None, ALU.add).then_inc(bn_ve, 1)

            def dve_affine(dve, js, n, scale, shift, gamma, beta):
                dve.wait_ge(bn_rs, n)
                v.tensor_tensor(scale, bve[:, js[0]:js[-1] + 1], gamma, ALU.mult).then_inc(bn_d, 1)
                dve.wait_ge(bn_d, 2 * n - 1)
                v.tensor_tensor(shift, bmv[:, js[0]:js[-1] + 1, 0], scale, ALU.mult).then_inc(bn_d, 1)
                dve.wait_ge(bn_d, 2 * n)
                v.tensor_tensor(shift, beta, shift, ALU.subtract).then_inc(bn_sc, 1)

            lt_ok = sem("lt_ok")

            with ExitStack() as qctx, nc.Block() as block:
                psg = qctx.enter_context(nc.psum_tensor("s0_psg", [P, 2, NODES], F32))
                psh = qctx.enter_context(nc.psum_tensor("s0_psh", [P, 2, 2, NODES], F32))

                @block.scalar
                def _(act):
                    for k in range(2):
                        act_norm_relu(k, hn[:, k]).then_inc(a_norm, 1)

                    def body(b, slot, more):
                        if more:
                            for k in range(2):
                                act_norm_relu(b + 2 + k, hn[:, (slot + 2 + k) % 4]).then_inc(a_norm, 1)
                        for k in range(2):
                            act.wait_ge(a_agg, b + k + 1)
                            a.activation(agg[:, k, :], psg[:, k, :], ACT.Copy).then_inc(a_aggc, 1)
                    pairs(act, body)

                @block.tensor
                def _(pe):
                    def body(b, slot, more):
                        for k in range(2):
                            pe.wait_ge(a_norm, b + k + 1)
                            over_nodes(psg[:, k, :], hn[:, slot + k], AhatT).then_inc(a_agg, 1)
                        for k in range(2):
                            pe.wait_ge(a_aggc, b + k + 1)
                            pe.wait_ge(a_hc, b + k + 1)
                            for h in range(2):
                                last = t.matmul(psh[:, k, h, :], WT[:, T_W1 + h, :], agg[:, k, :], start=True, stop=True)
                            last.then_inc(a_h, 1)
                    pairs(pe, body)

                @block.gpsimd
                def _(pool):
                    g.tensor_scalar(LT[:], adjT[:], two_over[:], 0.0, ALU.mult, ALU.add).then_inc(lt_ok, 1)
                    pool.wait_ge(lt_ok, 1)
                    alone(pool)
                    for m in range(NT):
                        blk = slice(m * P, (m + 1) * P)
                        g.tensor_tensor(LT[:, m, blk], LT[:, m, blk], ident[:], ALU.subtract)
                    g.tensor_copy(adjH[:], adjT[:]).then_inc(lt_ok, 1)
                    for i, name in enumerate(SPLIT_WEIGHTS):
                        last = g.tensor_copy(WH[:, i, :], wsq(name))
                    last.then_inc(lt_ok, 1)
                    pool.wait_ge(lt_ok, 3)
                    alone(pool)
                    g.tensor_tensor(adjL[:], adjT[:], adjH[:].bitcast(F32), ALU.subtract)
                    for i, name in enumerate(SPLIT_WEIGHTS):
                        g.tensor_tensor(WL[:, i, :], wsq(name), WH[:, i, :].bitcast(F32), ALU.subtract)
                    pool.wait_ge(bn_ve, 1)
                    g.tensor_tensor(bve[:, 0:2], bve[:, 0:2], MHALF[:, 0:2], ALU.pow).then_inc(bn_rs, 1)

                @block.vector
                def _(dve):
                    dve.sem_inc(a_hc, 2)

                    def body(b, slot):
                        dve.wait_ge(a_h, b + 1)
                        for h in range(2):
                            last = v.tensor_scalar(H1[:, h, b, :], psh[:, slot, h, :], col("L0_b1", h), None, ALU.add)
                        last.then_inc(a_hc, 1)
                        dve.wait_ge(a_hc, b + 3)
                        for h in range(2):
                            last = v.bn_stats(bst[:, h, b, :], H1[:, h, b, :])
                        last.then_inc(a_st, 1)
                    every(dve, body)
                    dve.wait_ge(a_st, GRAPHS)
                    dve_moments(dve, (0, 1), 1)
                    dve_affine(dve, (0, 1), 1, AFF[:, 0:2], AFF[:, 2:4], cols("L0_g1"), cols("L0_be1"))

            with ExitStack() as qctx, nc.Block() as block:
                psy = qctx.enter_context(nc.psum_tensor("s0_psy", [P, 2, NODES], F32))

                @block.scalar
                def _(act):
                    def body(b, slot):
                        act.wait_ge(b_y, b + 1)
                        for h in range(2):
                            last = a.activation(hr[:, slot, h, :], H1[:, h, b, :], ACT.Relu,
                                                bias=AFF[:, 2 + h:3 + h], scale=AFF[:, h:h + 1])
                        last.then_inc(b_hr, 1)
                    every(act, body)

                @block.tensor
                def _(pe):
                    pe.sem_inc(b_y, 2)

                    def body(b, slot):
                        pe.wait_ge(b_hr, b + 1)
                        pe.wait_ge(b_yc, b + 1)
                        for h in range(2):
                            last = t.matmul(psy[:, slot, :], WT[:, T_W2 + h, :], hr[:, slot, h, :], start=h == 0, stop=h == 1)
                        last.then_inc(b_y, 1)
                    every(pe, body)

                @block.vector
                def _(dve):
                    dve.sem_inc(b_yc, 2)

                    def body(b, slot):
                        dve.wait_ge(b_y, b + 3)
                        v.tensor_scalar(Y[:, b, :], psy[:, slot, :], col("L0_b2"), None, ALU.add).then_inc(b_yc, 1)
                        dve.wait_ge(b_yc, b + 3)
                        v.bn_stats(bst[:, 2, b, :], Y[:, b, :]).then_inc(b_st, 1)
                    every(dve, body)
                    dve.wait_ge(b_st, GRAPHS)
                    dve_moments(dve, (2,), 2)
                    dve_affine(dve, (2,), 2, AFF[:, 4:5], AFF[:, 5:6], cols("L0_g2"), cols("L0_be2"))

                @block.gpsimd
                def _(pool):
                    pool.wait_ge(bn_ve, 2)
                    g.tensor_tensor(bve[:, 2:3], bve[:, 2:3], MHALF[:, 0:1], ALU.pow).then_inc(bn_rs, 1)

            with ExitStack() as qctx, nc.Block() as block:
                pst = qctx.enter_context(nc.psum_tensor("s0_pst", [P, 2, NT, P], F32))

                @block.scalar
                def _(act):
                    def body(b, slot):
                        act.wait_ge(c_t, b + 1)
                        a.activation(agg[:, slot, :], Y[:, b, :], ACT.Identity, bias=AFF[:, 5:6], scale=AFF[:, 4:5]).then_inc(c_aff, 1)
                    every(act, body)

                @block.tensor
                def _(pe):
                    pe.sem_inc(c_t, 2)

                    def body(b, slot):
                        pe.wait_ge(c_aff, b + 1)
                        pe.wait_ge(c_x, b + 1)
                        transposes(pst[:, slot], [agg[:, slot, i * P:(i + 1) * P] for i in range(NT)]).then_inc(c_t, 1)
                    every(pe, body)

                @block.vector
                def _(dve):
                    dve.sem_inc(c_x, 2)

                    def body(b, slot):
                        dve.wait_ge(c_t, b + 3)
                        xb = X[:, bass.ds(4 * b, 4), :]
                        v.tensor_tensor(xb, xb, pst[:, slot], ALU.add).then_inc(c_x, 1)
                    every(dve, body)

        with ExitStack() as pctx:
            def psb(name, shape, dt=F32):
                return pctx.enter_context(nc.sbuf_tensor(name, shape, dt))

            HF = psb("HF", [P, GRAPHS, NODES])
            g_norm, g_high, g_low, g_aggl, g_h1l = (sem(f"s1_{n}") for n in ("norm", "high", "low", "aggl", "h1l"))
            g_agg, g_aggc, g_w, g_add, g_relu = (
                [sem(f"s1_{n}{layer}") for layer in range(2)] for n in ("agg", "aggc", "w", "add", "relu"))

            with ExitStack() as qctx, nc.Block() as block:
                def qsb(name, shape, dt=F32):
                    return qctx.enter_context(nc.sbuf_tensor("s1_" + name, shape, dt))

                hn = qsb("hn", [P, 2, NT, D])
                hnH = qsb("hnH", [P, 2, NT, D], F32R)
                hnL = qsb("hnL", [P, 2, NT, D], F32R)
                agg = qsb("agg", [P, 2, NODES])
                aggH = qsb("aggH", [P, 2, NODES], F32R)
                aggL = qsb("aggL", [P, 2, NODES], F32R)
                pre = qsb("pre", [P, 2, 2, NODES])
                h1H = qsb("h1H", [P, 2, NODES], F32R)
                h1L = qsb("h1L", [P, 2, NODES], F32R)
                psa = [qctx.enter_context(nc.psum_tensor(f"s1_psa{n}", [P, 2, NODES], F32)) for n in range(2)]
                psw = [qctx.enter_context(nc.psum_tensor(f"s1_psw{n}", [P, 2, NODES], F32)) for n in range(2)]


                base = ln.base

                def tiles(ap):
                    return ap.rearrange("p (t d) -> p t d", t=NT)

                @block.scalar
                def _(act):
                    def normalize(n):
                        for k in range(2):
                            act.wait_ge(ln.bias, base + 2 * n + k + 1)
                            alone(act)
                            act_norm_relu(2 * n + k, hn[:, k]).then_inc(g_norm, 1)

                    def aggregate(n, layer, dst):
                        for k in range(2):
                            act.wait_ge(g_agg[layer], 2 * n + k + 1)
                            a.activation(dst[:, k, :], psa[layer][:, k, :], ACT.Copy).then_inc(g_aggc[layer], 1)

                    def body(n):
                        if there(n + 1):
                            aggregate(n + 1, 0, agg)
                        if there(n + 2):
                            normalize(n + 2)
                        if there(n):
                            aggregate(n, 1, aggH)
                        for layer, m in ((0, n + 1), (1, n)):
                            if there(m):
                                for k in range(2):
                                    act.wait_ge(g_add[layer], 2 * m + k + 1 + 2 * layer)
                                    dst = h1H[:, k] if layer == 0 else HF[:, bass.ds(2 * m + k, 1), :].rearrange("p b n -> p (b n)")
                                    a.activation(dst, pre[:, layer, k, :], ACT.Relu).then_inc(g_relu[layer], 1)
                    skewed(act, 0, 3, body)

                @block.tensor
                def _(pe):
                    def body(n):
                        if there(n):
                            for k in range(2):
                                pe.wait_ge(g_h1l, 2 * n + k + 1)
                                over_nodes_split(psa[1][:, k, :], tiles(h1H[:, k]), tiles(h1L[:, k]), adjH, adjL).then_inc(g_agg[1], 1)
                        if there(n + 1):
                            for k in range(2):
                                pe.wait_ge(g_aggc[0], 2 * n + k + 3)
                                to_node_major(tiles(psw[0][:, k, :]), agg[:, k, :], wsq("L1_Wg0")).then_inc(g_w[0], 1)
                        if there(n + 2):
                            for k in range(2):
                                pe.wait_ge(g_low, 2 * n + k + 5)
                                over_nodes_split(psa[0][:, k, :], hnH[:, k], hnL[:, k], adjH, adjL).then_inc(g_agg[0], 1)
                        if there(n):
                            for k in range(2):
                                pe.wait_ge(g_aggl, 2 * n + k + 1)
                                pe.wait_ge(g_add[1], 2 * n + k + 1)
                                weights_split(psw[1][:, k, :], WH[:, 0, :], WL[:, 0, :], aggH[:, k, :], aggL[:, k, :]).then_inc(g_w[1], 1)
                    skewed(pe, 0, 3, body)

                @block.vector
                def _(dve):
                    dve.sem_inc(g_add[1], 2)

                    def body(n):
                        if there(n + 2):
                            for k in range(2):
                                dve.wait_ge(g_norm, 2 * n + k + 5)
                                v.tensor_copy(hnH[:, k], hn[:, k]).then_inc(g_high, 1)
                                dve.wait_ge(g_high, 2 * n + k + 5)
                                v.tensor_tensor(hnL[:, k], hn[:, k], hnH[:, k].bitcast(F32), ALU.subtract).then_inc(g_low, 1)
                        if there(n):
                            for k in range(2):
                                dve.wait_ge(g_aggc[1], 2 * n + k + 1)
                                v.tensor_tensor(aggL[:, k, :], psa[1][:, k, :], aggH[:, k, :].bitcast(F32), ALU.subtract).then_inc(g_aggl, 1)
                        if there(n + 1):
                            for k in range(2):
                                dve.wait_ge(g_w[0], 2 * n + k + 3)
                                v.tensor_tensor(tiles(pre[:, 0, k, :]), tiles(psw[0][:, k, :]), BM0[:], ALU.add).then_inc(g_add[0], 1)
                            for k in range(2):
                                dve.wait_ge(g_relu[0], 2 * n + k + 3)
                                v.scalar_tensor_tensor(h1L[:, k], pre[:, 0, k, :], 0.0, h1H[:, k].bitcast(F32),
                                                       ALU.max, ALU.subtract).then_inc(g_h1l, 1)
                        if there(n):
                            for k in range(2):
                                dve.wait_ge(g_w[1], 2 * n + k + 1)
                                v.tensor_tensor(pre[:, 1, k, :], psw[1][:, k, :], BM1[:], ALU.add).then_inc(g_add[1], 1)
                        if there(n + 3):
                            for k in range(2):
                                dve_x_stats(dve, ln, 2 * n + (6 + k), k)
                    skewed(dve, 0, 3, body)

                @block.gpsimd
                def _(pool):
                    every(pool, lambda b, slot: pool_x_rstd(pool, ln, b, slot))

            cells = []
            for p in range(1, 5):
                chunk_graphs = {1: 1, 2: 2, 3: 2, 4: 4}[p]
                chunks = 4 // chunk_graphs
                if p == 1:
                    cells += [(1, c, c, 1, 0, None) for c in range(4)]
                    continue
                base = len(cells)
                for step_t in range(p):
                    for c in range(chunks):
                        need = {2: 1 + 2 * c, 3: base - 2 + c, 4: base - 1}[p]
                        cells.append((p, c, c * chunk_graphs, chunk_graphs, step_t, need))
            NCELL = len(cells)
            GATES = [(0, 2, 3) if c[4] == 0 else (0, 2, 1, 3) for c in cells]
            gate_no = []
            for gs in GATES:
                gate_no.append({x: sum(map(len, gate_no)) + j + 1 for j, x in enumerate(gs)})
            GATES_GROUP = sum(map(len, GATES))

            def bank_reader(n, gate):
                m = n - 2
                while True:
                    if gate in gate_no[m % NCELL]:
                        return gate_no[m % NCELL][gate] + (0 if m >= 0 else -GATES_GROUP)
                    m -= 2

            l_gate, l_act, l_prod, l_c, l_tc, l_h, l_t, l_x = (
                sem(f"s1_{n}") for n in ("gate", "act", "prod", "c", "tc", "hid", "tr", "xadd"))
            ln.next()

            with ExitStack() as qctx, nc.Block() as block:
                LG = qctx.enter_context(nc.sbuf_tensor("LG", [P, 2, 4, NODES], F32))
                GA = qctx.enter_context(nc.sbuf_tensor("GA", [P, 2, 4, NODES], F32))
                CC = qctx.enter_context(nc.sbuf_tensor("CC", [P, 2, NODES], F32))
                HB = qctx.enter_context(nc.sbuf_tensor("HB", [P, 2, NODES], F32))
                IG = qctx.enter_context(nc.sbuf_tensor("IG", [P, NODES], F32))
                FC = qctx.enter_context(nc.sbuf_tensor("FC", [P, NODES], F32))
                TC = qctx.enter_context(nc.sbuf_tensor("TC", [P, 2, NODES], F32))
                psl = qctx.enter_context(nc.psum_tensor("psl", [P, 2, 4, NODES], F32))

                def windows(p, tensor, b0, nb, step_t):
                    nw = NODES // p
                    return tensor[:, b0:b0 + nb, step_t:(nw - 1) * p + step_t + 1:p]

                def flat(p, ap, nb):
                    nw = NODES // p
                    return ap[:, 0:nb * nw].rearrange("q (b j) -> q b j", b=nb)

                BACK = 4

                def groups(eng, body, last):
                    body(0, 0, False)
                    with eng.Fori(0, GRAPHS // 8 - 1) as i:
                        body(2 * i + 1, 1, True)
                        body(2 * i + 2, 0, True)
                    body(GRAPHS // 4 - 1, 1, True)
                    last(GRAPHS // 4 - 1, 1)

                def before(n):
                    return max(m for m in range(n) if cells[m][0:2] == cells[n][0:2])

                @block.tensor
                def _(pe):
                    def x_part(q, par, n, back):
                        p, c, b0, nb, step_t, need = cells[n]
                        if need is not None:
                            pe.wait_ge(l_h, NCELL * q + need + 1)
                        for gate in GATES[n]:
                            pe.wait_ge(l_act, GATES_GROUP * (q + 1) + bank_reader(n, gate))
                            if back and n == BACK:
                                pe.wait_ge(l_x, 4 * q + gate + 1)
                                alone(pe)
                            src = HF[:, bass.ds(4 * q + b0, 1), :] if p == 1 else windows(p, LG[:, par], b0, nb, step_t)
                            last = t.matmul(flat(p, psl[:, n % 2, gate, :], nb), WT[:, T_WIH + 4 * (p - 1) + gate, :], src,
                                            start=True, stop=step_t == 0)
                            if step_t == 0:
                                last.then_inc(l_gate, 1)

                    def give_back(q, par):
                        pe.wait_ge(l_h, NCELL * q + NCELL)
                        for b in range(4):
                            transposes(psl[:, 0, b, :].rearrange("p (t d) -> p t d", t=NT),
                                       [LG[:, par, b, i * P:(i + 1) * P] for i in range(NT)]).then_inc(l_t, 1)

                    def h_part(q, n):
                        p, c, b0, nb, step_t, need = cells[n]
                        pe.wait_ge(l_h, NCELL * q + before(n) + 1)
                        for gate in GATES[n]:
                            t.matmul(flat(p, psl[:, n % 2, gate, :], nb), WT[:, T_WHH + 4 * (p - 1) + gate, :],
                                     flat(p, HB[:, c, :], nb), start=False, stop=True).then_inc(l_gate, 1)

                    def body(q, par, back):
                        ahead = False
                        for n in range(NCELL):
                            if back and n == BACK:
                                pe.wait_ge(l_act, GATES_GROUP * (q + 1) + gate_no[BACK - 2][3])
                                alone(pe)
                                give_back(q - 1, 1 - par)
                            if not ahead:
                                x_part(q, par, n, back)
                            ahead = False
                            if cells[n][4] > 0:
                                if n + 1 < NCELL and cells[n + 1][4] > 0 and cells[n + 1][5] < before(n):
                                    x_part(q, par, n + 1, back)
                                    ahead = True
                                h_part(q, n)
                    groups(pe, body, give_back)

                @block.scalar
                def _(act):
                    act.sem_inc(l_act, GATES_GROUP)

                    def body(q, par, back):
                        for n in range(NCELL):
                            p, c, b0, nb, step_t, need = cells[n]
                            w = nb * (NODES // p)
                            for gate in GATES[n]:
                                act.wait_ge(l_gate, GATES_GROUP * q + gate_no[n][gate])
                                a.activation(GA[:, n % 2, gate, 0:w], psl[:, n % 2, gate, 0:w],
                                             ACT.Tanh if gate == 2 else ACT.Sigmoid,
                                             bias=GB[:, 4 * (p - 1) + gate:4 * (p - 1) + gate + 1]).then_inc(l_act, 1)
                            act.wait_ge(l_c, NCELL * q + n + 1)
                            a.activation(TC[:, n % 2, 0:w], CC[:, (c if p > 1 else n) % 2, 0:w], ACT.Tanh).then_inc(l_tc, 1)
                    groups(act, body, lambda q, par: None)

                @block.vector
                def _(dve):
                    dve.sem_inc(l_x, 4)
                    PRODS = sum(c[4] > 0 for c in cells)

                    def give_back(q):
                        for b in range(4):
                            dve.wait_ge(l_t, 4 * q + b + 1)
                            xb = X[:, bass.ds(16 * q + 4 * b, 4), :]
                            v.tensor_tensor(xb, xb, psl[:, 0, b, :].rearrange("p (t d) -> p t d", t=NT), ALU.add).then_inc(l_x, 1)

                    def body(q, par, back):
                        prods = 0
                        for n in range(NCELL):
                            if back and n == BACK - 1:
                                give_back(q - 1)
                            p, c, b0, nb, step_t, need = cells[n]
                            w = nb * (NODES // p)
                            gates = GA[:, n % 2, :, 0:w]
                            cc = CC[:, (c if p > 1 else n) % 2, 0:w]
                            dve.wait_ge(l_act, GATES_GROUP * (q + 1) + gate_no[n][1 if step_t else 2])
                            if step_t == 0:
                                v.tensor_tensor(cc, gates[:, 0], gates[:, 2], ALU.mult).then_inc(l_c, 1)
                            else:
                                v.tensor_tensor(IG[:, 0:w], gates[:, 0], gates[:, 2], ALU.mult)
                                v.tensor_tensor(FC[:, 0:w], gates[:, 1], cc, ALU.mult).then_inc(l_prod, 1)
                                prods += 1
                                dve.wait_ge(l_prod, PRODS * q + prods)
                                v.tensor_tensor(cc, IG[:, 0:w], FC[:, 0:w], ALU.add).then_inc(l_c, 1)
                            dve.wait_ge(l_tc, NCELL * q + n + 1)
                            dst = windows(p, LG[:, par], b0, nb, step_t) if step_t == p - 1 else flat(p, HB[:, c, :], nb)
                            v.tensor_tensor(dst, flat(p, gates[:, 3], nb), flat(p, TC[:, n % 2, :], nb), ALU.mult).then_inc(l_h, 1)
                            if back and BACK < n < BACK + 5:
                                dve_x_stats(dve, ln, 4 * q + (n - BACK - 5), (n - BACK - 1) % 2, l_x, 5)

                    groups(dve, body, lambda q, par: give_back(q))

                @block.gpsimd
                def _(pool):
                    with pool.Fori(0, (GRAPHS - 4) // 2) as i:
                        for slot in range(2):
                            pool_x_rstd(pool, ln, 2 * i + slot, slot)

        early.close()
        f_norm, f_t, f_tc, f_hh, f_hl, f_f, f_fc, f_h1h, f_h1l, f_o, f_oc, f_ot, f_xh, f_x = (
            sem(f"s2_{n}") for n in ("norm", "t", "tc", "hh", "hl", "f", "fc", "h1h", "h1l", "o", "oc", "ot", "xh", "x"))
        f_z, f_zh, f_zl = ([sem(f"s2_{n}{layer}") for layer in range(2)] for n in ("z", "zh", "zl"))
        ln.next()
        ln_in = ln.before()
        with ExitStack() as qctx, nc.Block() as block:
            def qsb(name, shape, dt=F32):
                return qctx.enter_context(nc.sbuf_tensor("s2_" + name, shape, dt))

            hn = qsb("hn", [P, 2, NT, D])
            hF = qsb("hF", [P, 2, NODES])
            h1F = qsb("h1F", [P, 2, NODES])
            hFH = qsb("hFH", [P, 2, NODES], F32R)
            hFL = qsb("hFL", [P, 2, NODES], F32R)
            h1FH = qsb("h1FH", [P, 2, NODES], F32R)
            h1FL = qsb("h1FL", [P, 2, NODES], F32R)
            zH = qsb("zH", [P, 2, 2, NT, D], F32R)
            zL = qsb("zL", [P, 2, 2, NT, D], F32R)
            oF = qsb("oF", [P, 2, NODES])
            psa = qctx.enter_context(nc.psum_tensor("s2_psa", [P, 2, NODES], F32))
            psz = [qctx.enter_context(nc.psum_tensor(f"s2_psz{n}", [P, 2, NT, D], F32)) for n in range(2)]
            pst = qctx.enter_context(nc.psum_tensor("s2_pst", [P, 2, NT, D], F32))


            @block.scalar
            def _(act):
                def z_high(n, layer):
                    for k in range(2):
                        act.wait_ge(f_z[layer], 2 * n + k + 1)
                        a.activation(zH[:, layer, k], psz[layer][:, k], ACT.Copy).then_inc(f_zh[layer], 1)

                def body(n):
                    if there(n + 1):
                        for k in range(2):
                            if there(n):
                                act.wait_ge(f_hl, 2 * n + k + 1)
                            act.wait_ge(f_t, 2 * n + k + 3)
                            a.activation(hF[:, k, :], pst[:, k].rearrange("p t d -> p (t d)"), ACT.Copy).then_inc(f_tc, 1)
                    if there(n + 2):
                        for k in range(2):
                            if there(n + 1):
                                act.wait_ge(f_xh, 2 * n + k + 3)
                                alone(act)
                            act.wait_ge(ln.bias, ln_in.base + 2 * n + (5 + k))
                            alone(act)
                            act_norm_relu(2 * n + (4 + k), hn[:, k]).then_inc(f_norm, 1)
                    if there(n):
                        for k in range(2):
                            act.wait_ge(f_f, 2 * n + k + 1)
                            a.activation(h1F[:, k, :], psa[:, k, :], ACT.Relu, bias=col("L2_b1")).then_inc(f_fc, 1)
                    if there(n + 1):
                        z_high(n + 1, 0)
                    if there(n):
                        z_high(n, 1)
                        for k in range(2):
                            act.wait_ge(f_o, 2 * n + k + 1)
                            a.activation(oF[:, k, :], psa[:, k, :], ACT.Relu, bias=col("L2_b2")).then_inc(f_oc, 1)
                act.sem_inc(f_oc, 2)
                skewed(act, 1, 2, body)

            @block.tensor
            def _(pe):
                def convolution(n, layer, parts, high, low, done):
                    for k in range(2):
                        pe.wait_ge(f_zl[layer], 2 * n + k + 1)
                        if layer == 0:
                            pe.wait_ge(f_oc, 2 * n + k + 1)
                        over_nodes_split(psa[:, k, :], zH[:, layer, k], zL[:, layer, k], adjH, adjL, stop=False)
                        pe.wait_ge(parts, 2 * n + k + 1)
                        weights_split(psa[:, k, :], WH[:, 1 + layer, :], WL[:, 1 + layer, :], high[:, k, :], low[:, k, :],
                                      start=False).then_inc(done, 1)

                def body(n):
                    if there(n + 1):
                        for k in range(2):
                            pe.wait_ge(f_norm, 2 * n + k + 3)
                            if there(n - 2):
                                pe.wait_ge(f_x, 2 * n + k - 1)
                            transposes(pst[:, k], [hn[:, k, i, :] for i in range(NT)]).then_inc(f_t, 1)
                    if there(n):
                        convolution(n, 0, f_hl, hFH, hFL, f_f)
                    if there(n + 1):
                        for k in range(2):
                            pe.wait_ge(f_tc, 2 * n + k + 3)
                            to_node_major(psz[0][:, k], hF[:, k, :], wsq("L2_w1_neigh")).then_inc(f_z[0], 1)
                    if there(n):
                        for k in range(2):
                            pe.wait_ge(f_fc, 2 * n + k + 1)
                            to_node_major(psz[1][:, k], h1F[:, k, :], wsq("L2_w2_neigh")).then_inc(f_z[1], 1)
                    if there(n - 1):
                        for k in range(2):
                            pe.wait_ge(f_oc, 2 * n + k + 1)
                            if not there(n + 1):
                                pe.wait_ge(f_x, 2 * n + k - 1)
                            transposes(pst[:, k], [oF[:, k, i * P:(i + 1) * P] for i in range(NT)]).then_inc(f_ot, 1)
                    if there(n):
                        convolution(n, 1, f_h1l, h1FH, h1FL, f_o)
                skewed(pe, 1, 2, body)

            @block.vector
            def _(dve):
                dve.sem_inc(f_x, 2)

                def split(n, made, src, high_ok, high, low_ok, low):
                    for k in range(2):
                        dve.wait_ge(made, 2 * n + k + 1)
                        v.tensor_copy(high[:, k, :], src[:, k, :]).then_inc(high_ok, 1)
                    for k in range(2):
                        dve.wait_ge(high_ok, 2 * n + k + 1)
                        v.tensor_tensor(low[:, k, :], src[:, k, :], high[:, k, :].bitcast(F32), ALU.subtract).then_inc(low_ok, 1)

                def z_low(n, layer):
                    for k in range(2):
                        dve.wait_ge(f_zh[layer], 2 * n + k + 1)
                        v.tensor_tensor(zL[:, layer, k], psz[layer][:, k], zH[:, layer, k].bitcast(F32), ALU.subtract).then_inc(f_zl[layer], 1)

                for b in range(GRAPHS - 4, GRAPHS):
                    dve_row_stats(dve, ln_in, b, b, lambda i: X[:, 4 * b + i, :])

                def x_of(n, k):
                    return X[:, bass.ds(8 * n + 4 * k, 4), :]

                def body(n):
                    if there(n + 1):
                        for k in range(2):
                            dve.wait_ge(f_norm, 2 * n + k + 3)
                            alone(dve)
                            xb = x_of(n + 1, k)
                            v.scalar_tensor_tensor(xb, hn[:, k], 0.5, xb, ALU.mult, ALU.add).then_inc(f_xh, 1)
                        z_low(n + 1, 0)
                    if there(n):
                        z_low(n, 1)
                        split(n, f_fc, h1F, f_h1h, h1FH, f_h1l, h1FL)
                    if there(n - 1):
                        for k in range(2):
                            dve.wait_ge(f_ot, 2 * n + k - 1)
                            dve.wait_ge(f_xh, 2 * n + k - 1)
                            alone(dve)
                            xb = x_of(n - 1, k)
                            v.scalar_tensor_tensor(xb, pst[:, k], 0.5, xb, ALU.mult, ALU.add).then_inc(f_x, 1)
                        for k in range(2):
                            dve_x_stats(dve, ln, 2 * n + (k - 2), k, f_x)
                    if there(n + 1):
                        split(n + 1, f_tc, hF, f_hh, hFH, f_hl, hFL)
                skewed(dve, 1, 2, body)

            @block.gpsimd
            def _(pool):
                for b in range(GRAPHS - 4, GRAPHS):
                    pool_x_rstd(pool, ln_in, b, b)
                every(pool, lambda b, slot: pool_x_rstd(pool, ln, b, slot))

        until2.close()
        with ExitStack() as pctx:
            X2 = pctx.enter_context(nc.sbuf_tensor("X2", [P, TILES, D], F32))

            p_norm, p_xp, p_xpc, p_wc, p_y, p_mul, p_add, p_x1 = (
                sem(f"s3_{n}") for n in ("norm", "xp", "xpc", "wc", "y", "mul", "add", "x1"))
            p_t, p_tc, p_q, p_qh, p_ql, p_k, p_kh, p_kl, p_v, p_vc = (
                sem(f"s3_{n}") for n in ("t", "tc", "q", "qh", "ql", "k", "kh", "kl", "v", "vc"))
            stacked, p_keep, at_x = sem("s3_stacked"), sem("s3_keep"), sem("at_x")
            STACK = 2 * HEADS * 4 * 16
            at_s, at_m, at_e, at_t, at_pd, at_pa, at_pv, at_r, at_rb, at_rt, at_rc, at_o = (
                sem(f"at_{n}") for n in ("s", "m", "e", "t", "pd", "pa", "pv", "r", "rb", "rt", "rc", "o"))
            q_wo, q_z, q_aff, q_mul, q_x2 = (
                sem(f"s3q_{n}") for n in ("wo", "z", "aff", "mul", "x2"))
            ln.next()
            ln1, ln2 = ln, LayerNormSems("ln_out")

            with ExitStack() as qctx, nc.Block() as block:
                def qsb(name, shape, dt=F32):
                    return qctx.enter_context(nc.sbuf_tensor("s3_" + name, shape, dt))

                hn = qsb("hn", [P, NT, D])
                xpF = qsb("xpF", [P, NODES])
                Y = qsb("Y", [P, NT, D])
                Y1 = qsb("Y1", [P, NT, D])
                x1 = qsb("x1", [P, NT, D])
                x1F = qsb("x1F", [P, NODES])
                qk = qsb("qk", [P, 2, 2, NODES], F32R)
                QS = qsb("QS", [P, 2, HEADS, NODES], F32R)
                KS = qsb("KS", [P, 2, HEADS, NODES], F32R)
                vT = qsb("vT", [P, 2, NT, D])
                SM = qsb("SM", [P, 2, NT, NODES])
                MN = qsb("MN", [P, 2, NT])
                SUM = qsb("SUM", [P, HEADS, NT])
                RS = qsb("RS", [P, HEADS, NT])
                RB = qsb("RB", [P, NT, HEADS, HD])
                RF = qsb("RF", [P, NODES])
                PT = qsb("PT", [P, 2, NODES])
                oF = qsb("oF", [P, NODES])
                Z = qsb("Z", [P, NT, D])
                Z1 = qsb("Z1", [P, NT, D])
                rstd1 = qsb("rstd1", [P, NT])
                rstd2 = qsb("rstd2", [P, NT])
                nb2 = qsb("nb2", [P, NT])
                pss = qctx.enter_context(nc.psum_tensor("s3_pss", [P, NT, NODES], F32))
                pst = qctx.enter_context(nc.psum_tensor("s3_pst", [P, 2, NODES], F32))
                pso = qctx.enter_context(nc.psum_tensor("s3_pso", [P, NODES], F32))
                ps1 = qctx.enter_context(nc.psum_tensor("s3_ps1", [P, NODES], F32))
                ps1t = ps1[:].rearrange("p (t d) -> p t d", t=NT)

                AHEAD = 5
                STEPS = HEADS * NT
                DVE_COPIES = (0, 1, 2, 3, 4, 15)
                ACT_COPIES = tuple(s for s in range(STEPS) if s not in DVE_COPIES)

                def run(first, round_, last):
                    def loop(eng):
                        first()
                        round_(0, 0, False, True, True, True)
                        with eng.Fori(0, GRAPHS // 2 - 2) as i:
                            round_(2 * i + 1, 1, True, True, True, True)
                            round_(2 * i + 2, 0, True, True, True, True)
                        round_(GRAPHS - 3, 1, True, True, True, False)
                        round_(GRAPHS - 2, 0, True, True, False, False)
                        round_(GRAPHS - 1, 1, True, False, False, False)
                        last()
                    return loop

                def ahead(s, value):
                    n = s + AHEAD
                    return (n, n // NT % HEADS, n % NT) if value or n < STEPS else None

                @block.tensor
                def _(pe):
                    def convolution(c, m):
                        if m == 0:
                            pe.wait_ge(p_norm, c + 1)
                            pe.wait_ge(at_rc, c + 1)
                        last = t.matmul(ps1[:], hn[:, m, :], LT[:, m, :], start=m == 0, stop=m == NT - 1)
                        if m == NT - 1:
                            last.then_inc(p_xp, 1)

                    def head_step(s, c):
                        if s < 4:
                            convolution(c, s)
                        if s == 4:
                            pe.wait_ge(p_xpc, c + 1)
                            to_node_major(ps1t, xpF[:], wsq("L3_Wc"), "L3_bc").then_inc(p_wc, 1)
                        if s == 9:
                            pe.wait_ge(p_vc, c)
                            pe.wait_ge(p_x1, c + 1)
                            transposes(ps1t, [x1[:, i, :] for i in range(NT)]).then_inc(p_t, 1)
                        if s == 10:
                            pe.wait_ge(p_tc, c + 1)
                            t.matmul(ps1[:], wsq("L3_Wq"), x1F[:], start=True, stop=True).then_inc(p_q, 1)
                        if s == 12:
                            pe.wait_ge(p_ql, c + 1)
                            t.matmul(ps1[:], wsq("L3_Wk"), x1F[:], start=True, stop=True).then_inc(p_k, 1)

                    def value_step(c):
                        to_node_major(ps1t, x1F[:], wsq("L3_Wv")).then_inc(p_v, 1)

                    def tail_step(c):
                        pe.wait_ge(at_o, c + 2)
                        to_node_major(ps1t, oF[:], wsq("L3_Wo"), "L3_bo").then_inc(q_wo, 1)

                    def scores(slot, h, j):
                        t.matmul(pss[:, j, :], QS[:, slot, h, j * P:(j + 1) * P], KS[:, slot, h, :], start=True, stop=True).then_inc(at_s, 1)

                    def weighted(b, slot, h, m):
                        copied, steps = (at_pd, DVE_COPIES) if NT * h + m in DVE_COPIES else (at_pa, ACT_COPIES)
                        pe.wait_ge(copied, len(steps) * b + steps.index(NT * h + m) + 1)
                        if m == 0 and h == 0:
                            pe.wait_ge(at_o, b + 1)
                            pe.wait_ge(p_vc, b + 1)
                        last = t.matmul(pso[HD * h:HD * h + HD, :], vT[:, slot, m, HD * h:HD * h + HD], PT[:, m % 2, :],
                                        start=m == 0, stop=m == NT - 1)
                        if m == NT - 1 and h == HEADS - 1:
                            last.then_inc(at_pv, 1)

                    def round_(b, slot, tail, value, head, norm):
                        for s in range(STEPS):
                            h, j = s // NT, s % NT
                            u = HEADS * b + h
                            tile = ahead(s, value)
                            if tile:
                                n, sh, sj = tile
                                if n == STEPS:
                                    pe.wait_ge(stacked, STACK * (b + 3))
                                pe.wait_ge(at_m, STEPS * b + n - NT + 1)
                                scores(slot if n < STEPS else 1 - slot, sh, sj)
                            if j == 0:
                                pe.wait_ge(at_e, NT * u + NT)
                            transposes(pst[:, j % 2, :].rearrange("p (t n) -> p t n", t=NT),
                                       [SM[:, h % 2, i, j * P:(j + 1) * P] for i in range(NT)]).then_inc(at_t, 1)
                            if s:
                                weighted(b, slot, (s - 1) // NT, (s - 1) % NT)
                            elif tail:
                                weighted(b - 1, 1 - slot, HEADS - 1, NT - 1)
                            if tail and s == 6:
                                if head:
                                    pe.wait_ge(p_y, b + 3)
                                tail_step(b - 1)
                            if value and s == 7:
                                if tail:
                                    pe.wait_ge(q_z, b)
                                else:
                                    pe.wait_ge(p_y, b + 3)
                                value_step(b + 1)
                            if head:
                                head_step(s, b + 2)
                            if s == 14:
                                if head:
                                    pe.wait_ge(p_kl, b + 3)
                                elif value:
                                    pe.wait_ge(p_vc, b + 2)
                                pe.wait_ge(at_rb, b + 1)
                                transposes(ps1t, [RB[:, i].rearrange("p h e -> p (h e)") for i in range(NT)]).then_inc(at_rt, 1)

                    def first():
                        for c in range(2):
                            for s in range(14):
                                if s == 0 and c:
                                    pe.wait_ge(p_vc, 1)
                                if s == 9 and c == 0:
                                    pe.wait_ge(p_x1, 1)
                                    transposes(ps1t, [x1[:, i, :] for i in range(NT)]).then_inc(p_t, 1)
                                else:
                                    head_step(s, c)
                            if c == 0:
                                pe.wait_ge(p_kl, 1)
                                value_step(0)
                        pe.wait_ge(p_kl, 2)
                        pe.wait_ge(stacked, 2 * STACK)
                        for n in range(AHEAD):
                            if n >= NT:
                                pe.wait_ge(at_m, n - NT + 1)
                            scores(0, n // NT, n % NT)

                    def last():
                        weighted(GRAPHS - 1, 1, HEADS - 1, NT - 1)
                        pe.wait_ge(at_rc, GRAPHS + 3)
                        tail_step(GRAPHS - 1)
                    run(first, round_, last)(pe)

                @block.sync
                def _(sp):
                    sp.sem_inc(stacked, STACK)

                    def stack(c, s):
                        for part, (made, dst, order) in enumerate(((p_ql, QS, (0, 0, 1, 1)), (p_kl, KS, (0, 1, 0, 1)))):
                            sp.wait_ge(made, c + 1)
                            if part == 0:
                                sp.wait_ge(at_x, c + 1)
                            for h in range(HEADS):
                                for r in range(4):
                                    sp.dma_start(dst[HD * r:HD * r + HD, s, h, :].bitcast(F32),
                                                 qk[HD * h:HD * h + HD, part, order[r], :].bitcast(F32)).then_inc(stacked, 16)
                    every(sp, stack)

                @block.scalar
                def _(act):
                    act.sem_inc(at_rc, 3)

                    def head_evacuation(s, c):
                        if s == 4:
                            act.wait_ge(p_xp, c + 1)
                            a.activation(xpF[:], ps1[:], ACT.Copy).then_inc(p_xpc, 1)
                        if s == 5:
                            act.wait_ge(p_wc, c + 1)
                            a.activation(Y[:], ps1t, ACT.Copy).then_inc(p_y, 1)
                        if s == 10:
                            act.wait_ge(p_t, c + 1)
                            a.activation(x1F[:], ps1[:], ACT.Copy).then_inc(p_tc, 1)
                        if s in (11, 13):
                            part = (s - 11) // 2
                            made, high = ((p_q, p_qh), (p_k, p_kh))[part]
                            act.wait_ge(made, c + 1)
                            act.wait_ge(stacked, STACK * c + STACK)
                            a.activation(qk[:, part, 0, :], ps1[:], ACT.Copy).then_inc(high, 1)

                    def keep(c):
                        a.activation(X2[:, bass.ds(4 * c, 4), :], x1[:], ACT.Copy).then_inc(p_keep, 1)

                    def value_evacuation(c, slot):
                        act.wait_ge(p_v, c + 1)
                        a.activation(vT[:, slot], ps1t, ACT.Copy).then_inc(p_vc, 1)

                    def exps(number, h, j):
                        act.wait_ge(at_m, number + 1)
                        a.activation(SM[:, h % 2, j, :], SM[:, h % 2, j, :], ACT.Exp, bias=MN[:, h % 2, j:j + 1], scale=-1.0,
                                     accum_out=SUM[:, h, j:j + 1]).then_inc(at_e, 1)

                    def normalize(c, i):
                        ins = a.activation(hn[:, i, :], X[:, 4 * c + i, :], ACT.Relu,
                                           bias=NBIAS[:, bass.ds(4 * c + i, 1)], scale=RSTD[:, bass.ds(4 * c + i, 1)])
                        if i == NT - 1:
                            ins.then_inc(p_norm, 1)

                    def round_(b, slot, tail, value, head, norm):
                        for s in range(STEPS):
                            j = s % NT
                            if value and s == 8:
                                value_evacuation(b + 1, 1 - slot)
                            if head:
                                head_evacuation(s, b + 2)
                            if s == 15:
                                act.wait_ge(at_rt, b + 1)
                                a.activation(RF[:], ps1[:], ACT.Copy).then_inc(at_rc, 1)
                            if s in ACT_COPIES:
                                act.wait_ge(at_t, STEPS * b + s + 1)
                                a.activation(PT[:, j % 2, :], pst[:, j % 2, :], ACT.Copy).then_inc(at_pa, 1)
                            tile = ahead(s, value)
                            if tile:
                                n, sh, sj = tile
                                if n == STEPS:
                                    act.wait_ge(at_r, b + 1)
                                    alone(act)
                                exps(STEPS * b + n, sh, sj)
                            if head and s == 10:
                                keep(b + 2)
                            if norm and s > 10 and s < 15:
                                normalize(b + 3, s - 11)

                    def first():
                        for c in range(2):
                            for i in range(NT):
                                normalize(c, i)
                            for s in range(15):
                                head_evacuation(s, c)
                                if s == 10:
                                    keep(c)
                            if c == 0:
                                value_evacuation(0, 0)
                        for i in range(NT):
                            normalize(2, i)
                        for n in range(AHEAD):
                            exps(n, n // NT, n % NT)

                    run(first, round_, lambda: None)(act)

                @block.vector
                def _(dve):
                    dve.sem_inc(at_o, 1)
                    dve.sem_inc(at_x, 2)

                    def head_step(s, c):
                        if s == 5:
                            dve.wait_ge(p_y, c + 1)
                            dve_row_stats(dve, ln1, c, 0, lambda i: Y[:, i, :])
                        if s == 6:
                            dve.wait_ge(ln1.moments, ln1.base + c + 1)
                            for i in range(NT):
                                last = v.scalar_tensor_tensor(Y1[:, i, :], Y[:, i, :], MV[:, 0, i, 0:1], ROW[:, ROWS.index("L3_g1"), :],
                                                              ALU.subtract, ALU.mult)
                            last.then_inc(p_mul, 1)
                        if s == 7:
                            dve.wait_ge(p_mul, c + 1)
                            dve.wait_ge(ln1.rstd, ln1.base + c + 1)
                            for i in range(NT):
                                last = v.scalar_tensor_tensor(Y1[:, i, :], Y1[:, i, :], rstd1[:, i:i + 1], ROW[:, ROWS.index("L3_be1"), :],
                                                              ALU.mult, ALU.add)
                            last.then_inc(p_add, 1)
                        if s == 8:
                            dve.wait_ge(p_add, c + 1)
                            dve.wait_ge(p_keep, c + 1)
                            v.scalar_tensor_tensor(x1[:], Y1[:], 0.0, hn[:], ALU.max, ALU.add).then_inc(p_x1, 1)
                        if s in (11, 13):
                            part = (s - 11) // 2
                            high, low = ((p_qh, p_ql), (p_kh, p_kl))[part]
                            dve.wait_ge(high, c + 1)
                            v.tensor_tensor(qk[:, part, 1, :], ps1[:], qk[:, part, 0, :].bitcast(F32), ALU.subtract).then_inc(low, 1)

                    def mask(number, h, j):
                        dve.wait_ge(at_s, number + 1)
                        alone(dve)
                        v.tensor_tensor_reduce(out=SM[:, h % 2, j, :], in0=pss[:, j, :], in1=NB[:, j, :], scale=NS[:, j:j + 1],
                                               scalar=3e38, op0=ALU.add, op1=ALU.min,
                                               accum_out=MN[:, h % 2, j:j + 1]).then_inc(at_m, 1)

                    def projection_evacuation(c):
                        dve.wait_ge(q_aff, c + 1)
                        dve.wait_ge(q_wo, c + 1)
                        alone(dve)
                        v.tensor_tensor(Z[:], ps1t, X2[:, bass.ds(4 * c, 4), :], ALU.add).then_inc(q_z, 1)

                    def output_stats(c):
                        dve.wait_ge(q_z, c + 1)
                        dve_row_stats(dve, ln2, c, 1, lambda i: Z[:, i, :])

                    def output(c):
                        dve.wait_ge(at_pv, c + 1)
                        dve.wait_ge(at_rc, c + 4)
                        v.tensor_tensor(oF[:], pso[:], RF[:], ALU.mult).then_inc(at_o, 1)

                    def round_(b, slot, tail, value, head, norm):
                        for s in range(STEPS):
                            h, j = s // NT, s % NT
                            if tail and s == 7:
                                projection_evacuation(b - 1)
                            if s in DVE_COPIES:
                                dve.wait_ge(at_t, STEPS * b + s + 1)
                                v.tensor_copy(PT[:, j % 2, :], pst[:, j % 2, :]).then_inc(at_pd, 1)
                            if tail and s == 0:
                                output(b - 1)
                            if s == 11:
                                dve.wait_ge(at_e, STEPS * b + STEPS)
                                v.reciprocal(RS[:], SUM[:]).then_inc(at_r, 1)
                            tile = ahead(s, value)
                            if tile:
                                n, sh, sj = tile
                                if sj == 0:
                                    dve.wait_ge(at_t, STEPS * b + s + 1)
                                mask(STEPS * b + n, sh, sj)
                            if s + AHEAD == STEPS - 1:
                                dve.sem_inc(at_x, 1)
                            if s == 12:
                                dve.wait_ge(at_r, b + 1)
                                for i in range(NT):
                                    last = v.tensor_copy(RB[:, i], RS[:, :, i].unsqueeze(2).to_broadcast([P, HEADS, HD]))
                                last.then_inc(at_rb, 1)
                            if tail and s == 7:
                                output_stats(b - 1)
                            if head:
                                head_step(s, b + 2)

                    def first():
                        dve.sem_inc(p_keep, 1)
                        for c in range(2):
                            for s in range(15):
                                head_step(s, c)
                        for n in range(AHEAD):
                            mask(n, n // NT, n % NT)

                    def last():
                        output(GRAPHS - 1)
                        projection_evacuation(GRAPHS - 1)
                        output_stats(GRAPHS - 1)
                    run(first, round_, last)(dve)

                @block.gpsimd
                def _(pool):
                    pool.sem_inc(ln2.free, 2)
                    pool.sem_inc(q_aff, 1)

                    def tail_rows(c):
                        pool.wait_ge(ln2.bias, c + 1)
                        alone(pool)
                        for i in range(NT):
                            last = g.tensor_scalar(Z1[:, i, :], Z[:, i, :], rstd2[:, i:i + 1], nb2[:, i:i + 1], ALU.mult, ALU.add)
                        last.then_inc(q_aff, 1)
                        pool.wait_ge(q_aff, c + 2)
                        alone(pool)
                        g.tensor_tensor(Z1[:], Z1[:], row4("L3_g2"), ALU.mult).then_inc(q_mul, 1)
                        pool.wait_ge(q_mul, c + 1)
                        alone(pool)
                        g.tensor_tensor(X2[:, bass.ds(4 * c, 4), :], Z1[:], row4("L3_be2"), ALU.add).then_inc(q_x2, 1)

                    def round_(b, slot, tail, value, head, norm):
                        if head:
                            pool_rstd(pool, ln1, b + 2, 0, rstd1[:], None)
                        if tail:
                            pool_rstd(pool, ln2, b - 1, 1, rstd2[:], nb2[:])
                            tail_rows(b - 1)

                    def first():
                        for c in range(2):
                            pool_rstd(pool, ln1, c, 0, rstd1[:], None)

                    def last():
                        pool_rstd(pool, ln2, GRAPHS - 1, 1, rstd2[:], nb2[:])
                        tail_rows(GRAPHS - 1)
                    run(first, round_, last)(pool)

            m_x, m_t, m_tc, m_w1, m_g, m_w2, m_z, m_aff, m_mul, m_add, m_out = (
                sem(f"s4_{n}") for n in ("x", "t", "tc", "w1", "g", "w2", "z", "aff", "mul", "add", "out"))
            m_st = [sem(f"s4_st{n}") for n in range(2)]
            ln.next()
            with ExitStack() as qctx, nc.Block() as block:
                def qsb(name, shape):
                    return qctx.enter_context(nc.sbuf_tensor("s4_" + name, shape, F32))

                xs = qsb("xs", [P, 2, NT, D])
                xF = qsb("xF", [P, 2, NODES])
                gF = qsb("gF", [P, 2, 2, NODES])
                Z = qsb("Z", [P, 2, NT, D])
                Z1 = qsb("Z1", [P, 2, NT, D])
                O = qsb("O", [P, 2, NT, D])
                rs = qsb("rs", [P, 2, NT])
                nb = qsb("nb", [P, 2, NT])
                pst = qctx.enter_context(nc.psum_tensor("s4_pst", [P, 2, NT, P], F32))
                psh = qctx.enter_context(nc.psum_tensor("s4_psh", [P, 2, 2, NODES], F32))
                psw = qctx.enter_context(nc.psum_tensor("s4_psw", [P, 2, NT, D], F32))

                def steps(eng, body):
                    for t_ in range(-3, 3):
                        body(t_, t_ % 2)
                    with eng.Fori(0, (GRAPHS - 6) // 2) as i:
                        for q in range(2):
                            body(2 * i + (3 + q), (3 + q) % 2)
                    for t_ in range(GRAPHS - 3, GRAPHS + 3):
                        body(t_, t_ % 2)

                @block.scalar
                def _(act):
                    def body(n, k):
                        if there(n + 2, GRAPHS):
                            act.wait_ge(m_t, n + 3)
                            a.activation(xF[:, k, :], pst[:, k].rearrange("p t d -> p (t d)"), ACT.Copy).then_inc(m_tc, 1)
                        if there(n + 3, GRAPHS):
                            a.activation(xs[:, 1 - k], X2[:, bass.ds(4 * (n + 3), 4), :], ACT.Copy).then_inc(m_x, 1)
                        if there(n + 1, GRAPHS):
                            act.wait_ge(m_w1, n + 2)
                            for h in range(2):
                                last = a.activation(gF[:, 1 - k, h, :], psh[:, 1 - k, h, :], ACT.Gelu, bias=col("L3_b1", h))
                            last.then_inc(m_g, 1)
                        if there(n - 1, GRAPHS):
                            act.wait_ge(ln.bias, ln.base + n)
                            act.wait_ge(m_out, n)
                            alone(act)
                            for i in range(NT):
                                last = a.activation(Z1[:, 1 - k, i, :], Z[:, 1 - k, i, :], ACT.Identity,
                                                    bias=nb[:, 1 - k, i:i + 1], scale=rs[:, 1 - k, i:i + 1])
                            last.then_inc(m_aff, 1)
                    steps(act, body)

                @block.tensor
                def _(pe):
                    def body(n, k):
                        if there(n + 2, GRAPHS):
                            pe.wait_ge(m_x, n + 3)
                            transposes(pst[:, k], [xs[:, k, i, :] for i in range(NT)]).then_inc(m_t, 1)
                        if there(n + 1, GRAPHS):
                            pe.wait_ge(m_tc, n + 2)
                            for h in range(2):
                                last = t.matmul(psh[:, 1 - k, h, :], W3A[:, h * P:(h + 1) * P], xF[:, 1 - k, :], start=True, stop=True)
                            last.then_inc(m_w1, 1)
                        if there(n, GRAPHS):
                            pe.wait_ge(m_g, n + 1)
                            pe.wait_ge(m_z, n + 1)
                            for i in range(NT):
                                for h in range(2):
                                    t.matmul(psw[:, k, i, :], gF[:, k, h, i * P:(i + 1) * P], W3B[:, h, :], start=h == 0, stop=False)
                                last = t.matmul(psw[:, k, i, :], ones[0:1, :], ROW[0:1, ROWS.index("L3_b2"), :], start=False, stop=True)
                            last.then_inc(m_w2, 1)
                    steps(pe, body)

                @block.vector
                def _(dve):
                    dve.sem_inc(m_z, 2)
                    dve.sem_inc(m_out, 2)

                    def body(n, k):
                        if there(n, GRAPHS):
                            if there(n - 2, GRAPHS):
                                dve.wait_ge(m_aff, n - 1)
                                alone(dve)
                            dve.wait_ge(m_w2, n + 1)
                            alone(dve)
                            v.tensor_tensor(Z[:, k], psw[:, k], X2[:, bass.ds(4 * n, 4), :], ALU.add).then_inc(m_z, 1)
                        if there(n - 3, GRAPHS):
                            dve.wait_ge(m_add, n - 2)
                            dve.wait_ge(m_st[1 - k], 8 * (n - 3) + (16 if k else 8))
                            v.tensor_tensor(O[:, 1 - k], Z1[:, 1 - k], X[:, bass.ds(4 * (n - 3), 4), :], ALU.add).then_inc(m_out, 1)
                        if there(n, GRAPHS):
                            dve.wait_ge(m_z, n + 3)
                            dve_row_stats(dve, ln, n, k, lambda i: Z[:, k, i, :])
                    steps(dve, body)

                @block.gpsimd
                def _(pool):
                    def body(n, k):
                        if there(n, GRAPHS):
                            pool_rstd(pool, ln, n, k, rs[:, k, :], nb[:, k, :])
                        if there(n - 1, GRAPHS):
                            pool.wait_ge(m_aff, n)
                            alone(pool)
                            g.tensor_tensor(Z1[:, 1 - k], Z1[:, 1 - k], row4("L3_g3"), ALU.mult).then_inc(m_mul, 1)
                            pool.wait_ge(m_mul, n)
                            alone(pool)
                            g.tensor_tensor(Z1[:, 1 - k], Z1[:, 1 - k], row4("L3_be3"), ALU.add).then_inc(m_add, 1)
                    steps(pool, body)

                @block.sync
                def _(sp):
                    for slot in range(2):
                        sp.sem_inc(m_st[slot], 16)
                    o_view = out.rearrange("b (t p) d -> b p t d", p=P)

                    def body(b, slot):
                        sp.wait_ge(m_out, b + 3)
                        sp.dma_start(o_view[bass.ds(b, 1), :, :, :].rearrange("b p t d -> p (b t) d"), O[:, slot]).then_inc(m_st[slot], 16)
                    every(sp, body)
                    for slot in range(2):
                        sp.wait_ge(m_st[slot], 8 * GRAPHS + 16)


_INS = ['x', 'adj', 'L0_gnn_W1', 'L0_gnn_b1', 'L0_gnn_g1', 'L0_gnn_be1', 'L0_gnn_W2', 'L0_gnn_b2', 'L0_gnn_g2',
        'L0_gnn_be2', 'L1_gnn_Wg0', 'L1_gnn_bg0', 'L1_gnn_Wg1', 'L1_gnn_bg1', 'L1_gnn_Wih', 'L1_gnn_Whh',
        'L1_gnn_bih', 'L1_gnn_bhh', 'L2_gnn_w1_loop', 'L2_gnn_w1_neigh', 'L2_gnn_b1', 'L2_gnn_w2_loop',
        'L2_gnn_w2_neigh', 'L2_gnn_b2', 'L3_gnn_Wc', 'L3_gnn_bc', 'L3_gnn_g1', 'L3_gnn_be1', 'L3_gnn_Wq',
        'L3_gnn_Wk', 'L3_gnn_Wv', 'L3_gnn_Wo', 'L3_gnn_bo', 'L3_gnn_g2', 'L3_gnn_be2', 'L3_gnn_W1', 'L3_gnn_b1',
        'L3_gnn_W2', 'L3_gnn_b2', 'L3_gnn_g3', 'L3_gnn_be3']


def kernel(**inputs):
    import numpy as _np
    import concourse.bacc as _bacc
    from concourse import mybir as _mybir
    from concourse.bass_utils import run_bass_kernel_spmd as _run

    nc = _bacc.Bacc("TRN2", target_bir_lowering=False, num_devices=1)
    arrays, handles = {}, {}
    for name in _INS:
        a = _np.ascontiguousarray(inputs[name])
        arrays[f"in_{name}_dram"] = a
        handles[name.replace("_gnn", "")] = nc.dram_tensor(f"in_{name}_dram", a.shape, _mybir.dt.from_np(a.dtype),
                                                           kind="ExternalInput").ap()
    out = nc.dram_tensor("out_0_dram", (GRAPHS, NODES, D), _mybir.dt.float32, kind="ExternalOutput").ap()
    build(nc, handles, out)
    r = _run(nc, [arrays], core_ids=[0])
    return r.results[0]["out_0_dram"]
```
